# Optimizing a Trainium2 kernel written in Bass

```python
import numpy as np
import jax
import jax.numpy as jnp

def _softmax(x, axis=-1):
    return jax.nn.softmax(x, axis=axis)

def _gelu(x):
    return jax.nn.gelu(x, approximate=True)

def _silu(x):
    return jax.nn.silu(x)

def _sigmoid(x):
    return jax.nn.sigmoid(x)

def _layernorm(x, axis=-1, eps=1e-05):
    m = jnp.mean(x, axis=axis, keepdims=True)
    v = jnp.var(x, axis=axis, keepdims=True)
    return (x - m) / jnp.sqrt(v + eps)

def _scatter_add(tgt, idx, src, axis=0):
    return tgt.at[idx].add(src)

def _segment_sum(src, seg, n):
    return jax.ops.segment_sum(src, seg, n)
kernel_name = 'mk_flamingo_gated_d2_seqx_r4_91dbd7'

def setup_inputs(seed: int=0):
    np.random.seed(seed)
    _w = jnp.asarray

    def _rec_inputs():
        import jax
        import jax.numpy as jnp
        _rk = jax.random.key(seed)
        x = -0.0002928 + 1 * jax.random.normal(jax.random.fold_in(_rk, 1), (2, 1024, 256), jnp.float32)
        _lenS = 1024 - jax.random.randint(jax.random.fold_in(_rk, 7), (2,), 0, max(1, 1024 // 4) + 1, jnp.int32)
        _lenS2 = 77 - jax.random.randint(jax.random.fold_in(_rk, 8), (2,), 0, max(1, 77 // 4) + 1, jnp.int32)
        _ctx_1024P = jax.random.normal(jax.random.fold_in(_rk, 11), (2, 16, 256), jnp.float32)
        _ctx_1024c = jax.random.dirichlet(jax.random.fold_in(_rk, 511), 0.3 * jnp.ones((16,), jnp.float32), (2, 77))
        _ctx_1024t = jnp.einsum('bsk,bkd->bsd', _ctx_1024c, _ctx_1024P)
        _ctx_1024t = _ctx_1024t * jax.lax.rsqrt(jnp.mean(jnp.square(_ctx_1024t)) + 1e-12) * 0.953939
        ctx_1024 = -1.39393e-06 + 0.999914 * (_ctx_1024t + 0.3 * jax.random.normal(jax.random.fold_in(_rk, 611), (2, 77, 256), jnp.float32))
        _g = jax.random.normal(jax.random.fold_in(_rk, 9001), (2, 2), jnp.float32)
        _g = jnp.sign(_g) * jnp.maximum(jnp.abs(_g), 1.0) + (_g == 0) * 1.0
        g_xattn = _g[0]
        g_ffn = _g[1]
        return (x, ctx_1024, g_xattn, g_ffn)
    x, ctx_1024, g_xattn, g_ffn = _rec_inputs()

    def _L0_xattn_setup():
        import jax, jax.numpy as jnp
        import numpy as np
        D_MODEL = 256
        NUM_HEADS = 16
        D_K = D_MODEL // NUM_HEADS

        def _split_heads(x):
            b, s, _ = x.shape
            return x.reshape(b, s, NUM_HEADS, D_K).transpose(0, 2, 1, 3)
        key = jax.random.key(seed)
        ks = jax.random.split(key, 8)
        s = 1.0 / np.sqrt(D_MODEL)
        inp = {'q': jax.random.normal(ks[0], (2, 512, D_MODEL), jnp.float32), 'k': jax.random.normal(ks[1], (2, 512, D_MODEL), jnp.float32), 'v': jax.random.normal(ks[2], (2, 512, D_MODEL), jnp.float32), 'Wq': jax.random.normal(ks[3], (D_MODEL, D_MODEL), jnp.float32) * s, 'bq': jnp.zeros((D_MODEL,), jnp.float32), 'Wk': jax.random.normal(ks[4], (D_MODEL, D_MODEL), jnp.float32) * s, 'bk': jnp.zeros((D_MODEL,), jnp.float32), 'Wv': jax.random.normal(ks[5], (D_MODEL, D_MODEL), jnp.float32) * s, 'bv': jnp.zeros((D_MODEL,), jnp.float32), 'Wo': jax.random.normal(ks[6], (D_MODEL, D_MODEL), jnp.float32) * s, 'bo': jnp.zeros((D_MODEL,), jnp.float32)}
        return inp
    _L0_xattn_all = _L0_xattn_setup()
    _L0_xattn_in = {k: v for k, v in _L0_xattn_all.items() if k in ('Wq', 'bq', 'Wk', 'bk', 'Wv', 'bv', 'Wo', 'bo')}
    del _L0_xattn_all

    def _L0_ffn_setup():
        import jax, jax.numpy as jnp
        import numpy as np
        NEG_INF = jnp.float32(-1000000000.0)

        def _router(x, Wr, br, top_k=2):
            logits = jnp.einsum('bsd,de->bse', x, Wr) + br
            _, top_idx = jax.lax.top_k(logits, top_k)
            num_experts = logits.shape[-1]
            mask = jnp.any(top_idx[..., None] == jnp.arange(num_experts), axis=-2)
            sparse_logits = jnp.where(mask, logits, NEG_INF)
            weights = jax.nn.softmax(sparse_logits, axis=-1)
            return (weights, top_idx, mask)
        key = jax.random.key(seed)
        ks = jax.random.split(key, 8)
        B, S, D, E, H = (4, 512, 256, 8, 1024)
        sd = 1.0 / np.sqrt(D)
        sh = 1.0 / np.sqrt(H)
        x = jax.random.normal(ks[0], (B, S, D), dtype=jnp.float32)
        Wr = jax.random.normal(ks[1], (D, E), dtype=jnp.float32) * sd
        br = jnp.zeros((E,), dtype=jnp.float32)
        W1 = jax.random.normal(ks[2], (E, D, H), dtype=jnp.float32) * sd
        b1 = jnp.zeros((E, H), dtype=jnp.float32)
        W2 = jax.random.normal(ks[3], (E, H, D), dtype=jnp.float32) * sh
        b2 = jnp.zeros((E, D), dtype=jnp.float32)
        return {'x': x, 'Wr': Wr, 'br': br, 'W1': W1, 'b1': b1, 'W2': W2, 'b2': b2}
    _L0_ffn_all = _L0_ffn_setup()
    _L0_ffn_in = {k: v for k, v in _L0_ffn_all.items() if k in ('Wr', 'br', 'W1', 'b1', 'W2', 'b2')}
    del _L0_ffn_all

    def _L1_xattn_setup():
        import jax, jax.numpy as jnp
        import numpy as np
        D_MODEL = 256
        NUM_HEADS = 16
        HEAD_DIM = D_MODEL // NUM_HEADS

        def _split_heads(x):
            B, N, _ = x.shape
            return x.reshape(B, N, NUM_HEADS, HEAD_DIM).transpose(0, 2, 1, 3)
        key = jax.random.key(seed)
        ks = jax.random.split(key, 11)
        B, N = (2, 512)
        s = 1.0 / np.sqrt(D_MODEL)
        return {'query': jax.random.normal(ks[0], (B, N, D_MODEL), jnp.float32), 'key': jax.random.normal(ks[1], (B, N, D_MODEL), jnp.float32), 'value': jax.random.normal(ks[2], (B, N, D_MODEL), jnp.float32), 'Wq': jax.random.normal(ks[3], (D_MODEL, D_MODEL), jnp.float32) * s, 'bq': jax.random.normal(ks[4], (D_MODEL,), jnp.float32) * 0.01, 'Wk': jax.random.normal(ks[5], (D_MODEL, D_MODEL), jnp.float32) * s, 'bk': jax.random.normal(ks[6], (D_MODEL,), jnp.float32) * 0.01, 'Wv': jax.random.normal(ks[7], (D_MODEL, D_MODEL), jnp.float32) * s, 'bv': jax.random.normal(ks[8], (D_MODEL,), jnp.float32) * 0.01, 'Wo': jax.random.normal(ks[9], (D_MODEL, D_MODEL), jnp.float32) * s, 'bo': jax.random.normal(ks[10], (D_MODEL,), jnp.float32) * 0.01}
    _L1_xattn_all = _L1_xattn_setup()
    _L1_xattn_in = {k: v for k, v in _L1_xattn_all.items() if k in ('Wq', 'bq', 'Wk', 'bk', 'Wv', 'bv', 'Wo', 'bo')}
    del _L1_xattn_all

    def _L1_ffn_setup():
        import jax, jax.numpy as jnp
        import numpy as np
        SWIGLU_ALPHA = 1.702
        SWIGLU_LIMIT = 7.0
        TOP_K = 4
        key = jax.random.key(seed)
        k = jax.random.split(key, 5)
        B, S, D, E, I = (2, 256, 256, 8, 512)
        return {'hidden_states': jax.random.normal(k[0], (B, S, D), dtype=jnp.float32), 'router_weight': jax.random.normal(k[1], (E, D), dtype=jnp.float32) * 0.02, 'router_bias': jnp.zeros((E,), dtype=jnp.float32), 'gate_up_proj': jax.random.normal(k[2], (E, 2 * I, D), dtype=jnp.float32) * 0.02, 'gate_up_proj_bias': jnp.zeros((E, 2 * I), dtype=jnp.float32), 'down_proj': jax.random.normal(k[3], (E, D, I), dtype=jnp.float32) * 0.02, 'down_proj_bias': jnp.zeros((E, D), dtype=jnp.float32)}
    _L1_ffn_all = _L1_ffn_setup()
    _L1_ffn_in = {k: v for k, v in _L1_ffn_all.items() if k in ('router_weight', 'router_bias', 'gate_up_proj', 'gate_up_proj_bias', 'down_proj', 'down_proj_bias')}
    del _L1_ffn_all
    return {'x': x, 'ctx_1024': ctx_1024, 'g_xattn': g_xattn, 'g_ffn': g_ffn, 'L0_xattn_Wq': _L0_xattn_in['Wq'], 'L0_xattn_bq': _L0_xattn_in['bq'], 'L0_xattn_Wk': _L0_xattn_in['Wk'], 'L0_xattn_bk': _L0_xattn_in['bk'], 'L0_xattn_Wv': _L0_xattn_in['Wv'], 'L0_xattn_bv': _L0_xattn_in['bv'], 'L0_xattn_Wo': _L0_xattn_in['Wo'], 'L0_xattn_bo': _L0_xattn_in['bo'], 'L0_ffn_Wr': _L0_ffn_in['Wr'], 'L0_ffn_br': _L0_ffn_in['br'], 'L0_ffn_W1': _L0_ffn_in['W1'], 'L0_ffn_b1': _L0_ffn_in['b1'], 'L0_ffn_W2': _L0_ffn_in['W2'], 'L0_ffn_b2': _L0_ffn_in['b2'], 'L1_xattn_Wq': _L1_xattn_in['Wq'], 'L1_xattn_bq': _L1_xattn_in['bq'], 'L1_xattn_Wk': _L1_xattn_in['Wk'], 'L1_xattn_bk': _L1_xattn_in['bk'], 'L1_xattn_Wv': _L1_xattn_in['Wv'], 'L1_xattn_bv': _L1_xattn_in['bv'], 'L1_xattn_Wo': _L1_xattn_in['Wo'], 'L1_xattn_bo': _L1_xattn_in['bo'], 'L1_ffn_router_weight': _L1_ffn_in['router_weight'], 'L1_ffn_router_bias': _L1_ffn_in['router_bias'], 'L1_ffn_gate_up_proj': _L1_ffn_in['gate_up_proj'], 'L1_ffn_gate_up_proj_bias': _L1_ffn_in['gate_up_proj_bias'], 'L1_ffn_down_proj': _L1_ffn_in['down_proj'], 'L1_ffn_down_proj_bias': _L1_ffn_in['down_proj_bias']}

def reference(x, ctx_1024, g_xattn, g_ffn, L0_xattn_Wq, L0_xattn_bq, L0_xattn_Wk, L0_xattn_bk, L0_xattn_Wv, L0_xattn_bv, L0_xattn_Wo, L0_xattn_bo, L0_ffn_Wr, L0_ffn_br, L0_ffn_W1, L0_ffn_b1, L0_ffn_W2, L0_ffn_b2, L1_xattn_Wq, L1_xattn_bq, L1_xattn_Wk, L1_xattn_bk, L1_xattn_Wv, L1_xattn_bv, L1_xattn_Wo, L1_xattn_bo, L1_ffn_router_weight, L1_ffn_router_bias, L1_ffn_gate_up_proj, L1_ffn_gate_up_proj_bias, L1_ffn_down_proj, L1_ffn_down_proj_bias):
    import jax
    import jax.numpy as jnp

    def _L0_xattn_ref(q, k, v, Wq, bq, Wk, bk, Wv, bv, Wo, bo):
        import jax, jax.numpy as jnp
        import numpy as np
        D_MODEL = 256
        NUM_HEADS = 16
        D_K = D_MODEL // NUM_HEADS

        def _split_heads(x):
            b, s, _ = x.shape
            return x.reshape(b, s, NUM_HEADS, D_K).transpose(0, 2, 1, 3)
        qh = _split_heads(q @ Wq + bq)
        kh = _split_heads(k @ Wk + bk)
        vh = _split_heads(v @ Wv + bv)
        scale = 1.0 / jnp.sqrt(jnp.asarray(D_K, qh.dtype))
        scores = jnp.einsum('bhqd,bhkd->bhqk', qh, kh) * scale
        probs = jax.nn.softmax(scores, axis=-1)
        ctx = jnp.einsum('bhqk,bhkd->bhqd', probs, vh)
        b, h, s, d = ctx.shape
        ctx = ctx.transpose(0, 2, 1, 3).reshape(b, s, h * d)
        return ctx @ Wo + bo

    def _L0_ffn_ref(x, Wr, br, W1, b1, W2, b2):
        import jax, jax.numpy as jnp
        import numpy as np
        NEG_INF = jnp.float32(-1000000000.0)

        def _router(x, Wr, br, top_k=2):
            logits = jnp.einsum('bsd,de->bse', x, Wr) + br
            _, top_idx = jax.lax.top_k(logits, top_k)
            num_experts = logits.shape[-1]
            mask = jnp.any(top_idx[..., None] == jnp.arange(num_experts), axis=-2)
            sparse_logits = jnp.where(mask, logits, NEG_INF)
            weights = jax.nn.softmax(sparse_logits, axis=-1)
            return (weights, top_idx, mask)
        weights, top_idx, mask = _router(x, Wr, br, top_k=2)
        num_experts = W1.shape[0]
        out = jnp.zeros_like(x)
        for e in range(num_experts):
            h = jax.nn.relu(jnp.einsum('bsd,dh->bsh', x, W1[e]) + b1[e])
            y = jnp.einsum('bsh,hd->bsd', h, W2[e]) + b2[e]
            w = weights[:, :, e] * mask[:, :, e].astype(x.dtype)
            out = out + y * w[:, :, None]
        return out

    def _L1_xattn_ref(query, key, value, Wq, bq, Wk, bk, Wv, bv, Wo, bo):
        import jax, jax.numpy as jnp
        import numpy as np
        D_MODEL = 256
        NUM_HEADS = 16
        HEAD_DIM = D_MODEL // NUM_HEADS

        def _split_heads(x):
            B, N, _ = x.shape
            return x.reshape(B, N, NUM_HEADS, HEAD_DIM).transpose(0, 2, 1, 3)
        B, N, _ = query.shape
        q = _split_heads(query @ Wq.T + bq)
        k = _split_heads(key @ Wk.T + bk)
        v = _split_heads(value @ Wv.T + bv)
        scores = jnp.einsum('bhnd,bhmd->bhnm', q, k)
        attn = jax.nn.softmax(scores, axis=-1)
        out = jnp.einsum('bhnm,bhmd->bhnd', attn, v)
        out = out.transpose(0, 2, 1, 3).reshape(B, N, D_MODEL)
        return out @ Wo.T + bo

    def _L1_ffn_ref(hidden_states, router_weight, router_bias, gate_up_proj, gate_up_proj_bias, down_proj, down_proj_bias):
        import jax, jax.numpy as jnp
        import numpy as np
        SWIGLU_ALPHA = 1.702
        SWIGLU_LIMIT = 7.0
        TOP_K = 4
        B, S, D = hidden_states.shape
        E = router_weight.shape[0]
        x = hidden_states.reshape(-1, D)
        N = x.shape[0]
        logits = x @ router_weight.T + router_bias
        topk_logits, topk_idx = jax.lax.top_k(logits, TOP_K)
        topk_w = jax.nn.softmax(topk_logits.astype(jnp.float32), axis=-1)
        combine = jnp.zeros((N, E), dtype=jnp.float32)
        combine = combine.at[jnp.arange(N)[:, None], topk_idx].set(topk_w)
        gate_up = jnp.einsum('nd,ejd->nej', x, gate_up_proj) + gate_up_proj_bias
        gate, up = jnp.split(gate_up, 2, axis=-1)
        gate = jnp.minimum(gate, SWIGLU_LIMIT)
        up = jnp.clip(up, -SWIGLU_LIMIT, SWIGLU_LIMIT)
        act = (up + 1.0) * gate * jax.nn.sigmoid(SWIGLU_ALPHA * gate)
        out = jnp.einsum('nei,edi->ned', act, down_proj) + down_proj_bias
        y = jnp.einsum('ned,ne->nd', out, combine.astype(out.dtype))
        return y.reshape(B, S, D)
    x = x + jnp.tanh(g_xattn[0]) * _L0_xattn_ref(_layernorm(x, axis=-1), ctx_1024, ctx_1024, L0_xattn_Wq, L0_xattn_bq, L0_xattn_Wk, L0_xattn_bk, L0_xattn_Wv, L0_xattn_bv, L0_xattn_Wo, L0_xattn_bo)
    x = x + jnp.tanh(g_ffn[0]) * _L0_ffn_ref(_layernorm(x, axis=-1), L0_ffn_Wr, L0_ffn_br, L0_ffn_W1, L0_ffn_b1, L0_ffn_W2, L0_ffn_b2)
    x = x + jnp.tanh(g_xattn[1]) * _L1_xattn_ref(_layernorm(x, axis=-1), ctx_1024, ctx_1024, L1_xattn_Wq, L1_xattn_bq, L1_xattn_Wk, L1_xattn_bk, L1_xattn_Wv, L1_xattn_bv, L1_xattn_Wo, L1_xattn_bo)
    x = x + jnp.tanh(g_ffn[1]) * _L1_ffn_ref(_layernorm(x, axis=-1), L1_ffn_router_weight, L1_ffn_router_bias, L1_ffn_gate_up_proj, L1_ffn_gate_up_proj_bias, L1_ffn_down_proj, L1_ffn_down_proj_bias)
    return x

_drawn_inputs = setup_inputs


def setup_inputs(seed=0):
    import zlib

    import numpy as np

    out = dict(_drawn_inputs(seed))
    spreads = {'g_ffn': (-1.0, 0.6),
     'L0_xattn_bq': (0.0, 0.1),
     'L0_xattn_bk': (0.0, 0.8),
     'L0_xattn_bv': (0.0, 0.1),
     'L0_xattn_bo': (0.0, 0.1),
     'L0_ffn_br': (0.0, 0.1),
     'L0_ffn_b1': (0.0, 0.1),
     'L0_ffn_b2': (0.0, 0.1),
     'L1_ffn_router_bias': (0.0, 0.639),
     'L1_ffn_gate_up_proj_bias': (0.0, 0.8),
     'L1_ffn_down_proj_bias': (0.0, 0.277)}
    factors = {'L1_xattn_bq': 7.344, 'L1_xattn_bk': 8.0, 'L1_xattn_bv': 8.0, 'L1_xattn_bo': 8.0}
    for name, (base, spread) in spreads.items():
        noise = np.random.default_rng([zlib.crc32(name.encode()), seed]).standard_normal(out[name].shape)
        drawn = base * np.exp(spread * noise) if base else spread * noise
        out[name] = jnp.asarray(drawn.astype(out[name].dtype))
    for name, factor in factors.items():
        out[name] = (out[name] * factor).astype(out[name].dtype)
    return out
```

```python
from contextlib import ExitStack

import numpy as np
import concourse.bass as bass
from concourse import mybir

F32 = mybir.dt.float32
R32 = mybir.dt.float32r
I32 = mybir.dt.int32
U32 = mybir.dt.uint32
ALU = mybir.AluOpType
ACT = mybir.ActivationFunctionType
AX = mybir.AxisListType

P = 128
LAYERS = 2
B, SEQ, D = 2, 1024, 256
N = B * SEQ
NT = N // P
KD = D // P
H, DH, S = 16, 16, 77
HC = P // DH
SC = 512
FLAT = H * S
NCH = -(-FLAT // P)
HPB = SC // S
DV = DH + 1
SPAN = 3
E = 8
TOPK = (2, 4)
WIDE = 1024
KH = (8, 4)
REGION = N + P
MT = tuple(N * k // P + E - 1 for k in TOPK)
IDLE = E - 1
SPARE = (E + IDLE) * P
ROW = D + E
W2AT = KD * WIDE
WCOLS = W2AT + 8 * D
BCOLS = WIDE + D
EPS = 1e-5
GROUPS = ((0, 4), (4, 8), (8, NCH))


def first_head(c):
    return c * P // S


def build_program(nc, a):
    with ExitStack() as ctx:
        def sb(name, shape, dt=F32):
            return ctx.enter_context(nc.sbuf_tensor(name, shape, dt))

        def sem(name):
            return ctx.enter_context(nc.semaphore(name))

        def dram(name, shape, dt=F32):
            return nc.dram_tensor(name, shape, dt, kind="Internal").ap()

        dispatched = [dram(f"dispatched{l}", (E * REGION + IDLE * P, ROW)) for l in range(LAYERS)]
        results = [dram(f"results{l}", (SPARE + TOPK[l] * N, D)) for l in range(LAYERS)]
        attended = [dram(f"attended{l}", (NT, P, D + 4)) for l in range(LAYERS)]
        flat_values = dram("flat_values", (LAYERS, B, H, S, DV))
        split_bias = dram("split_bias", (2, LAYERS * E, BCOLS))

        ident = sb("ident", [P, P])
        tri = sb("tri", [P, P])
        ones = sb("ones", [P, P])
        ones2 = sb("ones2", [2, P], R32)
        head_mask = sb("head_mask", [P, HC])
        block_mask = sb("block_mask", [P, NCH, SPAN])
        expert_ids = sb("expert_ids", [P, E])
        region_base = sb("region_base", [P, E])
        rank_rows = sb("rank_rows", [P, 4])
        token_ids = sb("token_ids", [P, NT])
        eps_col = sb("eps_col", [P, 1])
        minus_half = sb("minus_half", [P, 1])
        tile_edges = sb("tile_edges", [1, 15])
        tri8 = sb("tri8", [1, E, E])
        alternate = sb("alternate", [1, E])
        tile_ids = sb("tile_ids", [1, max(MT)])
        zero_rows = sb("zero_rows", [P, ROW])
        idle_rows = sb("idle_rows", [P, ROW])
        gates = sb("gates", [P, 4])
        tgates = sb("tgates", [P, 4])

        wo = sb("wo", [P, LAYERS, KD, D])
        wq_hi = sb("wq_hi", [P, LAYERS, KD, D], R32)
        wq_lo = sb("wq_lo", [P, LAYERS, KD, D], R32)
        wr = sb("wr", [P, LAYERS, KD, E])
        ctxT = sb("ctxT", [P, B, KD, S])
        bq = sb("bq", [P, LAYERS, KD])
        bk = sb("bk", [P, LAYERS, KD])
        bv = sb("bv", [S, LAYERS, D])
        bo = sb("bo", [P, LAYERS, D])
        br = sb("br", [P, LAYERS, E])
        key_hi = sb("key_hi", [P, B, KD, HC * S], R32)
        key_lo = sb("key_lo", [P, B, KD, HC * S], R32)
        kT = sb("kT", [P, S])
        kT_hi = sb("kT_hi", [P, S], R32)
        kT_lo = sb("kT_lo", [P, S])
        vals = sb("vals", [S, H, DV])
        flat_v = sb("flat_v", [P, NCH, DV])
        v_blocks = sb("v_blocks", [P, B, NCH, SPAN * DV])
        xt = sb("xt", [P, 4, D])
        x2 = sb("x2", [P, 4, D + 4])
        rows = sb("rows", [P, 4, ROW])
        xn = sb("xn", [P, 2, D])
        xT_hi = sb("xT_hi", [P, D], R32)
        xT_lo = sb("xT_lo", [P, D], R32)
        q_hi = sb("q_hi", [P, KD, P], R32)
        q_lo = sb("q_lo", [P, KD, P], R32)
        probs = sb("probs", [P, 2, NCH * P])
        probsT = sb("probsT", [P, NCH * P])
        top = sb("top", [P, H])
        rden = sb("rden", [P, H])
        ob = sb("ob", [P, D])
        oT = sb("oT", [P, D])
        xg = sb("xg", [P, 2, D])
        x2T = sb("x2T", [P, D])
        st1, mv1, rs1 = sb("st1", [P, 6]), sb("mv1", [P, 2]), sb("rs1", [P, 2])
        st2, mv2, rs2 = sb("st2", [P, 6]), sb("mv2", [P, 2]), sb("rs2", [P, 2])
        logits = sb("logits", [P, E])
        best = sb("best", [P, E])
        best_at = sb("best_at", [P, E], U32)
        best_f = sb("best_f", [P, 4])
        chosen = sb("chosen", [P, 4, E, 4])
        ranked = sb("ranked", [P, E, 4])
        ranks = sb("ranks", [P, E])
        mask = sb("mask", [P, 2, E])
        seen = sb("seen", [P, 2, E])
        slots = sb("slots", [P, E])
        slot_k = sb("slot_k", [P, 4, E])
        slot_f = sb("slot_f", [P, 4])
        slot_at = sb("slot_at", [P, 4, 4], U32)

        ysb = sb("ysb", [P, 2, 4, D])
        wkv = ysb[:, :, :, :].rearrange("p a b c -> p (a b c)").rearrange(
            "p (l w k n) -> p l w k n", l=LAYERS, w=2, k=KD)
        x2in = sb("x2in", [P, 2, D + 4])
        below = sb("below", [P, 4])
        expw = sb("expw", [P, 4])
        wsum = sb("wsum", [P, 1])
        rsum = sb("rsum", [P, 1])
        share = sb("share", [P, 4])

        raw = sb("raw", [P, WCOLS])
        w_hi = sb("w_hi", [P, 2, WCOLS], R32)
        w_lo = sb("w_lo", [P, 2, WCOLS], R32)
        w_bias = sb("w_bias", [2, 2, BCOLS], R32)
        braw = sb("braw", [P, LAYERS * E * BCOLS // P])
        b_hi = sb("b_hi", [P, LAYERS * E * BCOLS // P], R32)
        b_lo = sb("b_lo", [P, LAYERS * E * BCOLS // P], R32)
        hid = probs[:, 0, 0:WIDE]
        gate_s = probs[:, 1, 0:512]
        up_s = probs[:, 1, 512:1024]
        sig_s = probsT[:, 0:512]
        hT_hi = sb("hT_hi", [P, WIDE], R32)
        hT_lo = sb("hT_lo", [P, WIDE], R32)
        xm = sb("xm", [P, 4, ROW])
        wq = xm[:, :, :].rearrange("p a b -> p (a b)")[:, 0:LAYERS * KD * D].rearrange(
            "p (l k n) -> p l k n", l=LAYERS, k=KD)
        y = ysb[:, 0]
        y_at = sb("y_at", [P, 4], U32)
        TAB = 8
        ROWAT, EXPERT, SLOT, SPLIT0, SPLIT1, NEXT, LOAD, PLACE = range(TAB)
        row_of = lambda n, c0, d: probs[0:1, n, c0:c0 + E * max(MT)].rearrange(
            "p (a b) -> p a b", b=d)
        tab_f = row_of(1, 0, max(MT))
        tab = sb("tab", [1, TAB, max(MT)], I32)
        t_cnt = sb("t_cnt", [1, E])
        cnt_i = sb("cnt_i", [1, E], I32)
        t_gt = sb("t_gt", [1, E, 15])
        t_tiles = sb("t_tiles", [1, E])
        t_tri = sb("t_tri", [1, E, E])
        t_end = sb("t_end", [1, E])
        t_le = row_of(0, 0, E)
        t_m = row_of(0, E * max(MT), E)
        t_e = sb("t_e", [1, max(MT)])
        t_d = sb("t_d", [1, max(MT)])
        t_new = sb("t_new", [1, max(MT)])

        ps = ctx.enter_context(nc.psum_tensor("ps", [P, 8, SC], F32))

        (params_loaded, wkv_loaded, consts_made, small_made, gates_ready, bo_scaled,
         wq_hi_done, wq_lo_done, kT_ready, kT_done, kT_hi_done, kT_lo_done, keys_done, v_ready,
         v_done, v_stored, v_flat, v_blocks_done) = [sem(n) for n in (
            "params_loaded", "wkv_loaded", "consts_made", "small_made", "gates_ready",
            "bo_scaled", "wq_hi_done", "wq_lo_done", "kT_ready", "kT_done", "kT_hi_done",
            "kT_lo_done", "keys_done", "v_ready", "v_done", "v_stored", "v_flat",
            "v_blocks_done")]
        x_loaded = [sem(f"x_loaded{r}") for r in range(4)]
        (stats1, moments1, var1, rstd1, xn_done, xnT_ready, xT_hi_done, xT_lo_done, q_ready,
         q_hi_done, q_lo_done, scores_ready, max_done, shifted_part, shifted, exp_done, pT_ready, pT_copied,
         pv_ready, rden_done, o_done, oT_ready, oT_copied, proj_ready, xg_done, x2_done, stats2,
         moments2, var2, rstd2, rows_done, x2T_ready, x2T_copied, logits_ready, logits_done,
         best_done, best_kept, best_at_done, best_f_done, chosen_done, mask_done, ranked_done, ranks_done,
         code_done, seen_done, count_ready, slots_done, slot_k_done, slot_f_done, slot_done) = [
            sem(n) for n in (
                "stats1", "moments1", "var1", "rstd1", "xn_done", "xnT_ready", "xT_hi_done",
                "xT_lo_done", "q_ready", "q_hi_done", "q_lo_done", "scores_ready", "max_done",
                "shifted_part", "shifted", "exp_done", "pT_ready", "pT_copied", "pv_ready", "rden_done",
                "o_done", "oT_ready", "oT_copied", "proj_ready", "xg_done", "x2_done", "stats2",
                "moments2", "var2", "rstd2", "rows_done", "x2T_ready", "x2T_copied",
                "logits_ready", "logits_done", "best_done", "best_kept", "best_at_done", "best_f_done",
                "chosen_done", "mask_done", "ranked_done", "ranks_done", "code_done",
                "seen_done", "count_ready", "slots_done", "slot_k_done", "slot_f_done",
                "slot_done")]
        x2_stored = [sem(f"x2_stored{r}") for r in range(4)]
        scattered = [sem(f"scattered{r}") for r in range(4)]
        (total_ready, seen_zero, table_step, table_ready, zeros_stored, gates_passed) = [
            sem(n) for n in ("total_ready", "seen_zero", "table_step", "table_ready",
                             "zeros_stored", "gates_passed")]
        results_loaded = [sem(f"results_loaded{r}") for r in range(2)]
        (below_done, expw_done, rsum_done, share_done, added) = [sem(n) for n in (
            "below_done", "expw_done", "rsum_done", "share_done", "added")]
        out_stored = [sem(f"out_stored{r}") for r in range(4)]
        raw_loaded, hi_done, split_done, bias_split, bias_stored, bias_loaded = [sem(n) for n in (
            "raw_loaded", "hi_done", "split_done", "bias_split", "bias_stored", "bias_loaded")]
        rows_loaded = [sem(f"rows_loaded{r}") for r in range(4)]
        y_scattered = [sem(f"y_scattered{r}") for r in range(4)]
        (y_at_done, mT_ready, mT_hi_done, mT_lo_done, hid_ready, hid_dve, hid_act, gate_done,
         sig_done, up_done, up_gate_done, hT_ready, hT_hi_done, hT_lo_done, y_ready, y_done) = [
            sem(n) for n in (
                "y_at_done", "mT_ready", "mT_hi_done", "mT_lo_done", "hid_ready", "hid_dve",
                "hid_act", "gate_done", "sig_done", "up_done", "up_gate_done", "hT_ready",
                "hT_hi_done", "hT_lo_done", "y_ready", "y_done")]

        def need(eng, s, count):
            if isinstance(count, int) and count <= 0:
                return
            eng.wait_ge(s, count)

        def gate(eng, s, count):
            if isinstance(count, int) and count <= 0:
                return
            eng.wait_ge(s, count)
            eng.sem_inc(gates_passed, 1)

        class Tile:
            def __init__(self, j, const):
                self.c = const
                self.slot = const % 4
                self.at = const if j is None else j * 4 + const
                self.par = const % 2
                self.quad = const // 4 if j is None else j + const // 4
                self.pair = const // 2 if j is None else j * 2 + const // 2

        def attention_steps(eng, step):
            for s in range(4):
                step(None, s)
            with eng.Fori(0, NT // 4 - 1) as j:
                for u in range(4):
                    step(j, 4 + u)
            for s in range(NT, NT + 4):
                step(None, s)

        def stage(j, s, lag):
            if j is None and not 0 <= s - lag < NT:
                return None
            return Tile(j, s - lag)

        def expert_steps(eng, l, step):
            step(None, 0)
            loops = MT[l] // 4
            with eng.Fori(0, loops) as j:
                for u in range(4):
                    step(j, 1 + u)
            for s in range(4 * loops + 1, MT[l] + 1):
                step(None, s)

        def row_tile(l, j, s, lag):
            if j is None and not 0 <= s - lag < MT[l]:
                return None
            return Tile(j, s - lag)

        def scatter_count(l, r, quad):
            return quad * (16 * TOPK[l]) + l * (16 * TOPK[0] * (NT // 4))

        def uses(l, r):
            return sum(len(range(r, MT[x], 4)) for x in range(l))

        def adds(cl, at):
            return at * TOPK[cl] + cl * NT * TOPK[0]

        MBASE = [0, MT[0]]
        HBASE = [0, KH[0] // 4 * MT[0]]

        pieces = []
        for c in range(KD):
            h = c * HC
            while h < (c + 1) * HC:
                n = min((c + 1) * HC, (h // HPB + 1) * HPB) - h
                pieces.append((c, h, n))
                h += n
        SCORE_BANK, PT_BANK = 2, 5
        full = H // HPB
        rest = H - full * HPB


        tile_of = lambda ap: ap.rearrange("a p d -> (a p) d")
        x_tiles = a["x"].rearrange("(t p) d -> t p d", p=P)
        out_tiles = a["out"].rearrange("(t p) d -> t p d", p=P)

        block = ctx.enter_context(nc.Block())

        @block.sync
        def _(sp):
            for dst, src in ((wkv, a["wkv"]), (ctxT[:, :, :, :], a["ctxT"]),
                             (bk[:, :, :], a["bk"]),
                             (bv[:, :, :], a["bv"].partition_broadcast(S))):
                sp.dma_start(dst, src).then_inc(wkv_loaded, 16)
            for t in range(4):
                sp.dma_start(xt[:, t, :], x_tiles[t]).then_inc(x_loaded[t], 16)
            for dst, src in ((wq[:, :, :, :], a["wq"]), (wo[:, :, :, :], a["wo"]),
                             (wr[:, :, :, :], a["wr"]), (bq[:, :, :], a["bq"]),
                             (bo[:, :, :], a["bo"].partition_broadcast(P)),
                             (br[:, :, :], a["br"].partition_broadcast(P)),
                             (gates[:, :], a["gates"].partition_broadcast(P)),
                             (braw[:, :], a["biases"])):
                sp.dma_start(dst, src).then_inc(params_loaded, 16)

            def values(l):
                whole = FLAT // P
                for b in range(B):
                    n = l * B + b
                    sp.wait_ge(v_done, n + 1)
                    sp.dma_start(flat_values[l, b].rearrange("h s d -> s h d"),
                                 vals[:, :, :]).then_inc(v_stored, 16)
                    sp.wait_ge(v_stored, 16 * (n + 1))
                    gate(sp, v_blocks_done, n)
                    src = flat_values[l, b].rearrange("h s d -> (h s) d")
                    sp.dma_start(flat_v[:, 0:whole, :], src[0:whole * P].rearrange(
                        "(c p) d -> p c d", p=P)).then_inc(v_flat, 16)
                    sp.dma_start(flat_v[0:FLAT - whole * P, whole, :],
                                 src[whole * P:FLAT]).then_inc(v_flat, 16)

            def load_results(t, cl):
                K = TOPK[cl]
                gate(sp, added, adds(cl, t.at - 1) if cl or t.c > 1 or t.at is not t.c else 0)
                sp.dma_start(x2in[:, t.par, :], tile_of(attended[cl][bass.ds(t.at, 1)])
                             ).then_inc(results_loaded[t.par], 16)
                src = results[cl][SPARE:].rearrange("(k t p) d -> t p k d", k=K, p=P)
                sp.dma_start(ysb[:, t.par, 0:K, :], src[bass.ds(t.at, 1)].rearrange(
                    "a p k d -> (a p) k d")).then_inc(results_loaded[t.par], 16)

            def results_there(l):
                for r in range(4):
                    sp.wait_ge(y_scattered[r], 16 * uses(l + 1, r))
                    sp.wait_ge(x2_stored[r], 16 * (l + 1) * (NT // 4))

            def experts(l):
                sp.wait_ge(table_ready, l + 1)
                for e in range(E):
                    c = sp.value_load(cnt_i[0:1, e:e + 1], min_val=0, max_val=N)
                    sp.dma_start(dispatched[l][bass.ds(c + e * REGION, P), :],
                                 zero_rows[:, :]).then_inc(zeros_stored, 16)
                for r in range(4):
                    sp.wait_ge(scattered[r], scatter_count(l, r, NT // 4))
                sp.wait_ge(zeros_stored, 16 * (LAYERS * IDLE + E * (l + 1)))

                def load(t):
                    at = sp.value_load(tab[0:1, ROWAT, bass.ds(t.at, 1)], min_val=0,
                                       max_val=E * REGION + (IDLE - 1) * P)
                    before = MBASE[l] if isinstance(t.at, int) and t.at < 4 \
                        else t.at + (MBASE[l] - 3)
                    gate(sp, mT_ready, before)
                    gate(sp, y_at_done, before)
                    sp.dma_start(xm[:, t.slot, :], dispatched[l][bass.ds(at, P), :]
                                 ).then_inc(rows_loaded[t.slot], 16)

                for t in range(4):
                    load(Tile(None, t))
                loops = (MT[l] - 4) // 4
                with sp.Fori(0, loops) as j:
                    for u in range(4):
                        load(Tile(j, 4 + u))
                for t in range(4 + 4 * loops, MT[l]):
                    load(Tile(None, t))

            values(0)
            sp.wait_ge(consts_made, 1)
            for l in range(LAYERS):
                for k in range(IDLE):
                    sp.dma_start(dispatched[l][E * REGION + k * P:E * REGION + (k + 1) * P, :],
                                 idle_rows[:, :]).then_inc(zeros_stored, 16)
            for part, t in enumerate((b_hi, b_lo)):
                sp.wait_ge(bias_split, part + 1)
                sp.dma_start(split_bias[part].rearrange("e n -> (e n)").rearrange(
                    "(p n) -> p n", p=P), t[:, :].bitcast(F32)).then_inc(bias_stored, 16)
            with sp.Fori(0, NT // 4 - 1) as j:
                for u in range(4):
                    t = Tile(j, 4 + u)
                    gate(sp, x2_done, t.at - 3)
                    sp.dma_start(xt[:, t.slot, :], tile_of(x_tiles[bass.ds(t.at, 1)])
                                 ).then_inc(x_loaded[t.slot], 16)
            values(1)
            experts(0)
            results_there(0)
            for t in range(4):
                load_results(Tile(None, t), 0)
            with sp.Fori(0, NT // 4 - 1) as j:
                for u in range(4):
                    load_results(Tile(j, 4 + u), 0)
            experts(1)
            results_there(1)

            def store(t):
                gate(sp, added, adds(1, t.at + 1))
                sp.dma_start(tile_of(out_tiles[bass.ds(t.at, 1)]),
                             xt[:, t.slot, :]).then_inc(out_stored[t.slot], 16)

            for t in range(2):
                load_results(Tile(None, t), 1)
            with sp.Fori(0, NT // 4 - 1) as j:
                for u in range(4):
                    store(Tile(j, u))
                    load_results(Tile(j, u + 2), 1)
            for t in range(NT - 4, NT):
                store(Tile(None, t))
                if t + 2 < NT:
                    load_results(Tile(None, t + 2), 1)
            for r in range(4):
                sp.wait_ge(out_stored[r], 16 * (NT // 4))

        @block.gpsimd
        def _(pool):
            made = [0]

            def make(ins):
                made[0] += 1
                ins.then_inc(small_made, 1)

            def all_made():
                pool.wait_ge(small_made, made[0])

            def load_raw(e):
                pool.dma_start(raw[:, :], tile_of(a["weights"][bass.ds(e, 1)])
                               ).then_inc(raw_loaded, 16)

            def split(slot, e):
                pool.dma_start(w_bias[:, slot, :].bitcast(F32), split_bias[:, bass.ds(e, 1), :]
                               .rearrange("h a n -> h (a n)")).then_inc(bias_loaded, 16)
                gate(pool, raw_loaded, (e + 1) * 16)
                pool.tensor_scalar(w_hi[:, slot, :], raw[:, :], 1.0, 1.0, ALU.mult,
                                   ALU.mult).then_inc(hi_done, 1)
                gate(pool, hi_done, e + 1)
                pool.tensor_tensor(w_lo[:, slot, :], raw[:, :], w_hi[:, slot, :].bitcast(F32),
                                   ALU.subtract).then_inc(split_done, 1)

            load_raw(0)
            make(pool.memset(vals[:, :, :], 1.0))
            make(pool.memset(head_mask[:, :], 1.0))
            make(pool.memset(block_mask[:, :, :], 1.0))
            make(pool.memset(ident[:, :], 0.0))
            make(pool.memset(tri[:, :], 1.0))
            make(pool.memset(ones[:, :], 1.0))
            make(pool.memset(tri8[:, :, :], 1.0))
            make(pool.memset(zero_rows[:, :], 0.0))
            make(pool.memset(idle_rows[:, :], 0.0))
            make(pool.memset(flat_v[:, :, :], 0.0))
            make(pool.memset(alternate[:, 0:E:2], 1.0))
            make(pool.memset(alternate[:, 1:E:2], -1.0))
            all_made()

            def keep(t, pattern, compare, base, mult, fill=0.0):
                make(pool.affine_select(out=t, in_=t, pattern=pattern, compare_op=compare,
                                        fill=fill, base=base, channel_multiplier=mult))

            keep(head_mask[:, :], [[-DH, HC]], ALU.is_ge, 0, 1)
            all_made()
            keep(head_mask[:, :], [[DH, HC]], ALU.is_ge, DH - 1, -1)
            keep(ident[:, :], [[1, P]], ALU.not_equal, 0, -1, fill=1.0)
            for c in range(NCH):
                keep(block_mask[:, c, :], [[-S, SPAN]], ALU.is_ge, c * P - S * first_head(c), 1)
            all_made()
            for c in range(NCH):
                keep(block_mask[:, c, :], [[S, SPAN]], ALU.is_ge,
                     S - 1 - c * P + S * first_head(c), -1)
            keep(tri[:, :], [[1, P]], ALU.is_gt, 0, -1)
            keep(tri8[:, :, :], [[1, E], [-1, E]], ALU.is_ge, 0, 0)
            make(pool.memset(alternate[:, E - 1:E], 0.0))

            def count_up(t, pattern, base, mult):
                make(pool.iota(t, pattern=pattern, base=base, channel_multiplier=mult,
                               allow_small_or_imprecise_dtypes=True))

            count_up(expert_ids[:, :], [[1, E]], 0, 0)
            count_up(region_base[:, :], [[REGION, E]], 0, 0)
            count_up(rank_rows[:, :], [[N, 4]], 0, 0)
            count_up(token_ids[:, :], [[P, NT]], SPARE, 1)
            count_up(tile_edges[:, :], [[P, 15]], P, 0)
            count_up(tile_ids[:, :], [[1, max(MT)]], 0, 0)
            count_up(zero_rows[:, D:ROW], [[P, E]], 0, 1)
            count_up(idle_rows[:, D:ROW], [[P, E]], E * P, 1)
            make(pool.memset(eps_col[:, :], EPS))
            make(pool.memset(minus_half[:, :], -0.5))
            make(pool.memset(probs[:, :, FLAT:], 0.0))
            make(pool.tensor_copy(ones2[:, :], ones[0:2, :]))
            all_made()
            pool.sem_inc(consts_made, 1)

            pool.wait_ge(params_loaded, 16 * 8)
            pool.tensor_scalar(b_hi[:, :], braw[:, :], 1.0, 1.0, ALU.mult,
                               ALU.mult).then_inc(bias_split, 1)
            pool.wait_ge(bias_split, 1)
            pool.tensor_tensor(b_lo[:, :], braw[:, :], b_hi[:, :].bitcast(F32),
                               ALU.subtract).then_inc(bias_split, 1)
            pool.wait_ge(bo_scaled, LAYERS)

            def attention(l):
                def moments(A, T, mom, mv, rs, var, rstd, norm):
                    need(pool, norm, T)
                    need(pool, mom, T + 1)
                    pool.tensor_tensor(rs[:, 0:1], mv[:, 1:2], eps_col[:, :],
                                       ALU.add).then_inc(var, 1)
                    need(pool, var, T + 1)
                    pool.tensor_tensor(rs[:, 1:2], rs[:, 0:1], minus_half[:, :],
                                       ALU.pow).then_inc(rstd, 1)

                def step(j, s):
                    A, Q, F, _, Z = [stage(j, s, lag) for lag in range(5)]
                    if A:
                        moments(A, A.at + NT * l, moments1, mv1, rs1, var1, rstd1, xn_done)
                    if Q:
                        T = Q.at + NT * l
                        if l == 0:
                            need(pool, x_loaded[Q.slot], (Q.quad + 1) * 16)
                        else:
                            need(pool, added, adds(0, Q.at + 1))
                        need(pool, x2_done, T - 1)
                        pool.tensor_tensor(xg[:, Q.par, :], xt[:, Q.slot, :], bo[:, l, :],
                                           ALU.add).then_inc(xg_done, 1)
                    if F:
                        moments(F, F.at + NT * l, moments2, mv2, rs2, var2, rstd2, rows_done)
                    if Z:
                        T = Z.at + NT * l
                        gate(pool, slot_done, T + 1)
                        gate(pool, code_done, T + 1)
                        gate(pool, rows_done, T + 1)
                        for k in range(TOPK[l]):
                            pool.indirect_dma_start(
                                out=dispatched[l], out_offset=bass.IndirectOffsetOnAxis(
                                    ap=slot_at[:, Z.slot, k:k + 1], axis=0),
                                in_=rows[:, Z.slot, :], in_offset=None
                            ).then_inc(scattered[Z.slot], 16)
                attention_steps(pool, step)

            def experts(l):
                def step(j, s):
                    if t := row_tile(l, j, s, 1):
                        G = t.at + MBASE[l]
                        gate(pool, y_at_done, G + 1)
                        gate(pool, y_done, G + 1)
                        pool.indirect_dma_start(
                            out=results[l], out_offset=bass.IndirectOffsetOnAxis(
                                ap=y_at[:, t.slot:t.slot + 1], axis=0),
                            in_=y[:, t.slot, :], in_offset=None
                        ).then_inc(y_scattered[t.slot], 16)
                    t = row_tile(l, j, s, 0)
                    if t and not (j is None and s == 0):
                        read = lambda n, lo, hi: pool.value_load(
                            tab[0:1, n, bass.ds(t.at, 1)], min_val=lo, max_val=hi)
                        flags = [read(SPLIT0, 0, 1), read(SPLIT1, 0, 1)]
                        nxt = read(NEXT, 1, LAYERS * E - 1)
                        after = read(LOAD, 2, LAYERS * E - 1)
                        for slot in range(2):
                            with pool.If(flags[slot]):
                                split(slot, nxt)
                                gate(pool, split_done, nxt + 1)
                                load_raw(after)
                                pool.nop()
                expert_steps(pool, l, step)

            pool.wait_ge(bias_stored, 32)
            split(0, 0)
            pool.wait_ge(split_done, 1)
            load_raw(1)
            attention(0)
            split(1, 1)
            pool.wait_ge(split_done, 2)
            load_raw(2)
            pool.wait_ge(table_ready, 1)
            experts(0)
            split(1, E + 1)
            pool.wait_ge(split_done, E + 2)
            load_raw(E + 2)
            attention(1)
            pool.wait_ge(table_ready, 2)
            experts(1)
            pool.wait_ge(raw_loaded, 16 * (LAYERS * E + 1))

        @block.scalar
        def _(act):
            act.wait_ge(params_loaded, 16 * 8)
            act.activation(tgates[:, :], gates[:, :], ACT.Tanh).then_inc(gates_ready, 1)
            act.activation(wq_hi[:, :, :, :], wq[:, :, :, :], ACT.Copy).then_inc(wq_hi_done, 1)
            act.wait_ge(gates_ready, 1)
            for l in range(LAYERS):
                act.activation(bo[:, l, :], bo[:, l, :], ACT.Copy, scale=tgates[:, l:l + 1]
                               ).then_inc(bo_scaled, 1)

            def combine_weights(at, cl):
                C = at + NT * cl
                need(act, share_done, C)
                need(act, rsum_done, C)
                need(act, below_done, C + 1)
                act.activation(expw[:, 0:TOPK[cl]], below[:, 0:TOPK[cl]], ACT.Exp,
                               accum_out=wsum[:, :]).then_inc(expw_done, 1)

            def attention(l):
                def step(j, s):
                    A, Q, F, R, Z = [stage(j, s, lag) for lag in range(5)]
                    if Q:
                        T = Q.at + NT * l
                        need(act, q_ready, T)
                        need(act, xnT_ready, T + 1)
                        act.activation(xT_hi[:, :], ps[:, 0, 0:D], ACT.Copy
                                       ).then_inc(xT_hi_done, 1)
                    if A and l:
                        combine_weights(A.at, 0)
                    if F:
                        T = F.at + NT * l
                        need(act, pv_ready, T)
                        for n, (c0, c1) in enumerate(GROUPS):
                            need(act, pT_ready, T * 3 + n + 1)
                            act.activation(probsT[:, c0 * P:c1 * P],
                                           ps[:, PT_BANK + n % 2, 0:(c1 - c0) * P],
                                           ACT.Copy).then_inc(pT_copied, 1)
                    if Q:
                        T = Q.at + NT * l
                        need(act, scores_ready, T)
                        need(act, q_ready, T + 1)
                        for c in range(KD):
                            act.activation(q_hi[:, c, :], ps[:, 1, c * P:(c + 1) * P],
                                           ACT.Identity, bias=bq[:, l, c:c + 1]
                                           ).then_inc(q_hi_done, 1)
                    if F:
                        T = F.at + NT * l
                        need(act, proj_ready, T)
                        need(act, oT_ready, T + 1)
                        act.activation(oT[:, :], ps[:, 1, 0:D], ACT.Copy).then_inc(oT_copied, 1)
                    if R:
                        T = R.at + NT * l
                        need(act, logits_ready, T)
                        need(act, x2T_ready, T + 1)
                        act.activation(x2T[:, :], ps[:, 0, 0:D], ACT.Copy
                                       ).then_inc(x2T_copied, 1)
                    if Q:
                        T = Q.at + NT * l
                        need(act, shifted, T + 1)
                        act.activation(probs[:, Q.par, 0:FLAT], probs[:, Q.par, 0:FLAT], ACT.Exp,
                                       scale=(DH ** -0.5 if l == 0 else 1.0)
                                       ).then_inc(exp_done, 1)
                    if Z:
                        T = Z.at + NT * l
                        need(act, x2_done, T + 1)
                        need(act, best_kept, T + 1)
                        act.dma_start(tile_of(attended[l][bass.ds(Z.at, 1)]), x2[:, Z.slot, :]
                                      ).then_inc(x2_stored[Z.slot], 16)
                attention_steps(act, step)

            def experts(l):
                halves = KH[l] // 4

                def row_part(t):
                    need(act, hid_ready, (t.at + MBASE[l]) * 2)
                    need(act, mT_ready, t.at + MBASE[l] + 1)
                    act.activation(xT_hi[:, :], ps[:, 0, 0:D], ACT.Copy).then_inc(mT_hi_done, 1)

                def step(j, s):
                    t = row_tile(l, j, s, 0)
                    if t and l == 0:
                        need(act, hT_ready, t.at * 2)
                        need(act, hid_ready, t.at * 2 + 2)
                        act.activation(hid[:, SC:WIDE], ps[:, 2, :], ACT.Relu
                                       ).then_inc(hid_act, 1)
                    if t and l == 1:
                        need(act, hid_dve, MBASE[1] + t.at)
                        need(act, gate_done, t.at + 1)
                        act.activation(sig_s, gate_s, ACT.Sigmoid, scale=1.702
                                       ).then_inc(sig_done, 1)
                    if n := row_tile(l, j, s, -1):
                        row_part(n)
                    if t:
                        need(act, y_ready, t.at + MBASE[l])
                        for h in range(halves):
                            need(act, hT_ready, t.at * halves + (HBASE[l] + h + 1))
                            act.activation(hT_hi[:, h * SC:(h + 1) * SC], ps[:, 3 + h, :],
                                           ACT.Copy).then_inc(hT_hi_done, 1)
                row_part(Tile(None, 0))
                expert_steps(act, l, step)

            attention(0)
            experts(0)
            attention(1)
            experts(1)
            with act.Fori(0, NT) as t:
                combine_weights(t, 1)

        @block.vector
        def _(dve):
            dve.wait_ge(wq_hi_done, 1)
            dve.tensor_tensor(wq_lo[:, :, :, :], wq[:, :, :, :],
                              wq_hi[:, :, :, :].bitcast(F32), ALU.subtract
                              ).then_inc(wq_lo_done, 1)
            dve.wait_ge(consts_made, 1)

            def over(ap, axis, n):
                view = ap.unsqueeze(axis)
                return view.broadcast_to([n if i == axis else size
                                          for i, size in enumerate(view.shape)])

            def keys_values(l):
                dve.wait_ge(wkv_loaded, 16 * 4)
                for b in range(B):
                    for c in range(KD):
                        n = (l * B + b) * KD + c
                        dve.wait_ge(kT_ready, n + 1)
                        dve.tensor_scalar(kT[:, :], ps[:, n % 2, 0:S], bk[:, l, c:c + 1], None,
                                          ALU.add).then_inc(kT_done, 1)
                        dve.wait_ge(kT_done, n + 1)
                        dve.tensor_copy(kT_hi[:, :], kT[:, :]).then_inc(kT_hi_done, 1)
                        dve.wait_ge(kT_hi_done, n + 1)
                        dve.tensor_tensor(kT_lo[:, :], kT[:, :], kT_hi[:, :].bitcast(F32),
                                          ALU.subtract).then_inc(kT_lo_done, 1)
                        dve.wait_ge(kT_lo_done, n + 1)
                        for part, to in ((kT_hi[:, :].bitcast(F32), key_hi), (kT_lo[:, :], key_lo)):
                            dve.tensor_tensor(
                                to[:, b, c, :].rearrange("p (h s) -> p h s", h=HC),
                                over(part, 1, HC),
                                over(head_mask[:, :], 2, S),
                                ALU.mult).then_inc(keys_done, 1)
                    n = l * B + b
                    dve.wait_ge(v_ready, n + 1)
                    need(dve, v_stored, 16 * n)
                    dve.tensor_tensor(
                        vals[:, :, 0:DH], ps[0:S, 2, 0:D].rearrange("p (h d) -> p h d", h=H),
                        bv[:, l, :].rearrange("p (h d) -> p h d", h=H), ALU.add
                    ).then_inc(v_done, 1)
                for b in range(B):
                    n = l * B + b
                    dve.wait_ge(v_flat, 32 * (n + 1))
                    for r in range(SPAN):
                        ins = dve.tensor_tensor(
                            v_blocks[:, b, :, r * DV:(r + 1) * DV], flat_v[:, :, :],
                            over(block_mask[:, :, r], 2, DV), ALU.mult)
                    ins.then_inc(v_blocks_done, 1)

            def combine(t, cl):
                K, C = TOPK[cl], t.at + NT * cl
                dve.wait_ge(results_loaded[t.par], (t.pair + (NT // 2 * cl + 1)) * 32)
                dve.tensor_scalar(below[:, 0:K], x2in[:, t.par, D:D + K],
                                  x2in[:, t.par, D:D + 1], None, ALU.subtract
                                  ).then_inc(below_done, 1)
                need(dve, expw_done, C + 1)
                dve.reciprocal(rsum[:, :], wsum[:, :]).then_inc(rsum_done, 1)
                need(dve, rsum_done, C + 1)
                dve.tensor_scalar(share[:, 0:K], expw[:, 0:K], rsum[:, :],
                                  tgates[:, 2 + cl:3 + cl], ALU.mult, ALU.mult
                                  ).then_inc(share_done, 1)
                need(dve, share_done, C + 1)
                for k in range(K):
                    if k:
                        dve.wait_ge(added, adds(cl, t.at) + k)
                    prev = xt[:, t.slot, :] if k else x2in[:, t.par, 0:D]
                    dve.scalar_tensor_tensor(
                        out=xt[:, t.slot, :], in0=ysb[:, t.par, k, :], scalar=share[:, k:k + 1],
                        in1=prev, op0=ALU.mult, op1=ALU.add).then_inc(added, 1)

            def attention(l):
                K = TOPK[l]

                def first_moments(A):
                    T = A.at + NT * l
                    if l == 0:
                        need(dve, x_loaded[A.slot], (A.quad + 1) * 16)
                    else:
                        combine(A, 0)
                        need(dve, added, adds(0, A.at + 1))
                    dve.bn_stats(st1[:, :], xt[:, A.slot, :]).then_inc(stats1, 1)
                    gate(dve, stats1, T + 1)
                    dve.bn_aggr(mv1[:, :], st1[:, :]).then_inc(moments1, 1)

                def softmax_shift(Q):
                    T = Q.at + NT * l
                    a_cols, n_a = HPB * S, full * HPB
                    banks = ps[:, SCORE_BANK:SCORE_BANK + full, 0:a_cols].rearrange(
                        "p b (h s) -> p b h s", h=HPB)
                    last = ps[:, SCORE_BANK + full, 0:rest * S].rearrange(
                        "p (h s) -> p h s", h=rest)
                    top_a = top[:, 0:n_a].rearrange("p (b h) -> p b h", b=full)
                    need(dve, scores_ready, T + 1)
                    dve.tensor_reduce(top_a, banks, AX.X, ALU.max).then_inc(max_done, 1)
                    dve.tensor_reduce(top[:, n_a:H], last, AX.X, ALU.max).then_inc(max_done, 1)
                    need(dve, pT_ready, T * 3 - 3)
                    need(dve, max_done, T * 2 + 2)
                    dve.tensor_tensor(
                        probs[:, Q.par, 0:n_a * S].rearrange("p (b h s) -> p b h s", b=full,
                                                             h=HPB),
                        banks, over(top_a, 3, S), ALU.subtract
                    ).then_inc(shifted_part, 1)
                    dve.tensor_tensor(
                        probs[:, Q.par, n_a * S:FLAT].rearrange("p (h s) -> p h s", h=rest),
                        last, over(top[:, n_a:H], 2, S), ALU.subtract
                    ).then_inc(shifted, 1)

                def choose(R, Z):
                    if R:
                        T = R.at + NT * l
                        need(dve, logits_ready, T + 1)
                        dve.tensor_tensor(logits[:, :], ps[:, 0, D:D + E], br[:, l, :],
                                          ALU.add).then_inc(logits_done, 1)
                    if Z:
                        TZ = Z.at + NT * l
                        need(dve, count_ready, TZ + 1)
                        dve.tensor_tensor(slots[:, :], ps[:, 0, D + E:D + 2 * E],
                                          region_base[:, :], ALU.add).then_inc(slots_done, 1)
                    if R:
                        gate(dve, logits_done, T + 1)
                        dve.max(best[:, :], logits[:, :]).then_inc(best_done, 1)
                        gate(dve, best_done, T + 1)
                        dve.max_index(best_at[:, :], best[:, :], logits[:, :]
                                      ).then_inc(best_at_done, 1)
                        need(dve, x2_done, T + 1)
                        dve.tensor_copy(x2[:, R.slot, D:D + 4], best[:, 0:4]
                                        ).then_inc(best_kept, 1)
                        need(dve, best_at_done, T + 1)
                        dve.tensor_copy(best_f[:, 0:K], best_at[:, 0:K]).then_inc(best_f_done, 1)
                    if Z:
                        need(dve, slots_done, TZ + 1)
                        dve.tensor_tensor(
                            slot_k[:, 0:K, :],
                            chosen[:, Z.slot, :, 0:K].rearrange("p e k -> p k e"),
                            over(slots[:, :], 1, K), ALU.mult
                        ).then_inc(slot_k_done, 1)
                    if R:
                        need(dve, best_f_done, T + 1)
                        dve.tensor_tensor(
                            chosen[:, R.slot, :, 0:K],
                            over(expert_ids[:, :], 2, K),
                            over(best_f[:, 0:K], 1, E),
                            ALU.is_equal).then_inc(chosen_done, 1)
                    if Z:
                        need(dve, slot_k_done, TZ + 1)
                        dve.tensor_reduce(slot_f[:, 0:K], slot_k[:, 0:K, :], AX.X,
                                          ALU.add).then_inc(slot_f_done, 1)
                    if R:
                        need(dve, chosen_done, T + 1)
                        dve.tensor_reduce(mask[:, R.par, :], chosen[:, R.slot, :, 0:K], AX.X,
                                          ALU.add).then_inc(mask_done, 1)
                        dve.tensor_tensor(
                            ranked[:, :, 0:K], chosen[:, R.slot, :, 0:K],
                            over(rank_rows[:, 0:K], 1, E),
                            ALU.mult).then_inc(ranked_done, 1)
                    if Z:
                        need(dve, scattered[Z.slot], scatter_count(l, Z.slot, Z.quad))
                        need(dve, slot_f_done, TZ + 1)
                        dve.tensor_copy(slot_at[:, Z.slot, 0:K], slot_f[:, 0:K]
                                        ).then_inc(slot_done, 1)
                    if R:
                        need(dve, mask_done, T + 1)
                        need(dve, seen_done, T)
                        dve.tensor_tensor(seen[:, 1 - R.par, :], seen[:, R.par, :],
                                          mask[:, R.par, :], ALU.add).then_inc(seen_done, 1)
                        need(dve, ranked_done, T + 1)
                        dve.tensor_reduce(ranks[:, :], ranked[:, :, 0:K], AX.X,
                                          ALU.add).then_inc(ranks_done, 1)
                        need(dve, ranks_done, T + 1)
                        dve.tensor_scalar(rows[:, R.slot, D:ROW], ranks[:, :],
                                          token_ids[:, bass.ds(R.at, 1)], None, ALU.add
                                          ).then_inc(code_done, 1)

                def step(j, s):
                    A, Q, F, R, Z = [stage(j, s, lag) for lag in range(5)]
                    if Q:
                        T = Q.at + NT * l
                        need(dve, xT_hi_done, T + 1)
                        dve.tensor_tensor(xT_lo[:, :], ps[:, 0, 0:D], xT_hi[:, :].bitcast(F32),
                                          ALU.subtract).then_inc(xT_lo_done, 1)
                    if A:
                        first_moments(A)
                    if Q:
                        need(dve, q_hi_done, T * 2 + 2)
                        for c in range(KD):
                            dve.scalar_tensor_tensor(
                                out=q_lo[:, c, :], in0=ps[:, 1, c * P:(c + 1) * P],
                                scalar=bq[:, l, c:c + 1], in1=q_hi[:, c, :].bitcast(F32),
                                op0=ALU.add, op1=ALU.subtract).then_inc(q_lo_done, 1)
                    if A:
                        TA = A.at + NT * l
                        need(dve, xnT_ready, TA - 1)
                        need(dve, rstd1, TA + 1)
                        dve.tensor_scalar(xn[:, A.par, :], xt[:, A.slot, :], mv1[:, 0:1],
                                          rs1[:, 1:2], ALU.subtract, ALU.mult
                                          ).then_inc(xn_done, 1)
                    if F:
                        TF = F.at + NT * l
                        out = ps[:, 7, 0:H * DV].rearrange("p (h d) -> p h d", h=H)
                        need(dve, pv_ready, TF + 1)
                        dve.reciprocal(rden[:, :].rearrange("p (h o) -> p h o", o=1),
                                       out[:, :, DH:DV]).then_inc(rden_done, 1)
                        need(dve, oT_ready, TF)
                        need(dve, rden_done, TF + 1)
                        dve.tensor_tensor(ob[:, :].rearrange("p (h d) -> p h d", h=H),
                                          out[:, :, 0:DH],
                                          over(rden[:, :], 2, DH),
                                          ALU.mult).then_inc(o_done, 1)
                    if Q:
                        softmax_shift(Q)
                    if F:
                        need(dve, x2_stored[F.slot], (F.quad + l * (NT // 4)) * 16)
                        need(dve, xg_done, TF + 1)
                        need(dve, proj_ready, TF + 1)
                        dve.scalar_tensor_tensor(
                            out=x2[:, F.slot, 0:D], in0=ps[:, 7, 0:D], scalar=tgates[:, l:l + 1],
                            in1=xg[:, F.par, :], op0=ALU.mult, op1=ALU.add
                        ).then_inc(x2_done, 1)
                        need(dve, x2_done, TF + 1)
                        dve.bn_stats(st2[:, :], x2[:, F.slot, 0:D]).then_inc(stats2, 1)
                        gate(dve, stats2, TF + 1)
                        dve.bn_aggr(mv2[:, :], st2[:, :]).then_inc(moments2, 1)
                    choose(R, Z)
                    if F:
                        need(dve, scattered[F.slot], scatter_count(l, F.slot, F.quad))
                        need(dve, rstd2, TF + 1)
                        dve.tensor_scalar(rows[:, F.slot, 0:D], x2[:, F.slot, 0:D], mv2[:, 0:1],
                                          rs2[:, 1:2], ALU.subtract, ALU.mult
                                          ).then_inc(rows_done, 1)

                dve.memset(seen[:, 0, :], 0.0).then_inc(seen_zero, 1)
                dve.wait_ge(seen_zero, l + 1)
                attention_steps(dve, step)

            steps = [0]

            def table(l):
                M = MT[l]
                ids, end, tiles = tile_ids[:, 0:M], t_end[:, :], t_tiles[:, :]
                le, m, e_, d = t_le[:, 0:M, :], t_m[:, 0:M, :], t_e[:, 0:M], t_d[:, 0:M]

                def then(ins):
                    steps[0] += 1
                    ins.then_inc(table_step, 1)
                    dve.wait_ge(table_step, steps[0])

                def row(n):
                    return tab_f[:, n, 0:M]

                dve.wait_ge(total_ready, l + 1)
                then(dve.tensor_copy(t_cnt[:, :], ps[0:1, 0, 0:E]))
                then(dve.tensor_copy(cnt_i[:, :], t_cnt[:, :]))
                then(dve.tensor_tensor(t_gt[:, :, :], over(t_cnt[:, :], 2, 15),
                                       over(tile_edges[:, :], 1, E),
                                       ALU.is_gt))
                then(dve.tensor_reduce(tiles, t_gt[:, :, :], AX.X, ALU.add))
                then(dve.tensor_scalar(tiles, tiles, 1.0, None, ALU.add))
                then(dve.tensor_tensor(t_tri[:, :, :], over(tiles, 1, E),
                                       tri8[:, :, :], ALU.mult))
                then(dve.tensor_reduce(end, t_tri[:, :, :], AX.X, ALU.add))
                then(dve.tensor_tensor(le, over(end, 1, M),
                                       over(ids, 2, E), ALU.is_le))
                then(dve.tensor_reduce(e_, le, AX.X, ALU.add))
                then(dve.tensor_tensor(m, le, over(tiles, 1, M), ALU.mult))
                then(dve.tensor_reduce(d, m, AX.X, ALU.add))
                then(dve.tensor_tensor(d, ids, d, ALU.subtract))
                then(dve.tensor_scalar(row(ROWAT), e_, float(REGION), None, ALU.mult))
                then(dve.scalar_tensor_tensor(out=row(ROWAT), in0=d, scalar=float(P),
                                              in1=row(ROWAT), op0=ALU.mult, op1=ALU.add))
                then(dve.tensor_tensor(m, le, over(alternate[:, :], 1, M),
                                       ALU.mult))
                then(dve.tensor_reduce(row(SLOT), m, AX.X, ALU.add))
                then(dve.tensor_scalar(row(EXPERT), e_, float(E - 1), None, ALU.min))
                then(dve.tensor_scalar(t_new[:, 0:M], e_, float(E), None, ALU.is_ge))
                then(dve.scalar_tensor_tensor(out=d, in0=d, scalar=1.0 - E, in1=t_new[:, 0:M],
                                              op0=ALU.add, op1=ALU.mult))
                then(dve.tensor_tensor(row(PLACE), row(EXPERT), d, ALU.add))
                then(dve.memset(t_new[:, 0:1], 0.0))
                then(dve.tensor_tensor(t_new[:, 1:M], row(EXPERT)[:, 1:M],
                                       row(EXPERT)[:, 0:M - 1], ALU.not_equal))
                if l == LAYERS - 1:
                    then(dve.scalar_tensor_tensor(
                        out=t_new[:, 0:M], in0=row(EXPERT), scalar=float(E - 1),
                        in1=t_new[:, 0:M], op0=ALU.is_lt, op1=ALU.mult))
                then(dve.tensor_tensor(row(SPLIT0), t_new[:, 0:M], row(SLOT), ALU.mult))
                then(dve.tensor_tensor(row(SPLIT1), t_new[:, 0:M], row(SPLIT0), ALU.subtract))
                last = float(LAYERS * E - 1)
                then(dve.tensor_scalar(row(NEXT), row(EXPERT), float(l * E + 1), last, ALU.add,
                                       ALU.min))
                then(dve.tensor_scalar(row(LOAD), row(EXPERT), float(l * E + 2), last, ALU.add,
                                       ALU.min))
                dve.tensor_copy(tab[:, :, 0:M], tab_f[:, :, 0:M]).then_inc(table_ready, 1)

            def experts(l):
                halves = KH[l] // 4

                def row_part(t):
                    G = t.at + MBASE[l]
                    place = dve.value_load(tab[0:1, PLACE, bass.ds(t.at, 1)], min_val=0,
                                           max_val=E - 1)
                    need(dve, mT_hi_done, G + 1)
                    dve.tensor_tensor(xT_lo[:, :], ps[:, 0, 0:D], xT_hi[:, :].bitcast(F32),
                                      ALU.subtract).then_inc(mT_lo_done, 1)
                    gate(dve, y_scattered[t.slot], (t.quad + uses(l, t.slot)) * 16)
                    gate(dve, rows_loaded[t.slot], (t.quad + (uses(l, t.slot) + 1)) * 16)
                    dve.tensor_copy(y_at[:, t.slot:t.slot + 1],
                                    xm[:, t.slot, bass.ds(place + D, 1)]).then_inc(y_at_done, 1)

                def hidden(t):
                    T = t.at
                    if l == 0:
                        need(dve, hT_ready, T * halves)
                        need(dve, hid_ready, T * 2 + 1)
                        dve.tensor_scalar(hid[:, 0:SC], ps[:, 1, :], 0.0, None, ALU.max
                                          ).then_inc(hid_dve, 1)
                        return
                    need(dve, hid_ready, (T + MBASE[1]) * 2 + 1)
                    dve.tensor_scalar(gate_s, ps[:, 1, :], 7.0, None, ALU.min
                                      ).then_inc(gate_done, 1)
                    need(dve, hid_ready, (T + MBASE[1]) * 2 + 2)
                    dve.tensor_scalar(up_s, ps[:, 2, :], 7.0, -7.0, ALU.min, ALU.max
                                      ).then_inc(up_done, 1)
                    need(dve, up_done, T + 1)
                    dve.scalar_tensor_tensor(out=up_s, in0=up_s, scalar=1.0, in1=gate_s,
                                             op0=ALU.add, op1=ALU.mult
                                             ).then_inc(up_gate_done, 1)
                    need(dve, hT_ready, T * halves + HBASE[1])
                    need(dve, sig_done, T + 1)
                    need(dve, up_gate_done, T + 1)
                    dve.tensor_tensor(hid[:, 0:SC], up_s, sig_s, ALU.mult).then_inc(hid_dve, 1)

                def step(j, s):
                    t, n, y_t = [row_tile(l, j, s, lag) for lag in (0, -1, 1)]
                    if t:
                        hidden(t)
                    if n:
                        row_part(n)
                    if y_t:
                        need(dve, y_scattered[y_t.slot],
                             (y_t.quad + uses(l, y_t.slot)) * 16)
                        need(dve, y_ready, y_t.at + MBASE[l] + 1)
                        dve.tensor_copy(y[:, y_t.slot, :], ps[:, 5, 0:D]).then_inc(y_done, 1)
                    if t:
                        for h in range(halves):
                            need(dve, hT_hi_done, t.at * halves + (HBASE[l] + h + 1))
                            dve.tensor_tensor(
                                hT_lo[:, h * SC:(h + 1) * SC], ps[:, 3 + h, :],
                                hT_hi[:, h * SC:(h + 1) * SC].bitcast(F32), ALU.subtract
                            ).then_inc(hT_lo_done, 1)
                dve.wait_ge(table_ready, l + 1)
                row_part(Tile(None, 0))
                expert_steps(dve, l, step)

            keys_values(0)
            attention(0)
            table(0)
            keys_values(1)
            experts(0)
            attention(1)
            table(1)
            experts(1)
            for t in range(4):
                combine(Tile(None, t), 1)
            with dve.Fori(0, NT // 4 - 1) as j:
                for u in range(4):
                    t = Tile(j, 4 + u)
                    dve.wait_ge(out_stored[t.slot], t.quad * 16)
                    combine(t, 1)

        @block.tensor
        def _(pe):
            def keys_values(l):
                need(pe, slots_done, NT * l)
                need(pe, logits_done, NT * l)
                need(pe, table_ready, l)
                need(pe, oT_copied, NT * l)
                need(pe, shifted, NT * l)
                for b in range(B):
                    for c in range(KD):
                        n = (l * B + b) * KD + c
                        need(pe, kT_done, n - 1)
                        for k in range(KD):
                            mm = pe.matmul(ps[:, n % 2, 0:S], wkv[:, l, 0, k, c * P:(c + 1) * P],
                                           ctxT[:, b, k, :], start=k == 0, stop=k == KD - 1)
                        mm.then_inc(kT_ready, 1)
                    need(pe, v_done, l * B + b)
                    for k in range(KD):
                        mm = pe.matmul(ps[0:S, 2, 0:D], ctxT[:, b, k, :], wkv[:, l, 1, k, :],
                                       start=k == 0, stop=k == KD - 1)
                    mm.then_inc(v_ready, 1)
                pe.wait_ge(keys_done, 2 * B * KD * (l + 1))
                pe.wait_ge(v_blocks_done, B * (l + 1))
                pe.wait_ge(v_done, B * (l + 1))

            def transposed(bank, src, ready):
                for c in range(KD):
                    mm = pe.transpose(ps[:, bank, c * P:(c + 1) * P],
                                      src[:, c * P:(c + 1) * P], ident[:, :])
                mm.then_inc(ready, 1)

            def split_product(out, terms, start=True, stop=True):
                for n, (l_hi, l_lo, r_hi, r_lo) in enumerate(terms):
                    for m, (lhs, rhs) in enumerate(((l_hi, r_hi), (l_hi, r_lo), (l_lo, r_hi))):
                        mm = pe.matmul(out, lhs, rhs, start=start and n == 0 and m == 0,
                                       stop=stop and n == len(terms) - 1 and m == 2)
                return mm

            def attention(l):
                def scores(Q):
                    T = Q.at + NT * l
                    batch = Q.at // (NT // B)
                    need(pe, shifted, T)
                    need(pe, q_lo_done, T * 2 + 2)
                    for c, h, n in pieces:
                        at = (h - c * HC) * S
                        keys = [key[:, bass.ds(batch, 1), c, at:at + n * S].rearrange(
                            "p a n -> p (a n)") for key in (key_hi, key_lo)]
                        mm = split_product(
                            ps[:, SCORE_BANK + h // HPB, h % HPB * S:(h % HPB + n) * S],
                            [(q_hi[:, c, :], q_lo[:, c, :], *keys)])
                    mm.then_inc(scores_ready, 1)

                def step(j, s):
                    _, Q, F, R, Z = [stage(j, s, lag) for lag in range(5)]
                    if Q:
                        T = Q.at + NT * l
                        if l == 0 or j is not None or s > 4:
                            need(pe, logits_done, T - 2)
                            need(pe, slots_done, T - 3)
                        need(pe, xn_done, T + 1)
                        transposed(0, xn[:, Q.par, :], xnT_ready)
                    if F:
                        TF = F.at + NT * l
                        need(pe, exp_done, TF + 1)
                        for n, (c0, c1) in enumerate(GROUPS):
                            need(pe, pT_copied, TF * 3 + (1 if n == 2 else 0))
                            for c in range(c0, c1):
                                mm = pe.transpose(
                                    ps[:, PT_BANK + n % 2, (c - c0) * P:(c - c0 + 1) * P],
                                    probs[:, F.par, c * P:(c + 1) * P], ident[:, :])
                            mm.then_inc(pT_ready, 1)
                    if Q:
                        need(pe, oT_copied, T - 1)
                        need(pe, xT_lo_done, T + 1)
                        for c in range(KD):
                            mm = split_product(ps[:, 1, c * P:(c + 1) * P], [
                                (wq_hi[:, l, k, c * P:(c + 1) * P],
                                 wq_lo[:, l, k, c * P:(c + 1) * P],
                                 xT_hi[:, k * P:(k + 1) * P], xT_lo[:, k * P:(k + 1) * P])
                                for k in range(KD)])
                        mm.then_inc(q_ready, 1)
                    if F:
                        need(pe, x2_done, TF)
                        batch = F.at // (NT // B)
                        for n, (c0, c1) in enumerate(GROUPS):
                            need(pe, pT_copied, TF * 3 + n + 1)
                            for c in range(c0, c1):
                                at = first_head(c) * DV
                                mm = pe.matmul(
                                    ps[:, 7, at:at + SPAN * DV], probsT[:, c * P:(c + 1) * P],
                                    v_blocks[:, bass.ds(batch, 1), c, :].rearrange(
                                        "p a n -> p (a n)"),
                                    start=c == 0, stop=c == NCH - 1, skip_group_check=True)
                        mm.then_inc(pv_ready, 1)
                    if Q:
                        scores(Q)
                    if F:
                        need(pe, o_done, TF + 1)
                        transposed(1, ob, oT_ready)
                    if R:
                        TR = R.at + NT * l
                        need(pe, rows_done, TR + 1)
                        transposed(0, rows[:, R.slot, :], x2T_ready)
                    if F:
                        need(pe, oT_copied, TF + 1)
                        for k in range(KD):
                            mm = pe.matmul(ps[:, 7, 0:D], oT[:, k * P:(k + 1) * P],
                                           wo[:, l, k, :], start=k == 0, stop=k == KD - 1)
                        mm.then_inc(proj_ready, 1)
                    if R:
                        need(pe, x2T_copied, TR + 1)
                    if Z:
                        TZ = Z.at + NT * l
                        need(pe, mask_done, TZ + 1)
                        pe.matmul(ps[:, 0, D + E:D + 2 * E], tri[:, :], mask[:, Z.par, :],
                                  start=True, stop=False)
                        mm = pe.matmul(ps[:, 0, D + E:D + 2 * E], ones[:, :],
                                       seen[:, Z.par, :], start=False, stop=True)
                        mm.then_inc(count_ready, 1)
                    if R:
                        for k in range(KD):
                            mm = pe.matmul(ps[:, 0, D:D + E], x2T[:, k * P:(k + 1) * P],
                                           wr[:, l, k, :], start=k == 0, stop=k == KD - 1)
                        mm.then_inc(logits_ready, 1)
                attention_steps(pe, step)
                pe.wait_ge(slots_done, NT * (l + 1))
                pe.wait_ge(seen_done, NT * (l + 1))
                pe.matmul(ps[:, 0, 0:E], ones[:, :], seen[:, 0, :], start=True,
                          stop=True).then_inc(total_ready, 1)

            def experts(l):
                def row_part(t):
                    G = t.at + MBASE[l]
                    need(pe, mT_lo_done, G)
                    pe.wait_ge(rows_loaded[t.slot], (t.quad + (uses(l, t.slot) + 1)) * 16)
                    transposed(0, xm[:, t.slot, :], mT_ready)

                def weights_slot(t):
                    return pe.value_load(tab[0:1, SLOT, bass.ds(t.at, 1)], min_val=0, max_val=1)

                def at_slot(w, slot, c0, n):
                    return w[:, bass.ds(slot, 1), c0:c0 + n].rearrange("p a n -> p (a n)")

                def first_product(t):
                    T = t.at
                    slot = weights_slot(t)
                    expert = pe.value_load(tab[0:1, EXPERT, bass.ds(T, 1)], min_val=0,
                                           max_val=E - 1)
                    pe.wait_ge(split_done, expert + (l * E + 1))
                    pe.wait_ge(bias_loaded, (expert + (l * E + 1)) * 16)
                    need(pe, mT_lo_done, T + MBASE[l] + 1)
                    for half in range(2):
                        done = ((hid_dve, hid_act), (gate_done, up_done))[l][half]
                        need(pe, done, T)
                        split_product(ps[:, 1 + half, :], [
                            (xT_hi[:, k * P:(k + 1) * P], xT_lo[:, k * P:(k + 1) * P],
                             at_slot(w_hi, slot, k * WIDE + half * SC, SC),
                             at_slot(w_lo, slot, k * WIDE + half * SC, SC)) for k in range(KD)],
                            stop=False)
                        pe.matmul(ps[:, 1 + half, :], ones2[:, :],
                                  at_slot(w_bias, slot, half * SC, SC), start=False, stop=True
                                  ).then_inc(hid_ready, 1)

                def second_product(t):
                    G = t.at + MBASE[l]
                    halves = KH[l] // 4
                    slot = weights_slot(t)
                    need(pe, y_done, G)
                    need(pe, hT_lo_done, t.at * halves + (HBASE[l] + halves))
                    split_product(ps[:, 5, 0:D], [
                        (hT_hi[:, k * P:(k + 1) * P], hT_lo[:, k * P:(k + 1) * P],
                         at_slot(w_hi, slot, W2AT + k * D, D),
                         at_slot(w_lo, slot, W2AT + k * D, D)) for k in range(KH[l])],
                        stop=False)
                    pe.matmul(ps[:, 5, 0:D], ones2[:, :], at_slot(w_bias, slot, WIDE, D),
                              start=False, stop=True).then_inc(y_ready, 1)

                def hidden_transposes(t):
                    halves = KH[l] // 4
                    need(pe, hT_lo_done, t.at * halves + HBASE[l])
                    for h in range(halves):
                        need(pe, ((hid_dve, hid_act)[h] if l == 0 else hid_dve),
                             t.at + (MBASE[l] + 1))
                        for c in range(4):
                            mm = pe.transpose(ps[:, 3 + h, c * P:(c + 1) * P],
                                              hid[:, h * SC + c * P:h * SC + (c + 1) * P],
                                              ident[:, :])
                        mm.then_inc(hT_ready, 1)

                def step(j, s):
                    t, n, y_t = [row_tile(l, j, s, lag) for lag in (0, -1, 1)]
                    if t:
                        first_product(t)
                    if n:
                        row_part(n)
                    if y_t:
                        second_product(y_t)
                    if t:
                        hidden_transposes(t)
                pe.wait_ge(table_ready, l + 1)
                row_part(Tile(None, 0))
                expert_steps(pe, l, step)
                pe.wait_ge(y_done, MBASE[l] + MT[l])

            pe.wait_ge(wkv_loaded, 16 * 4)
            pe.wait_ge(consts_made, 1)
            keys_values(0)
            pe.wait_ge(params_loaded, 16 * 8)
            pe.wait_ge(wq_lo_done, 1)
            attention(0)
            keys_values(1)
            experts(0)
            attention(1)
            experts(1)


def _chunks(w):
    return w.reshape(-1, P, w.shape[-1]).transpose(1, 0, 2)


def kernel(**inputs):
    import concourse.bacc as bacc
    from concourse.bass_utils import run_bass_kernel_spmd

    i = {k: np.asarray(v) for k, v in inputs.items()}
    attn = lambda n: [i["L0_xattn_W" + n], i["L1_xattn_W" + n].T]
    bias = lambda n: np.stack([i[f"L{l}_xattn_b{n}"] for l in range(LAYERS)])
    both = lambda n: np.stack([_chunks(w) for w in attn(n)], axis=1)
    w = np.zeros((LAYERS * E, P, WCOLS), np.float32)
    firsts = (i["L0_ffn_W1"], i["L1_ffn_gate_up_proj"].transpose(0, 2, 1))
    seconds = (i["L0_ffn_W2"], i["L1_ffn_down_proj"].transpose(0, 2, 1))
    for l in range(LAYERS):
        for e in range(E):
            w[l * E + e, :, 0:W2AT] = _chunks(firsts[l][e]).reshape(P, -1)
            second = _chunks(seconds[l][e]).reshape(P, -1)
            w[l * E + e, :, W2AT:W2AT + second.shape[1]] = second
    biases = np.concatenate([
        np.concatenate([i["L0_ffn_b1"], i["L0_ffn_b2"]], axis=1),
        np.concatenate([i["L1_ffn_gate_up_proj_bias"], i["L1_ffn_down_proj_bias"]], axis=1)])
    per_row = lambda v: v.reshape(LAYERS, KD, P).transpose(2, 0, 1)
    data = {
        "x": i["x"].reshape(N, D),
        "ctxT": i["ctx_1024"].transpose(2, 0, 1).reshape(KD, P, B, S).transpose(1, 2, 0, 3),
        "wkv": np.stack([both("k"), both("v")], axis=2),
        "wq": both("q"), "wo": both("o"),
        "wr": np.stack([_chunks(i["L0_ffn_Wr"]), _chunks(i["L1_ffn_router_weight"].T)], axis=1),
        "bq": per_row(bias("q")), "bk": per_row(bias("k")), "bv": bias("v"), "bo": bias("o"),
        "br": np.stack([i["L0_ffn_br"], i["L1_ffn_router_bias"]]),
        "gates": np.concatenate([i["g_xattn"], i["g_ffn"]]),
        "biases": biases.reshape(P, -1), "weights": w,
    }
    data = {k: np.ascontiguousarray(v) for k, v in data.items()}
    nc = bacc.Bacc("TRN2", target_bir_lowering=False, num_devices=1)
    aps = {k: nc.dram_tensor(f"in_{k}", v.shape, F32, kind="ExternalInput").ap()
           for k, v in data.items()}
    aps["out"] = nc.dram_tensor("out", (N, D), F32, kind="ExternalOutput").ap()
    build_program(nc, aps)
    r = run_bass_kernel_spmd(nc, [{f"in_{k}": v for k, v in data.items()}], core_ids=[0])
    return r.results[0]["out"].reshape(B, SEQ, D)
```

```python
from contextlib import ExitStack

import numpy as np
import concourse.bass as bass
from concourse import mybir

F32 = mybir.dt.float32
R32 = mybir.dt.float32r
I32 = mybir.dt.int32
U32 = mybir.dt.uint32
ALU = mybir.AluOpType
ACT = mybir.ActivationFunctionType
AX = mybir.AxisListType

P = 128
LAYERS = 2
B, SEQ, D = 2, 1024, 256
N = B * SEQ
NT = N // P
KD = D // P
H, DH, S = 16, 16, 77
HC = P // DH
SC = 512
FLAT = H * S
NCH = -(-FLAT // P)
HPB = SC // S
DV = DH + 1
SPAN = 3
E = 8
TOPK = (2, 4)
WIDE = 1024
KH = (8, 4)
REGION = N + P
MT = tuple(N * k // P + E - 1 for k in TOPK)
IDLE = E - 1
SPARE = (E + IDLE) * P
ROW = D + E
W2AT = KD * WIDE
WCOLS = W2AT + 8 * D
BCOLS = WIDE + D
EPS = 1e-5
GROUPS = ((0, 4), (4, 8), (8, NCH))


def first_head(c):
    return c * P // S


def build_program(nc, a):
    with ExitStack() as ctx:
        def sb(name, shape, dt=F32):
            return ctx.enter_context(nc.sbuf_tensor(name, shape, dt))

        def sem(name):
            return ctx.enter_context(nc.semaphore(name))

        def dram(name, shape, dt=F32):
            return nc.dram_tensor(name, shape, dt, kind="Internal").ap()

        dispatched = [dram(f"dispatched{l}", (E * REGION + IDLE * P, ROW)) for l in range(LAYERS)]
        results = [dram(f"results{l}", (SPARE + TOPK[l] * N, D)) for l in range(LAYERS)]
        attended = [dram(f"attended{l}", (NT, P, D + 4)) for l in range(LAYERS)]
        flat_values = dram("flat_values", (LAYERS, B, H, S, DV))
        split_bias = dram("split_bias", (2, LAYERS * E, BCOLS))

        ident = sb("ident", [P, P])
        tri = sb("tri", [P, P])
        ones = sb("ones", [P, P])
        ones2 = sb("ones2", [2, P], R32)
        head_mask = sb("head_mask", [P, HC])
        block_mask = sb("block_mask", [P, NCH, SPAN])
        expert_ids = sb("expert_ids", [P, E])
        region_base = sb("region_base", [P, E])
        rank_rows = sb("rank_rows", [P, 4])
        token_ids = sb("token_ids", [P, NT])
        eps_col = sb("eps_col", [P, 1])
        minus_half = sb("minus_half", [P, 1])
        minus_one = sb("minus_one", [P, 1])
        tile_edges = sb("tile_edges", [1, 15])
        tri8 = sb("tri8", [1, E, E])
        alternate = sb("alternate", [1, E])
        tile_ids = sb("tile_ids", [1, max(MT)])
        zero_rows = sb("zero_rows", [P, ROW])
        idle_rows = sb("idle_rows", [P, ROW])
        gates = sb("gates", [P, 4])
        tgates = sb("tgates", [P, 4])

        wo = sb("wo", [P, LAYERS, KD, D])
        wq_hi = sb("wq_hi", [P, LAYERS, KD, D], R32)
        wq_lo = sb("wq_lo", [P, LAYERS, KD, D], R32)
        wr = sb("wr", [P, LAYERS, KD, E])
        ctxT = sb("ctxT", [P, B, KD, S])
        bq = sb("bq", [P, LAYERS, KD])
        bk = sb("bk", [P, LAYERS, KD])
        bv = sb("bv", [S, LAYERS, D])
        bo = sb("bo", [P, LAYERS, D])
        br = sb("br", [P, LAYERS, E])
        key_hi = sb("key_hi", [P, B, KD, HC * S], R32)
        key_lo = sb("key_lo", [P, B, KD, HC * S], R32)
        kT = sb("kT", [P, S])
        kT_hi = sb("kT_hi", [P, S], R32)
        kT_lo = sb("kT_lo", [P, S])
        vals = sb("vals", [S, H, DV])
        flat_v = sb("flat_v", [P, NCH, DV])
        v_blocks = sb("v_blocks", [P, B, NCH, SPAN * DV])
        xt = sb("xt", [P, 4, D])
        x2 = sb("x2", [P, 4, D + 4])
        rows = sb("rows", [P, 4, ROW])
        xn = sb("xn", [P, 2, D])
        xT_hi = sb("xT_hi", [P, D], R32)
        xT_lo = sb("xT_lo", [P, D], R32)
        q_hi = sb("q_hi", [P, KD, P], R32)
        q_lo = sb("q_lo", [P, KD, P], R32)
        probs = sb("probs", [P, 2, NCH * P])
        probsT = sb("probsT", [P, NCH * P])
        top = sb("top", [P, H])
        rden = sb("rden", [P, H])
        ob = sb("ob", [P, D])
        oT = sb("oT", [P, D])
        xg = sb("xg", [P, 4, D])
        x2T = sb("x2T", [P, D])
        st1, mv1, rs1 = sb("st1", [P, 6]), sb("mv1", [P, 2]), sb("rs1", [P, 4])
        st2, mv2, rs2 = sb("st2", [P, 6]), sb("mv2", [P, 2]), sb("rs2", [P, 4])
        logits = sb("logits", [P, E])
        best = sb("best", [P, E])
        best_at = sb("best_at", [P, E], U32)
        best_f = sb("best_f", [P, 4])
        chosen = sb("chosen", [P, 4, E, 4])
        ranked = sb("ranked", [P, E, 4])
        ranks = sb("ranks", [P, E])
        mask = sb("mask", [P, 2, E])
        seen = sb("seen", [P, 2, E])
        slots = sb("slots", [P, E])
        slot_k = sb("slot_k", [P, 4, E])
        slot_f = sb("slot_f", [P, 4])
        slot_at = sb("slot_at", [P, 4, 4], U32)

        ysb = sb("ysb", [P, 2, 4, D])
        wkv = ysb[:, :, :, :].rearrange("p a b c -> p (a b c)").rearrange(
            "p (l w k n) -> p l w k n", l=LAYERS, w=2, k=KD)
        x2in = sb("x2in", [P, 2, D + 4])
        below = sb("below", [P, 4])
        expw = sb("expw", [P, 4])
        wsum = sb("wsum", [P, 1])
        rsum = sb("rsum", [P, 1])
        share = sb("share", [P, 4])

        raw = sb("raw", [P, WCOLS])
        w_hi = sb("w_hi", [P, 2, WCOLS], R32)
        w_lo = sb("w_lo", [P, 2, WCOLS], R32)
        w_bias = sb("w_bias", [2, 2, BCOLS], R32)
        braw = sb("braw", [P, LAYERS * E * BCOLS // P])
        hid = probs[:, 0, 0:WIDE]
        gate_s = probs[:, 1, 0:512]
        up_s = probs[:, 1, 512:1024]
        sig_s = probsT[:, 0:512]
        GH = SC // 2
        hT_hi = sb("hT_hi", [P, WIDE], R32)
        hT_lo = sb("hT_lo", [P, WIDE], R32)
        b_hi, b_lo = [t[:, 0:LAYERS * E * BCOLS // P] for t in (hT_hi, hT_lo)]
        xm = sb("xm", [P, 4, ROW])
        wq = xm[:, :, :].rearrange("p a b -> p (a b)")[:, 0:LAYERS * KD * D].rearrange(
            "p (l k n) -> p l k n", l=LAYERS, k=KD)
        y = ysb[:, :].rearrange("p a b c -> p (a b) c")
        y_at = sb("y_at", [P, 8], U32)
        TAB = 8
        ROWAT, EXPERT, SLOT, SPLIT0, SPLIT1, NEXT, LOAD, PLACE = range(TAB)
        row_of = lambda n, c0, d: probs[0:1, n, c0:c0 + E * max(MT)].rearrange(
            "p (a b) -> p a b", b=d)
        tab_f = row_of(1, 0, max(MT))
        tab = sb("tab", [1, TAB, max(MT)], I32)
        t_cnt = sb("t_cnt", [1, E])
        cnt_i = sb("cnt_i", [1, E], I32)
        t_gt = sb("t_gt", [1, E, 15])
        t_tiles = sb("t_tiles", [1, E])
        t_tri = sb("t_tri", [1, E, E])
        t_end = sb("t_end", [1, E])
        t_le = row_of(0, 0, E)
        t_m = row_of(0, E * max(MT), E)
        t_e = sb("t_e", [1, max(MT)])
        t_d = sb("t_d", [1, max(MT)])
        t_new = sb("t_new", [1, max(MT)])

        ps = ctx.enter_context(nc.psum_tensor("ps", [P, 8, SC], F32))

        (params_loaded, wkv_loaded, consts_made, small_made, gates_ready, bo_scaled,
         wq_hi_done, wq_lo_done, kT_ready, kT_done, kT_hi_done, kT_lo_done, keys_done, v_ready,
         v_done, v_stored, v_flat, v_blocks_done) = [sem(n) for n in (
            "params_loaded", "wkv_loaded", "consts_made", "small_made", "gates_ready",
            "bo_scaled", "wq_hi_done", "wq_lo_done", "kT_ready", "kT_done", "kT_hi_done",
            "kT_lo_done", "keys_done", "v_ready", "v_done", "v_stored", "v_flat",
            "v_blocks_done")]
        x_loaded = [sem(f"x_loaded{r}") for r in range(4)]
        (stats1, moments1, var1, rstd1, offset1, xn_done, xnT_ready, xT_hi_done, xT_lo_done, q_ready,
         q_hi_done, q_lo_done, scores_ready, max_done, shifted_part, shifted, exp_done, pT_ready, pT_copied,
         pv_ready, rden_done, o_done, oT_ready, oT_copied, proj_ready, xg_done, x2_done, stats2,
         moments2, var2, rstd2, offset2, rows_done, x2T_ready, x2T_copied, logits_ready, logits_done,
         best_done, best_kept, best_at_done, best_f_done, chosen_done, mask_done, ranked_done, ranks_done,
         code_done, seen_done, count_ready, slots_done, slot_k_done, slot_f_done, slot_done) = [
            sem(n) for n in (
                "stats1", "moments1", "var1", "rstd1", "offset1", "xn_done", "xnT_ready", "xT_hi_done",
                "xT_lo_done", "q_ready", "q_hi_done", "q_lo_done", "scores_ready", "max_done",
                "shifted_part", "shifted", "exp_done", "pT_ready", "pT_copied", "pv_ready", "rden_done",
                "o_done", "oT_ready", "oT_copied", "proj_ready", "xg_done", "x2_done", "stats2",
                "moments2", "var2", "rstd2", "offset2", "rows_done", "x2T_ready", "x2T_copied",
                "logits_ready", "logits_done", "best_done", "best_kept", "best_at_done", "best_f_done",
                "chosen_done", "mask_done", "ranked_done", "ranks_done", "code_done",
                "seen_done", "count_ready", "slots_done", "slot_k_done", "slot_f_done",
                "slot_done")]
        x2_stored = [sem(f"x2_stored{r}") for r in range(4)]
        scattered = [sem(f"scattered{r}") for r in range(4)]
        (total_ready, seen_zero, table_step, table_ready, zeros_stored, gates_passed) = [
            sem(n) for n in ("total_ready", "seen_zero", "table_step", "table_ready",
                             "zeros_stored", "gates_passed")]
        results_loaded = [sem(f"results_loaded{r}") for r in range(2)]
        (below_done, expw_done, rsum_done, share_done, added) = [sem(n) for n in (
            "below_done", "expw_done", "rsum_done", "share_done", "added")]
        out_stored = [sem(f"out_stored{r}") for r in range(4)]
        raw_loaded, hi_done, split_done, bias_split, bias_stored, bias_loaded = [sem(n) for n in (
            "raw_loaded", "hi_done", "split_done", "bias_split", "bias_stored", "bias_loaded")]
        rows_loaded = [sem(f"rows_loaded{r}") for r in range(4)]
        y_scattered = [sem(f"y_scattered{r}") for r in range(8)]
        (y_at_done, mT_ready, mT_hi_done, mT_lo_done, hid_ready, hid_dve, hid_act, gate_done,
         sig_done, up_done, glu_done, glu_hid, hT_ready, hT_hi_done, hT_lo_done, y_ready, y_done) = [
            sem(n) for n in (
                "y_at_done", "mT_ready", "mT_hi_done", "mT_lo_done", "hid_ready", "hid_dve",
                "hid_act", "gate_done", "sig_done", "up_done", "glu_done", "glu_hid", "hT_ready",
                "hT_hi_done", "hT_lo_done", "y_ready", "y_done")]

        def need(eng, s, count):
            if isinstance(count, int) and count <= 0:
                return
            eng.wait_ge(s, count)

        def gate(eng, s, count):
            if isinstance(count, int) and count <= 0:
                return
            eng.wait_ge(s, count)
            eng.sem_inc(gates_passed, 1)

        class Tile:
            def __init__(self, j, const, unroll=4):
                self.c = const
                self.slot = const % 4
                self.slot8 = const % 8
                self.par = const % 2
                self.at, self.pair, self.quad, self.oct = [
                    const // n if j is None else j * (unroll // n) + const // n
                    for n in (1, 2, 4, 8)]

        LAGS = 7
        LOOPS = (NT - LAGS) // 4

        def attention_steps(eng, step):
            for s in range(LAGS):
                step(None, s)
            with eng.Fori(0, LOOPS) as j:
                for u in range(4):
                    step(j, LAGS + u)
            for s in range(LAGS + 4 * LOOPS, NT + LAGS):
                step(None, s)

        def stage(j, s, lag):
            if j is None and not 0 <= s - lag < NT:
                return None
            return Tile(j, s - lag)

        def expert_steps(eng, l, step):
            for s in range(3):
                step(None, s)
            loops = (MT[l] - 4) // 8
            with eng.Fori(0, loops) as j:
                for u in range(8):
                    step(j, 3 + u)
            for s in range(8 * loops + 3, MT[l] + 2):
                step(None, s)

        def row_tile(l, j, s, lag):
            if j is None and not 0 <= s - lag < MT[l]:
                return None
            return Tile(j, s - lag, 8)

        def scatter_count(l, r, quad):
            return quad * (16 * TOPK[l]) + (l * (16 * TOPK[0] * (NT // 4)) + HEAD_START)

        def idle_part(k):
            at = E * REGION + k % IDLE * P
            return dispatched[k // IDLE][at:at + P, :]

        def uses(l, r, ring=4):
            return sum(len(range(r, MT[x], ring)) for x in range(l))

        def y_count(l, t):
            return t.oct * 16 + (uses(l, t.slot8, 8) * 16 + HEAD_START)

        def adds(cl, at):
            return at * TOPK[cl] + cl * NT * TOPK[0]

        HEAD_START = 16
        MBASE = [0, MT[0]]
        HBASE = [0, KH[0] // 4 * MT[0]]

        pieces = []
        for c in range(KD):
            h = c * HC
            while h < (c + 1) * HC:
                n = min((c + 1) * HC, (h // HPB + 1) * HPB) - h
                pieces.append((c, h, n))
                h += n
        SCORE_BANK, PT_BANK = 2, 5
        full = H // HPB
        rest = H - full * HPB


        tile_of = lambda ap: ap.rearrange("a p d -> (a p) d")
        x_tiles = a["x"].rearrange("(t p) d -> t p d", p=P)
        out_tiles = a["out"].rearrange("(t p) d -> t p d", p=P)

        block = ctx.enter_context(nc.Block())

        @block.sync
        def _(sp):
            for dst, src in ((wkv, a["wkv"]), (ctxT[:, :, :, :], a["ctxT"]),
                             (bk[:, :, :], a["bk"]),
                             (bv[:, :, :], a["bv"].partition_broadcast(S))):
                sp.dma_start(dst, src).then_inc(wkv_loaded, 16)
            for t in range(4):
                sp.dma_start(xt[:, t, :], x_tiles[t]).then_inc(x_loaded[t], 16)
            for dst, src in ((wq[:, :, :, :], a["wq"]), (wo[:, :, :, :], a["wo"]),
                             (wr[:, :, :, :], a["wr"]), (bq[:, :, :], a["bq"]),
                             (bo[:, :, :], a["bo"].partition_broadcast(P)),
                             (br[:, :, :], a["br"].partition_broadcast(P)),
                             (gates[:, :], a["gates"].partition_broadcast(P)),
                             (braw[:, :], a["biases"])):
                sp.dma_start(dst, src).then_inc(params_loaded, 16)

            def values(l):
                whole = FLAT // P
                for b in range(B):
                    n = l * B + b
                    sp.wait_ge(v_done, n + 1)
                    sp.dma_start(flat_values[l, b].rearrange("h s d -> s h d"),
                                 vals[:, :, :]).then_inc(v_stored, 16)
                    sp.wait_ge(v_stored, 16 * (n + 1))
                    gate(sp, v_blocks_done, n)
                    src = flat_values[l, b].rearrange("h s d -> (h s) d")
                    sp.dma_start(flat_v[:, 0:whole, :], src[0:whole * P].rearrange(
                        "(c p) d -> p c d", p=P)).then_inc(v_flat, 16)
                    sp.dma_start(flat_v[0:FLAT - whole * P, whole, :],
                                 src[whole * P:FLAT]).then_inc(v_flat, 16)

            def load_results(t, cl):
                K = TOPK[cl]
                gate(sp, added, adds(cl, t.at - 1) if cl or t.c > 1 or t.at is not t.c else 0)
                sp.dma_start(x2in[:, t.par, :], tile_of(attended[cl][bass.ds(t.at, 1)])
                             ).then_inc(results_loaded[t.par], 16)
                src = results[cl][SPARE:].rearrange("(k t p) d -> t p k d", k=K, p=P)
                sp.dma_start(ysb[:, t.par, 0:K, :], src[bass.ds(t.at, 1)].rearrange(
                    "a p k d -> (a p) k d")).then_inc(results_loaded[t.par], 16)

            def results_there(l):
                for r in range(8):
                    sp.wait_ge(y_scattered[r], 16 * uses(l + 1, r, 8) + HEAD_START)
                for r in range(4):
                    sp.wait_ge(x2_stored[r], 16 * (l + 1) * (NT // 4) + HEAD_START)

            def experts(l):
                sp.wait_ge(table_ready, l + 1)
                for e in range(E):
                    c = sp.value_load(cnt_i[0:1, e:e + 1], min_val=0, max_val=N)
                    sp.dma_start(dispatched[l][bass.ds(c + e * REGION, P), :],
                                 zero_rows[:, :]).then_inc(zeros_stored, 16)
                for r in range(4):
                    sp.wait_ge(scattered[r], scatter_count(l, r, NT // 4))
                for r in range(8):
                    sp.wait_ge(y_scattered[r], uses(l, r, 8) * 16 + HEAD_START)
                sp.wait_ge(zeros_stored, 16 * (LAYERS * IDLE - 12 + E * (l + 1)))

                def load(t):
                    at = sp.value_load(tab[0:1, ROWAT, bass.ds(t.at, 1)], min_val=0,
                                       max_val=E * REGION + (IDLE - 1) * P)
                    before = MBASE[l] if isinstance(t.at, int) and t.at < 4 \
                        else t.at + (MBASE[l] - 3)
                    gate(sp, mT_ready, before)
                    gate(sp, y_at_done, before)
                    sp.dma_start(xm[:, t.slot, :], dispatched[l][bass.ds(at, P), :]
                                 ).then_inc(rows_loaded[t.slot], 16)

                for t in range(4):
                    load(Tile(None, t))
                loops = (MT[l] - 4) // 4
                with sp.Fori(0, loops) as j:
                    for u in range(4):
                        load(Tile(j, 4 + u))
                for t in range(4 + 4 * loops, MT[l]):
                    load(Tile(None, t))

            values(0)
            sp.wait_ge(consts_made, 1)
            for k in range(12, LAYERS * IDLE):
                sp.dma_start(idle_part(k), idle_rows[:, :]).then_inc(zeros_stored, 16)
            for part, t in enumerate((b_hi, b_lo)):
                sp.wait_ge(bias_split, part + 1)
                sp.dma_start(split_bias[part].rearrange("e n -> (e n)").rearrange(
                    "(p n) -> p n", p=P), t[:, :].bitcast(F32)).then_inc(bias_stored, 16)
            with sp.Fori(0, NT // 4 - 1) as j:
                for u in range(4):
                    t = Tile(j, 4 + u)
                    gate(sp, xg_done, t.at - 3)
                    sp.dma_start(xt[:, t.slot, :], tile_of(x_tiles[bass.ds(t.at, 1)])
                                 ).then_inc(x_loaded[t.slot], 16)
            values(1)
            experts(0)
            results_there(0)
            for t in range(4):
                load_results(Tile(None, t), 0)
            with sp.Fori(0, NT // 4 - 1) as j:
                for u in range(4):
                    load_results(Tile(j, 4 + u), 0)
            experts(1)
            results_there(1)

            def store(t):
                gate(sp, added, adds(1, t.at + 1))
                sp.dma_start(tile_of(out_tiles[bass.ds(t.at, 1)]),
                             xt[:, t.slot, :]).then_inc(out_stored[t.slot], 16)

            for t in range(2):
                load_results(Tile(None, t), 1)
            with sp.Fori(0, NT // 4 - 1) as j:
                for u in range(4):
                    store(Tile(j, u))
                    load_results(Tile(j, u + 2), 1)
            for t in range(NT - 4, NT):
                store(Tile(None, t))
                if t + 2 < NT:
                    load_results(Tile(None, t + 2), 1)
            for r in range(4):
                sp.wait_ge(out_stored[r], 16 * (NT // 4))

        @block.gpsimd
        def _(pool):
            made = [0]

            def make(ins):
                made[0] += 1
                ins.then_inc(small_made, 1)

            def all_made():
                pool.wait_ge(small_made, made[0])

            def load_raw(e):
                pool.dma_start(raw[:, :], tile_of(a["weights"][bass.ds(e, 1)])
                               ).then_inc(raw_loaded, 16)

            def split(slot, e):
                gate(pool, bias_loaded, e * 16)
                pool.dma_start(w_bias[:, slot, :].bitcast(F32), split_bias[:, bass.ds(e, 1), :]
                               .rearrange("h a n -> h (a n)")).then_inc(bias_loaded, 16)
                gate(pool, raw_loaded, (e + 1) * 16)
                pool.tensor_scalar(w_hi[:, slot, :], raw[:, :], 1.0, 1.0, ALU.mult,
                                   ALU.mult).then_inc(hi_done, 1)
                gate(pool, hi_done, e + 1)
                pool.tensor_tensor(w_lo[:, slot, :], raw[:, :], w_hi[:, slot, :].bitcast(F32),
                                   ALU.subtract).then_inc(split_done, 1)

            load_raw(0)
            make(pool.memset(vals[:, :, :], 1.0))
            make(pool.memset(head_mask[:, :], 1.0))
            make(pool.memset(block_mask[:, :, :], 1.0))
            make(pool.memset(ident[:, :], 0.0))
            make(pool.memset(tri[:, :], 1.0))
            make(pool.memset(ones[:, :], 1.0))
            make(pool.memset(tri8[:, :, :], 1.0))
            make(pool.memset(zero_rows[:, :], 0.0))
            make(pool.memset(idle_rows[:, :], 0.0))
            make(pool.memset(flat_v[:, :, :], 0.0))
            make(pool.memset(alternate[:, 0:E:2], 1.0))
            make(pool.memset(alternate[:, 1:E:2], -1.0))
            all_made()

            def keep(t, pattern, compare, base, mult, fill=0.0):
                make(pool.affine_select(out=t, in_=t, pattern=pattern, compare_op=compare,
                                        fill=fill, base=base, channel_multiplier=mult))

            keep(head_mask[:, :], [[-DH, HC]], ALU.is_ge, 0, 1)
            all_made()
            keep(head_mask[:, :], [[DH, HC]], ALU.is_ge, DH - 1, -1)
            keep(ident[:, :], [[1, P]], ALU.not_equal, 0, -1, fill=1.0)
            for c in range(NCH):
                keep(block_mask[:, c, :], [[-S, SPAN]], ALU.is_ge, c * P - S * first_head(c), 1)
            all_made()
            for c in range(NCH):
                keep(block_mask[:, c, :], [[S, SPAN]], ALU.is_ge,
                     S - 1 - c * P + S * first_head(c), -1)
            keep(tri[:, :], [[1, P]], ALU.is_gt, 0, -1)
            keep(tri8[:, :, :], [[1, E], [-1, E]], ALU.is_ge, 0, 0)
            make(pool.memset(alternate[:, E - 1:E], 0.0))

            def count_up(t, pattern, base, mult):
                make(pool.iota(t, pattern=pattern, base=base, channel_multiplier=mult,
                               allow_small_or_imprecise_dtypes=True))

            count_up(expert_ids[:, :], [[1, E]], 0, 0)
            count_up(region_base[:, :], [[REGION, E]], 0, 0)
            count_up(rank_rows[:, :], [[N, 4]], 0, 0)
            count_up(token_ids[:, :], [[P, NT]], SPARE, 1)
            count_up(tile_edges[:, :], [[P, 15]], P, 0)
            count_up(tile_ids[:, :], [[1, max(MT)]], 0, 0)
            count_up(zero_rows[:, D:ROW], [[P, E]], 0, 1)
            count_up(idle_rows[:, D:ROW], [[P, E]], E * P, 1)
            make(pool.memset(eps_col[:, :], EPS))
            make(pool.memset(minus_half[:, :], -0.5))
            make(pool.memset(minus_one[:, :], -1.0))
            make(pool.memset(probs[:, :, FLAT:], 0.0))
            make(pool.tensor_copy(ones2[:, :], ones[0:2, :]))
            all_made()
            pool.sem_inc(consts_made, 1)
            for k, s in enumerate(scattered + y_scattered):
                pool.dma_start(idle_part(k), idle_rows[:, :]).then_inc(s, HEAD_START)

            pool.wait_ge(params_loaded, 16 * 8)
            pool.tensor_scalar(b_hi[:, :], braw[:, :], 1.0, 1.0, ALU.mult,
                               ALU.mult).then_inc(bias_split, 1)
            pool.wait_ge(bias_split, 1)
            pool.tensor_tensor(b_lo[:, :], braw[:, :], b_hi[:, :].bitcast(F32),
                               ALU.subtract).then_inc(bias_split, 1)
            pool.wait_ge(bo_scaled, LAYERS)

            def attention(l):
                def scale_and_offset(T, mom, mv, rs, var, rstd, offset, used):
                    need(pool, used, T)
                    need(pool, mom, T + 1)
                    pool.tensor_tensor(rs[:, 0:1], mv[:, 1:2], eps_col[:, :],
                                       ALU.add).then_inc(var, 1)
                    pool.tensor_tensor(rs[:, 2:3], mv[:, 0:1], minus_one[:, :], ALU.mult)
                    need(pool, var, T + 1)
                    pool.tensor_tensor(rs[:, 1:2], rs[:, 0:1], minus_half[:, :],
                                       ALU.pow).then_inc(rstd, 1)
                    need(pool, rstd, T + 1)
                    pool.tensor_tensor(rs[:, 3:4], rs[:, 2:3], rs[:, 1:2],
                                       ALU.mult).then_inc(offset, 1)

                def step(j, s):
                    A, Q, _, _, G, _, _, Z = [stage(j, s, lag) for lag in range(LAGS + 1)]
                    if Q:
                        T = Q.at + NT * l
                        if l == 0:
                            need(pool, x_loaded[Q.slot], (Q.quad + 1) * 16)
                        else:
                            need(pool, added, adds(0, Q.at + 1))
                        need(pool, x2_done, T - 3)
                        need(pool, xn_done, T + 1)
                        pool.tensor_tensor(xg[:, Q.slot, :], xt[:, Q.slot, :], bo[:, l, :],
                                           ALU.add).then_inc(xg_done, 1)
                    if G:
                        scale_and_offset(G.at + NT * l, moments2, mv2, rs2, var2, rstd2, offset2,
                                         rows_done)
                    if Z:
                        T = Z.at + NT * l
                        gate(pool, slot_done, T + 1)
                        gate(pool, code_done, T + 1)
                        gate(pool, rows_done, T + 1)
                        for k in range(TOPK[l]):
                            pool.indirect_dma_start(
                                out=dispatched[l], out_offset=bass.IndirectOffsetOnAxis(
                                    ap=slot_at[:, Z.slot, k:k + 1], axis=0),
                                in_=rows[:, Z.slot, :], in_offset=None
                            ).then_inc(scattered[Z.slot], 16)
                    if A:
                        scale_and_offset(A.at + NT * l, moments1, mv1, rs1, var1, rstd1, offset1,
                                         xn_done)
                attention_steps(pool, step)

            def experts(l):
                def step(j, s):
                    if t := row_tile(l, j, s, 2):
                        G = t.at + MBASE[l]
                        gate(pool, y_at_done, G + 1)
                        gate(pool, y_done, G + 1)
                        pool.indirect_dma_start(
                            out=results[l], out_offset=bass.IndirectOffsetOnAxis(
                                ap=y_at[:, t.slot8:t.slot8 + 1], axis=0),
                            in_=y[:, t.slot8, :], in_offset=None
                        ).then_inc(y_scattered[t.slot8], 16)
                    t = row_tile(l, j, s, 1)
                    if t and not (j is None and t.c == 0):
                        read = lambda n, lo, hi: pool.value_load(
                            tab[0:1, n, bass.ds(t.at, 1)], min_val=lo, max_val=hi)
                        flags = [read(SPLIT0, 0, 1), read(SPLIT1, 0, 1)]
                        nxt = read(NEXT, 1, LAYERS * E - 1)
                        after = read(LOAD, 2, LAYERS * E - 1)
                        for slot in range(2):
                            with pool.If(flags[slot]):
                                split(slot, nxt)
                                gate(pool, split_done, nxt + 1)
                                load_raw(after)
                                pool.nop()
                expert_steps(pool, l, step)

            attention(0)
            pool.wait_ge(bias_stored, 32)
            split(0, 0)
            pool.wait_ge(split_done, 1)
            load_raw(1)
            split(1, 1)
            pool.wait_ge(split_done, 2)
            load_raw(2)
            pool.wait_ge(table_ready, 1)
            experts(0)
            split(1, E + 1)
            pool.wait_ge(split_done, E + 2)
            load_raw(E + 2)
            attention(1)
            pool.wait_ge(table_ready, 2)
            experts(1)
            pool.wait_ge(raw_loaded, 16 * (LAYERS * E + 1))

        @block.scalar
        def _(act):
            for r in range(4):
                act.sem_inc(x2_stored[r], HEAD_START)
            act.wait_ge(params_loaded, 16 * 8)
            act.activation(tgates[:, :], gates[:, :], ACT.Tanh).then_inc(gates_ready, 1)
            act.activation(wq_hi[:, :, :, :], wq[:, :, :, :], ACT.Copy).then_inc(wq_hi_done, 1)
            act.wait_ge(gates_ready, 1)
            for l in range(LAYERS):
                act.activation(bo[:, l, :], bo[:, l, :], ACT.Copy, scale=tgates[:, l:l + 1]
                               ).then_inc(bo_scaled, 1)

            def combine_weights(at, cl):
                C = at + NT * cl
                need(act, share_done, C)
                need(act, rsum_done, C)
                need(act, below_done, C + 1)
                act.activation(expw[:, 0:TOPK[cl]], below[:, 0:TOPK[cl]], ACT.Exp,
                               accum_out=wsum[:, :]).then_inc(expw_done, 1)

            def attention(l):
                def copy_probs(n, TF):
                    c0, c1 = GROUPS[n]
                    need(act, pT_ready, TF * 3 + (n + 1))
                    act.activation(probsT[:, c0 * P:c1 * P],
                                   ps[:, PT_BANK + n % 2, 0:(c1 - c0) * P],
                                   ACT.Copy).then_inc(pT_copied, 1)

                def step(j, s):
                    A, Q, S2, F, G, R, _, Z = [stage(j, s, lag) for lag in range(LAGS + 1)]
                    if Q:
                        T = Q.at + NT * l
                        need(act, xnT_ready, T - 1)
                        need(act, offset1, T + 1)
                        act.activation(xn[:, Q.par, :], xt[:, Q.slot, :], ACT.Identity,
                                       bias=rs1[:, 3:4], scale=rs1[:, 1:2]).then_inc(xn_done, 1)
                    if A and l:
                        combine_weights(A.at, 0)
                    if Q:
                        need(act, q_ready, T)
                        need(act, xnT_ready, T + 1)
                        act.activation(xT_hi[:, :], ps[:, 0, 0:D], ACT.Copy
                                       ).then_inc(xT_hi_done, 1)
                    if F:
                        TF = F.at + NT * l
                        need(act, pv_ready, TF)
                        for n in range(2):
                            copy_probs(n, TF)
                    if G:
                        TG = G.at + NT * l
                        need(act, scattered[G.slot], scatter_count(l, G.slot, G.quad))
                        need(act, offset2, TG + 1)
                        act.activation(rows[:, G.slot, 0:D], x2[:, G.slot, 0:D], ACT.Identity,
                                       bias=rs2[:, 3:4], scale=rs2[:, 1:2]).then_inc(rows_done, 1)
                    if Q:
                        need(act, scores_ready, T)
                        need(act, q_ready, T + 1)
                        for c in range(KD):
                            act.activation(q_hi[:, c, :], ps[:, 1, c * P:(c + 1) * P],
                                           ACT.Identity, bias=bq[:, l, c:c + 1]
                                           ).then_inc(q_hi_done, 1)
                    if F:
                        copy_probs(2, TF)
                    if R:
                        TR = R.at + NT * l
                        need(act, logits_ready, TR)
                        need(act, x2T_ready, TR + 1)
                        act.activation(x2T[:, :], ps[:, 0, 0:D], ACT.Copy
                                       ).then_inc(x2T_copied, 1)
                    if F:
                        need(act, proj_ready, TF)
                        need(act, oT_ready, TF + 1)
                        act.activation(oT[:, :], ps[:, 1, 0:D], ACT.Copy).then_inc(oT_copied, 1)
                    if S2:
                        T = S2.at + NT * l
                        need(act, shifted, T + 1)
                        act.activation(probs[:, S2.par, 0:FLAT], probs[:, S2.par, 0:FLAT],
                                       ACT.Exp, scale=(DH ** -0.5 if l == 0 else 1.0)
                                       ).then_inc(exp_done, 1)
                    if Z:
                        T = Z.at + NT * l
                        need(act, x2_done, T + 1)
                        need(act, best_kept, T + 1)
                        act.dma_start(tile_of(attended[l][bass.ds(Z.at, 1)]), x2[:, Z.slot, :]
                                      ).then_inc(x2_stored[Z.slot], 16)
                attention_steps(act, step)

            def experts(l):
                halves = KH[l] // 4

                def row_part(t):
                    need(act, hid_ready, (t.at + MBASE[l]) * 2)
                    need(act, mT_ready, t.at + MBASE[l] + 1)
                    act.activation(xT_hi[:, :], ps[:, 0, 0:D], ACT.Copy).then_inc(mT_hi_done, 1)

                def step(j, s):
                    t, n, h_t, y_t = [row_tile(l, j, s, lag) for lag in (0, -1, 1, 2)]
                    if y_t:
                        need(act, y_scattered[y_t.slot8], y_count(l, y_t))
                        need(act, y_ready, y_t.at + (MBASE[l] + 1))
                        act.activation(y[:, y_t.slot8, :], ps[:, 5, 0:D], ACT.Copy
                                       ).then_inc(y_done, 1)
                    if h_t:
                        for h in range(halves):
                            need(act, hT_ready, h_t.at * halves + (HBASE[l] + h + 1))
                            act.activation(hT_hi[:, h * SC:(h + 1) * SC], ps[:, 3 + h, :],
                                           ACT.Copy).then_inc(hT_hi_done, 1)
                    if t and l == 0:
                        need(act, hT_ready, t.at * 2)
                        need(act, hid_ready, t.at * 2 + 2)
                        act.activation(hid[:, SC:WIDE], ps[:, 2, :], ACT.Relu
                                       ).then_inc(hid_act, 1)
                    if t and l == 1:
                        need(act, glu_hid, t.at * 2)
                        for h in range(2):
                            half = slice(h * GH, (h + 1) * GH)
                            need(act, gate_done, t.at * 2 + (h + 1))
                            act.activation(sig_s[:, half], gate_s[:, half], ACT.Sigmoid,
                                           scale=1.702).then_inc(sig_done, 1)
                    if n:
                        row_part(n)
                row_part(Tile(None, 0))
                expert_steps(act, l, step)

            attention(0)
            experts(0)
            attention(1)
            experts(1)
            with act.Fori(0, NT) as t:
                combine_weights(t, 1)

        @block.vector
        def _(dve):
            dve.wait_ge(wq_hi_done, 1)
            dve.tensor_tensor(wq_lo[:, :, :, :], wq[:, :, :, :],
                              wq_hi[:, :, :, :].bitcast(F32), ALU.subtract
                              ).then_inc(wq_lo_done, 1)
            dve.wait_ge(consts_made, 1)

            def over(ap, axis, n):
                view = ap.unsqueeze(axis)
                return view.broadcast_to([n if i == axis else size
                                          for i, size in enumerate(view.shape)])

            def keys_values(l):
                dve.wait_ge(wkv_loaded, 16 * 4)
                for b in range(B):
                    for c in range(KD):
                        n = (l * B + b) * KD + c
                        dve.wait_ge(kT_ready, n + 1)
                        dve.tensor_scalar(kT[:, :], ps[:, n % 2, 0:S], bk[:, l, c:c + 1], None,
                                          ALU.add).then_inc(kT_done, 1)
                        dve.wait_ge(kT_done, n + 1)
                        dve.tensor_copy(kT_hi[:, :], kT[:, :]).then_inc(kT_hi_done, 1)
                        dve.wait_ge(kT_hi_done, n + 1)
                        dve.tensor_tensor(kT_lo[:, :], kT[:, :], kT_hi[:, :].bitcast(F32),
                                          ALU.subtract).then_inc(kT_lo_done, 1)
                        dve.wait_ge(kT_lo_done, n + 1)
                        for part, to in ((kT_hi[:, :].bitcast(F32), key_hi), (kT_lo[:, :], key_lo)):
                            dve.tensor_tensor(
                                to[:, b, c, :].rearrange("p (h s) -> p h s", h=HC),
                                over(part, 1, HC),
                                over(head_mask[:, :], 2, S),
                                ALU.mult).then_inc(keys_done, 1)
                    n = l * B + b
                    dve.wait_ge(v_ready, n + 1)
                    need(dve, v_stored, 16 * n)
                    dve.tensor_tensor(
                        vals[:, :, 0:DH], ps[0:S, 2, 0:D].rearrange("p (h d) -> p h d", h=H),
                        bv[:, l, :].rearrange("p (h d) -> p h d", h=H), ALU.add
                    ).then_inc(v_done, 1)
                for b in range(B):
                    n = l * B + b
                    dve.wait_ge(v_flat, 32 * (n + 1))
                    for r in range(SPAN):
                        ins = dve.tensor_tensor(
                            v_blocks[:, b, :, r * DV:(r + 1) * DV], flat_v[:, :, :],
                            over(block_mask[:, :, r], 2, DV), ALU.mult)
                    ins.then_inc(v_blocks_done, 1)

            def combine_start(t, cl):
                K = TOPK[cl]
                dve.wait_ge(results_loaded[t.par], (t.pair + (NT // 2 * cl + 1)) * 32)
                dve.tensor_scalar(below[:, 0:K], x2in[:, t.par, D:D + K],
                                  x2in[:, t.par, D:D + 1], None, ALU.subtract
                                  ).then_inc(below_done, 1)

            def combine_shares(t, cl):
                K, C = TOPK[cl], t.at + NT * cl
                need(dve, expw_done, C + 1)
                dve.reciprocal(rsum[:, :], wsum[:, :]).then_inc(rsum_done, 1)
                need(dve, rsum_done, C + 1)
                dve.tensor_scalar(share[:, 0:K], expw[:, 0:K], rsum[:, :],
                                  tgates[:, 2 + cl:3 + cl], ALU.mult, ALU.mult
                                  ).then_inc(share_done, 1)

            def combine_results(t, cl):
                K, C = TOPK[cl], t.at + NT * cl
                need(dve, share_done, C + 1)
                for k in range(K):
                    if k:
                        dve.wait_ge(added, adds(cl, t.at) + k)
                    prev = xt[:, t.slot, :] if k else x2in[:, t.par, 0:D]
                    dve.scalar_tensor_tensor(
                        out=xt[:, t.slot, :], in0=ysb[:, t.par, k, :], scalar=share[:, k:k + 1],
                        in1=prev, op0=ALU.mult, op1=ALU.add).then_inc(added, 1)

            def combine(t, cl):
                combine_start(t, cl)
                combine_shares(t, cl)
                combine_results(t, cl)

            def attention(l):
                K = TOPK[l]

                def first_moments(A):
                    T = A.at + NT * l
                    if l == 0:
                        need(dve, x_loaded[A.slot], (A.quad + 1) * 16)
                    else:
                        combine_results(A, 0)
                        need(dve, added, adds(0, A.at + 1))
                    dve.bn_stats(st1[:, :], xt[:, A.slot, :]).then_inc(stats1, 1)
                    gate(dve, stats1, T + 1)
                    gate(dve, offset1, T)
                    dve.bn_aggr(mv1[:, :], st1[:, :]).then_inc(moments1, 1)

                a_cols, n_a = HPB * S, full * HPB
                banks = ps[:, SCORE_BANK:SCORE_BANK + full, 0:a_cols].rearrange(
                    "p b (h s) -> p b h s", h=HPB)
                last = ps[:, SCORE_BANK + full, 0:rest * S].rearrange(
                    "p (h s) -> p h s", h=rest)
                top_a = top[:, 0:n_a].rearrange("p (b h) -> p b h", b=full)

                def maxima(Q):
                    need(dve, scores_ready, Q.at + (NT * l + 1))
                    dve.tensor_reduce(top_a, banks, AX.X, ALU.max).then_inc(max_done, 1)
                    dve.tensor_reduce(top[:, n_a:H], last, AX.X, ALU.max).then_inc(max_done, 1)

                def softmax_shift(Q):
                    T = Q.at + NT * l
                    need(dve, pT_ready, T * 3 - 3)
                    need(dve, max_done, T * 2 + 2)
                    dve.tensor_tensor(
                        probs[:, Q.par, 0:n_a * S].rearrange("p (b h s) -> p b h s", b=full,
                                                             h=HPB),
                        banks, over(top_a, 3, S), ALU.subtract
                    ).then_inc(shifted_part, 1)
                    dve.tensor_tensor(
                        probs[:, Q.par, n_a * S:FLAT].rearrange("p (h s) -> p h s", h=rest),
                        last, over(top[:, n_a:H], 2, S), ALU.subtract
                    ).then_inc(shifted, 1)

                def choose(R, Z):
                    if R:
                        T = R.at + NT * l
                        need(dve, oT_copied,
                             min(T + 3, NT * (l + 1)) if isinstance(T, int) else T + 3)
                        need(dve, logits_ready, T + 1)
                        dve.tensor_tensor(logits[:, :], ps[:, 1, D:D + E], br[:, l, :],
                                          ALU.add).then_inc(logits_done, 1)
                    if Z:
                        TZ = Z.at + NT * l
                        need(dve, count_ready, TZ + 1)
                        dve.tensor_tensor(slots[:, :], ps[:, 1, D + E:D + 2 * E],
                                          region_base[:, :], ALU.add).then_inc(slots_done, 1)
                    if R:
                        gate(dve, logits_done, T + 1)
                        dve.max(best[:, :], logits[:, :]).then_inc(best_done, 1)
                        gate(dve, best_done, T + 1)
                        dve.max_index(best_at[:, :], best[:, :], logits[:, :]
                                      ).then_inc(best_at_done, 1)
                        need(dve, x2_done, T + 1)
                        dve.tensor_copy(x2[:, R.slot, D:D + 4], best[:, 0:4]
                                        ).then_inc(best_kept, 1)
                        need(dve, best_at_done, T + 1)
                        dve.tensor_copy(best_f[:, 0:K], best_at[:, 0:K]).then_inc(best_f_done, 1)
                    if Z:
                        need(dve, slots_done, TZ + 1)
                        dve.tensor_tensor(
                            slot_k[:, 0:K, :],
                            chosen[:, Z.slot, :, 0:K].rearrange("p e k -> p k e"),
                            over(slots[:, :], 1, K), ALU.mult
                        ).then_inc(slot_k_done, 1)
                    if R:
                        need(dve, best_f_done, T + 1)
                        dve.tensor_tensor(
                            chosen[:, R.slot, :, 0:K],
                            over(expert_ids[:, :], 2, K),
                            over(best_f[:, 0:K], 1, E),
                            ALU.is_equal).then_inc(chosen_done, 1)
                    if Z:
                        need(dve, slot_k_done, TZ + 1)
                        dve.tensor_reduce(slot_f[:, 0:K], slot_k[:, 0:K, :], AX.X,
                                          ALU.add).then_inc(slot_f_done, 1)
                    if R:
                        need(dve, chosen_done, T + 1)
                        dve.tensor_reduce(mask[:, R.par, :], chosen[:, R.slot, :, 0:K], AX.X,
                                          ALU.add).then_inc(mask_done, 1)
                        dve.tensor_tensor(
                            ranked[:, :, 0:K], chosen[:, R.slot, :, 0:K],
                            over(rank_rows[:, 0:K], 1, E),
                            ALU.mult).then_inc(ranked_done, 1)
                    if Z:
                        need(dve, scattered[Z.slot], scatter_count(l, Z.slot, Z.quad))
                        need(dve, slot_f_done, TZ + 1)
                        dve.tensor_copy(slot_at[:, Z.slot, 0:K], slot_f[:, 0:K]
                                        ).then_inc(slot_done, 1)
                    if R:
                        need(dve, mask_done, T + 1)
                        need(dve, seen_done, T)
                        dve.tensor_tensor(seen[:, 1 - R.par, :], seen[:, R.par, :],
                                          mask[:, R.par, :], ALU.add).then_inc(seen_done, 1)
                        need(dve, ranked_done, T + 1)
                        dve.tensor_reduce(ranks[:, :], ranked[:, :, 0:K], AX.X,
                                          ALU.add).then_inc(ranks_done, 1)
                        need(dve, ranks_done, T + 1)
                        dve.tensor_scalar(rows[:, R.slot, D:ROW], ranks[:, :],
                                          token_ids[:, bass.ds(R.at, 1)], None, ALU.add
                                          ).then_inc(code_done, 1)

                def step(j, s):
                    A, Q, S2, F, G, _, C, Z = [stage(j, s, lag) for lag in range(LAGS + 1)]
                    if A and l:
                        combine_start(A, 0)
                    choose(C, Z)
                    if G:
                        TG = G.at + NT * l
                        need(dve, x2_stored[G.slot],
                             G.quad * 16 + (l * (NT // 4) * 16 + HEAD_START))
                        need(dve, xg_done, TG + 1)
                        need(dve, proj_ready, TG + 1)
                        dve.scalar_tensor_tensor(
                            out=x2[:, G.slot, 0:D], in0=ps[:, 7, 0:D], scalar=tgates[:, l:l + 1],
                            in1=xg[:, G.slot, :], op0=ALU.mult, op1=ALU.add
                        ).then_inc(x2_done, 1)
                    if Q:
                        T = Q.at + NT * l
                        need(dve, xT_hi_done, T + 1)
                        dve.tensor_tensor(xT_lo[:, :], ps[:, 0, 0:D], xT_hi[:, :].bitcast(F32),
                                          ALU.subtract).then_inc(xT_lo_done, 1)
                    if G:
                        need(dve, x2_done, TG + 1)
                        dve.bn_stats(st2[:, :], x2[:, G.slot, 0:D]).then_inc(stats2, 1)
                        gate(dve, stats2, TG + 1)
                        gate(dve, offset2, TG)
                        dve.bn_aggr(mv2[:, :], st2[:, :]).then_inc(moments2, 1)
                    if A and l:
                        combine_shares(A, 0)
                    if S2:
                        maxima(S2)
                    if Q:
                        need(dve, q_hi_done, T * 2 + 2)
                        for c in range(KD):
                            dve.scalar_tensor_tensor(
                                out=q_lo[:, c, :], in0=ps[:, 1, c * P:(c + 1) * P],
                                scalar=bq[:, l, c:c + 1], in1=q_hi[:, c, :].bitcast(F32),
                                op0=ALU.add, op1=ALU.subtract).then_inc(q_lo_done, 1)
                    if F:
                        TF = F.at + NT * l
                        out = ps[:, 7, 0:H * DV].rearrange("p (h d) -> p h d", h=H)
                        need(dve, pv_ready, TF + 1)
                        dve.reciprocal(rden[:, :].rearrange("p (h o) -> p h o", o=1),
                                       out[:, :, DH:DV]).then_inc(rden_done, 1)
                        need(dve, oT_ready, TF)
                        need(dve, rden_done, TF + 1)
                        dve.tensor_tensor(ob[:, :].rearrange("p (h d) -> p h d", h=H),
                                          out[:, :, 0:DH],
                                          over(rden[:, :], 2, DH),
                                          ALU.mult).then_inc(o_done, 1)
                    if S2:
                        softmax_shift(S2)
                    if A:
                        first_moments(A)

                dve.memset(seen[:, 0, :], 0.0).then_inc(seen_zero, 1)
                dve.wait_ge(seen_zero, l + 1)
                attention_steps(dve, step)

            steps = [0]

            def table(l):
                M = MT[l]
                ids, end, tiles = tile_ids[:, 0:M], t_end[:, :], t_tiles[:, :]
                le, m, e_, d = t_le[:, 0:M, :], t_m[:, 0:M, :], t_e[:, 0:M], t_d[:, 0:M]

                def then(ins):
                    steps[0] += 1
                    ins.then_inc(table_step, 1)
                    dve.wait_ge(table_step, steps[0])

                def row(n):
                    return tab_f[:, n, 0:M]

                dve.wait_ge(total_ready, l + 1)
                then(dve.tensor_copy(t_cnt[:, :], ps[0:1, 0, 0:E]))
                then(dve.tensor_copy(cnt_i[:, :], t_cnt[:, :]))
                then(dve.tensor_tensor(t_gt[:, :, :], over(t_cnt[:, :], 2, 15),
                                       over(tile_edges[:, :], 1, E),
                                       ALU.is_gt))
                then(dve.tensor_reduce(tiles, t_gt[:, :, :], AX.X, ALU.add))
                then(dve.tensor_scalar(tiles, tiles, 1.0, None, ALU.add))
                then(dve.tensor_tensor(t_tri[:, :, :], over(tiles, 1, E),
                                       tri8[:, :, :], ALU.mult))
                then(dve.tensor_reduce(end, t_tri[:, :, :], AX.X, ALU.add))
                then(dve.tensor_tensor(le, over(end, 1, M),
                                       over(ids, 2, E), ALU.is_le))
                then(dve.tensor_reduce(e_, le, AX.X, ALU.add))
                then(dve.tensor_tensor(m, le, over(tiles, 1, M), ALU.mult))
                then(dve.tensor_reduce(d, m, AX.X, ALU.add))
                then(dve.tensor_tensor(d, ids, d, ALU.subtract))
                then(dve.tensor_scalar(row(ROWAT), e_, float(REGION), None, ALU.mult))
                then(dve.scalar_tensor_tensor(out=row(ROWAT), in0=d, scalar=float(P),
                                              in1=row(ROWAT), op0=ALU.mult, op1=ALU.add))
                then(dve.tensor_tensor(m, le, over(alternate[:, :], 1, M),
                                       ALU.mult))
                then(dve.tensor_reduce(row(SLOT), m, AX.X, ALU.add))
                then(dve.tensor_scalar(row(EXPERT), e_, float(E - 1), None, ALU.min))
                then(dve.tensor_scalar(t_new[:, 0:M], e_, float(E), None, ALU.is_ge))
                then(dve.scalar_tensor_tensor(out=d, in0=d, scalar=1.0 - E, in1=t_new[:, 0:M],
                                              op0=ALU.add, op1=ALU.mult))
                then(dve.tensor_tensor(row(PLACE), row(EXPERT), d, ALU.add))
                then(dve.memset(t_new[:, 0:1], 0.0))
                then(dve.tensor_tensor(t_new[:, 1:M], row(EXPERT)[:, 1:M],
                                       row(EXPERT)[:, 0:M - 1], ALU.not_equal))
                if l == LAYERS - 1:
                    then(dve.scalar_tensor_tensor(
                        out=t_new[:, 0:M], in0=row(EXPERT), scalar=float(E - 1),
                        in1=t_new[:, 0:M], op0=ALU.is_lt, op1=ALU.mult))
                then(dve.tensor_tensor(row(SPLIT0), t_new[:, 0:M], row(SLOT), ALU.mult))
                then(dve.tensor_tensor(row(SPLIT1), t_new[:, 0:M], row(SPLIT0), ALU.subtract))
                last = float(LAYERS * E - 1)
                then(dve.tensor_scalar(row(NEXT), row(EXPERT), float(l * E + 1), last, ALU.add,
                                       ALU.min))
                then(dve.tensor_scalar(row(LOAD), row(EXPERT), float(l * E + 2), last, ALU.add,
                                       ALU.min))
                dve.tensor_copy(tab[:, :, 0:M], tab_f[:, :, 0:M]).then_inc(table_ready, 1)

            def experts(l):
                halves = KH[l] // 4

                def place_of(t):
                    return dve.value_load(tab[0:1, PLACE, bass.ds(t.at, 1)], min_val=0,
                                          max_val=E - 1)

                def row_part(t, place):
                    G = t.at + MBASE[l]
                    need(dve, mT_hi_done, G + 1)
                    dve.tensor_tensor(xT_lo[:, :], ps[:, 0, 0:D], xT_hi[:, :].bitcast(F32),
                                      ALU.subtract).then_inc(mT_lo_done, 1)
                    gate(dve, y_scattered[t.slot8], y_count(l, t))
                    gate(dve, rows_loaded[t.slot], (t.quad + (uses(l, t.slot) + 1)) * 16)
                    dve.tensor_copy(y_at[:, t.slot8:t.slot8 + 1],
                                    xm[:, t.slot, bass.ds(place + D, 1)]).then_inc(y_at_done, 1)

                def step(j, s):
                    t, n, h_t = [row_tile(l, j, s, lag) for lag in (0, -1, 1)]
                    place = place_of(n) if n else None
                    if h_t:
                        for h in range(halves):
                            need(dve, hT_hi_done, h_t.at * halves + (HBASE[l] + h + 1))
                            dve.tensor_tensor(
                                hT_lo[:, h * SC:(h + 1) * SC], ps[:, 3 + h, :],
                                hT_hi[:, h * SC:(h + 1) * SC].bitcast(F32), ALU.subtract
                            ).then_inc(hT_lo_done, 1)
                    if t and l == 0:
                        need(dve, hT_ready, t.at * 2)
                        need(dve, hid_ready, t.at * 2 + 1)
                        dve.tensor_scalar(hid[:, 0:SC], ps[:, 1, :], 0.0, None, ALU.max
                                          ).then_inc(hid_dve, 1)
                    if t and l == 1:
                        for h in range(2):
                            T = t.at * 2 + h
                            half = slice(h * GH, (h + 1) * GH)
                            need(dve, hid_ready, T + (MBASE[1] * 2 + 1))
                            dve.tensor_scalar(gate_s[:, half], ps[:, 1 + h, 0:GH], 7.0, None,
                                              ALU.min).then_inc(gate_done, 1)
                            dve.tensor_scalar(up_s[:, half], ps[:, 1 + h, GH:2 * GH], 7.0, -7.0,
                                              ALU.min, ALU.max).then_inc(up_done, 1)
                            need(dve, sig_done, T + 1)
                            dve.tensor_tensor(gate_s[:, half], gate_s[:, half],
                                              sig_s[:, half], ALU.mult).then_inc(glu_done, 1)
                            if h == 0:
                                need(dve, hT_ready, t.at + HBASE[1])
                            need(dve, glu_done, T + 1)
                            dve.scalar_tensor_tensor(
                                out=hid[:, half], in0=up_s[:, half], scalar=1.0,
                                in1=gate_s[:, half], op0=ALU.add, op1=ALU.mult
                            ).then_inc(glu_hid, 1)
                    if n:
                        row_part(n, place)
                dve.wait_ge(table_ready, l + 1)
                row_part(Tile(None, 0), place_of(Tile(None, 0)))
                expert_steps(dve, l, step)

            keys_values(0)
            attention(0)
            table(0)
            keys_values(1)
            experts(0)
            attention(1)
            table(1)
            experts(1)
            for t in range(4):
                combine(Tile(None, t), 1)
            with dve.Fori(0, NT // 4 - 1) as j:
                for u in range(4):
                    t = Tile(j, 4 + u)
                    dve.wait_ge(out_stored[t.slot], t.quad * 16)
                    combine(t, 1)

        @block.tensor
        def _(pe):
            def keys_values(l):
                need(pe, slots_done, NT * l)
                need(pe, logits_done, NT * l)
                need(pe, table_ready, l)
                need(pe, oT_copied, NT * l)
                need(pe, shifted, NT * l)
                for b in range(B):
                    for c in range(KD):
                        n = (l * B + b) * KD + c
                        need(pe, kT_done, n - 1)
                        for k in range(KD):
                            mm = pe.matmul(ps[:, n % 2, 0:S], wkv[:, l, 0, k, c * P:(c + 1) * P],
                                           ctxT[:, b, k, :], start=k == 0, stop=k == KD - 1)
                        mm.then_inc(kT_ready, 1)
                    need(pe, v_done, l * B + b)
                    for k in range(KD):
                        mm = pe.matmul(ps[0:S, 2, 0:D], ctxT[:, b, k, :], wkv[:, l, 1, k, :],
                                       start=k == 0, stop=k == KD - 1)
                    mm.then_inc(v_ready, 1)
                pe.wait_ge(keys_done, 2 * B * KD * (l + 1))
                pe.wait_ge(v_blocks_done, B * (l + 1))
                pe.wait_ge(v_done, B * (l + 1))

            def transposed(bank, src, ready):
                for c in range(KD):
                    mm = pe.transpose(ps[:, bank, c * P:(c + 1) * P],
                                      src[:, c * P:(c + 1) * P], ident[:, :])
                mm.then_inc(ready, 1)

            def split_product(out, terms, start=True, stop=True):
                for n, (l_hi, l_lo, r_hi, r_lo) in enumerate(terms):
                    for m, (lhs, rhs) in enumerate(((l_hi, r_hi), (l_hi, r_lo), (l_lo, r_hi))):
                        mm = pe.matmul(out, lhs, rhs, start=start and n == 0 and m == 0,
                                       stop=stop and n == len(terms) - 1 and m == 2)
                return mm

            def attention(l):
                def scores(Q):
                    T = Q.at + NT * l
                    batch = Q.at // (NT // B)
                    need(pe, shifted, T)
                    need(pe, q_lo_done, T * 2 + 2)
                    for c, h, n in pieces:
                        at = (h - c * HC) * S
                        keys = [key[:, bass.ds(batch, 1), c, at:at + n * S].rearrange(
                            "p a n -> p (a n)") for key in (key_hi, key_lo)]
                        mm = split_product(
                            ps[:, SCORE_BANK + h // HPB, h % HPB * S:(h % HPB + n) * S],
                            [(q_hi[:, c, :], q_lo[:, c, :], *keys)])
                    mm.then_inc(scores_ready, 1)

                def transpose_probs(F, n):
                    c0, c1 = GROUPS[n]
                    need(pe, pT_copied, (F.at + NT * l) * 3 + (1 if n == 2 else 0))
                    for c in range(c0, c1):
                        mm = pe.transpose(ps[:, PT_BANK + n % 2, (c - c0) * P:(c - c0 + 1) * P],
                                          probs[:, F.par, c * P:(c + 1) * P], ident[:, :])
                    mm.then_inc(pT_ready, 1)

                def step(j, s):
                    _, Q, S2, F, G, R, C, _ = [stage(j, s, lag) for lag in range(LAGS + 1)]
                    if S2:
                        scores(S2)
                    if G:
                        TG = G.at + NT * l
                        need(pe, oT_copied, TG + 1)
                        for k in range(KD):
                            mm = pe.matmul(ps[:, 7, 0:D], oT[:, k * P:(k + 1) * P],
                                           wo[:, l, k, :], start=k == 0, stop=k == KD - 1)
                        mm.then_inc(proj_ready, 1)
                    if Q:
                        T = Q.at + NT * l
                        need(pe, xn_done, T + 1)
                        transposed(0, xn[:, Q.par, :], xnT_ready)
                    if F:
                        TF = F.at + NT * l
                        need(pe, exp_done, TF + 1)
                        transpose_probs(F, 0)
                        transpose_probs(F, 1)
                    if Q:
                        need(pe, best_done, T - 4)
                        need(pe, xT_lo_done, T + 1)
                        for c in range(KD):
                            mm = split_product(ps[:, 1, c * P:(c + 1) * P], [
                                (wq_hi[:, l, k, c * P:(c + 1) * P],
                                 wq_lo[:, l, k, c * P:(c + 1) * P],
                                 xT_hi[:, k * P:(k + 1) * P], xT_lo[:, k * P:(k + 1) * P])
                                for k in range(KD)])
                        mm.then_inc(q_ready, 1)
                    if F:
                        transpose_probs(F, 2)
                        need(pe, x2_done, TF)
                        batch = F.at // (NT // B)
                        for n, (c0, c1) in enumerate(GROUPS):
                            need(pe, pT_copied, TF * 3 + (n + 1))
                            for c in range(c0, c1):
                                at = first_head(c) * DV
                                mm = pe.matmul(
                                    ps[:, 7, at:at + SPAN * DV], probsT[:, c * P:(c + 1) * P],
                                    v_blocks[:, bass.ds(batch, 1), c, :].rearrange(
                                        "p a n -> p (a n)"),
                                    start=c == 0, stop=c == NCH - 1, skip_group_check=True)
                        mm.then_inc(pv_ready, 1)
                    if R:
                        TR = R.at + NT * l
                        need(pe, rows_done, TR + 1)
                        transposed(0, rows[:, R.slot, :], x2T_ready)
                    if Q:
                        need(pe, q_lo_done, T * 2 + 2)
                    if C:
                        TC = C.at + NT * l
                        need(pe, mask_done, TC + 1)
                        pe.matmul(ps[:, 1, D + E:D + 2 * E], tri[:, :], mask[:, C.par, :],
                                  start=True, stop=False)
                        pe.matmul(ps[:, 1, D + E:D + 2 * E], ones[:, :], seen[:, C.par, :],
                                  start=False, stop=True).then_inc(count_ready, 1)
                    if R:
                        need(pe, x2T_copied, TR + 1)
                        for k in range(KD):
                            mm = pe.matmul(ps[:, 1, D:D + E], x2T[:, k * P:(k + 1) * P],
                                           wr[:, l, k, :], start=k == 0, stop=k == KD - 1)
                        mm.then_inc(logits_ready, 1)
                    if F:
                        need(pe, o_done, TF + 1)
                        transposed(1, ob, oT_ready)
                attention_steps(pe, step)
                pe.wait_ge(slots_done, NT * (l + 1))
                pe.wait_ge(seen_done, NT * (l + 1))
                pe.matmul(ps[:, 0, 0:E], ones[:, :], seen[:, 0, :], start=True,
                          stop=True).then_inc(total_ready, 1)

            def experts(l):
                def row_part(t):
                    G = t.at + MBASE[l]
                    need(pe, mT_lo_done, G)
                    pe.wait_ge(rows_loaded[t.slot], (t.quad + (uses(l, t.slot) + 1)) * 16)
                    transposed(0, xm[:, t.slot, :], mT_ready)

                def look_up(t, n, most):
                    return pe.value_load(tab[0:1, n, bass.ds(t.at, 1)], min_val=0, max_val=most)

                def at_slot(w, slot, c0, n):
                    return w[:, bass.ds(slot, 1), c0:c0 + n].rearrange("p a n -> p (a n)")

                def first_product(t, slot, expert):
                    T = t.at
                    pe.wait_ge(split_done, expert + (l * E + 1))
                    pe.wait_ge(bias_loaded, (expert + (l * E + 1)) * 16)
                    need(pe, mT_lo_done, T + MBASE[l] + 1)
                    for half in range(2):
                        if l == 0:
                            need(pe, (hid_dve, hid_act)[half], T)
                        else:
                            need(pe, up_done, T * 2 + (half - 1))
                        split_product(ps[:, 1 + half, :], [
                            (xT_hi[:, k * P:(k + 1) * P], xT_lo[:, k * P:(k + 1) * P],
                             at_slot(w_hi, slot, k * WIDE + half * SC, SC),
                             at_slot(w_lo, slot, k * WIDE + half * SC, SC)) for k in range(KD)],
                            stop=False)
                        pe.matmul(ps[:, 1 + half, :], ones2[:, :],
                                  at_slot(w_bias, slot, half * SC, SC), start=False, stop=True
                                  ).then_inc(hid_ready, 1)

                def second_product(t, slot):
                    G = t.at + MBASE[l]
                    halves = KH[l] // 4
                    need(pe, y_done, G)
                    need(pe, hT_lo_done, t.at * halves + (HBASE[l] + halves))
                    split_product(ps[:, 5, 0:D], [
                        (hT_hi[:, k * P:(k + 1) * P], hT_lo[:, k * P:(k + 1) * P],
                         at_slot(w_hi, slot, W2AT + k * D, D),
                         at_slot(w_lo, slot, W2AT + k * D, D)) for k in range(KH[l])],
                        stop=False)
                    pe.matmul(ps[:, 5, 0:D], ones2[:, :], at_slot(w_bias, slot, WIDE, D),
                              start=False, stop=True).then_inc(y_ready, 1)

                def hidden_transposes(t):
                    halves = KH[l] // 4
                    need(pe, hT_lo_done, t.at * halves + HBASE[l])
                    for h in range(halves):
                        if l == 0:
                            need(pe, (hid_dve, hid_act)[h], t.at + 1)
                        for c in range(4):
                            if l == 1 and c % 2 == 0:
                                need(pe, glu_hid, t.at * 2 + (c // 2 + 1))
                            mm = pe.transpose(ps[:, 3 + h, c * P:(c + 1) * P],
                                              hid[:, h * SC + c * P:h * SC + (c + 1) * P],
                                              ident[:, :])
                        mm.then_inc(hT_ready, 1)

                def step(j, s):
                    t, n, h_t, y_t = [row_tile(l, j, s, lag) for lag in (0, -1, 1, 2)]
                    slot = look_up(t, SLOT, 1) if t else None
                    expert = look_up(t, EXPERT, E - 1) if t else None
                    y_slot = look_up(y_t, SLOT, 1) if y_t else None
                    if y_t:
                        second_product(y_t, y_slot)
                    if h_t:
                        hidden_transposes(h_t)
                    if t:
                        first_product(t, slot, expert)
                    if n:
                        row_part(n)
                pe.wait_ge(table_ready, l + 1)
                row_part(Tile(None, 0))
                expert_steps(pe, l, step)
                pe.wait_ge(y_done, MBASE[l] + MT[l])

            pe.wait_ge(wkv_loaded, 16 * 4)
            pe.wait_ge(consts_made, 1)
            keys_values(0)
            pe.wait_ge(params_loaded, 16 * 8)
            pe.wait_ge(wq_lo_done, 1)
            attention(0)
            keys_values(1)
            experts(0)
            attention(1)
            experts(1)


def _chunks(w):
    return w.reshape(-1, P, w.shape[-1]).transpose(1, 0, 2)


def _halves(w):
    return w.reshape(*w.shape[:-1], 2, 2, WIDE // 4).swapaxes(-3, -2).reshape(w.shape)


def kernel(**inputs):
    import concourse.bacc as bacc
    from concourse.bass_utils import run_bass_kernel_spmd

    i = {k: np.asarray(v) for k, v in inputs.items()}
    attn = lambda n: [i["L0_xattn_W" + n], i["L1_xattn_W" + n].T]
    bias = lambda n: np.stack([i[f"L{l}_xattn_b{n}"] for l in range(LAYERS)])
    both = lambda n: np.stack([_chunks(w) for w in attn(n)], axis=1)
    w = np.zeros((LAYERS * E, P, WCOLS), np.float32)
    firsts = (i["L0_ffn_W1"], _halves(i["L1_ffn_gate_up_proj"].transpose(0, 2, 1)))
    seconds = (i["L0_ffn_W2"], i["L1_ffn_down_proj"].transpose(0, 2, 1))
    for l in range(LAYERS):
        for e in range(E):
            w[l * E + e, :, 0:W2AT] = _chunks(firsts[l][e]).reshape(P, -1)
            second = _chunks(seconds[l][e]).reshape(P, -1)
            w[l * E + e, :, W2AT:W2AT + second.shape[1]] = second
    biases = np.concatenate([
        np.concatenate([i["L0_ffn_b1"], i["L0_ffn_b2"]], axis=1),
        np.concatenate([_halves(i["L1_ffn_gate_up_proj_bias"]), i["L1_ffn_down_proj_bias"]], axis=1)])
    per_row = lambda v: v.reshape(LAYERS, KD, P).transpose(2, 0, 1)
    data = {
        "x": i["x"].reshape(N, D),
        "ctxT": i["ctx_1024"].transpose(2, 0, 1).reshape(KD, P, B, S).transpose(1, 2, 0, 3),
        "wkv": np.stack([both("k"), both("v")], axis=2),
        "wq": both("q"), "wo": both("o"),
        "wr": np.stack([_chunks(i["L0_ffn_Wr"]), _chunks(i["L1_ffn_router_weight"].T)], axis=1),
        "bq": per_row(bias("q")), "bk": per_row(bias("k")), "bv": bias("v"), "bo": bias("o"),
        "br": np.stack([i["L0_ffn_br"], i["L1_ffn_router_bias"]]),
        "gates": np.concatenate([i["g_xattn"], i["g_ffn"]]),
        "biases": biases.reshape(P, -1), "weights": w,
    }
    data = {k: np.ascontiguousarray(v) for k, v in data.items()}
    nc = bacc.Bacc("TRN2", target_bir_lowering=False, num_devices=1)
    aps = {k: nc.dram_tensor(f"in_{k}", v.shape, F32, kind="ExternalInput").ap()
           for k, v in data.items()}
    aps["out"] = nc.dram_tensor("out", (N, D), F32, kind="ExternalOutput").ap()
    build_program(nc, aps)
    r = run_bass_kernel_spmd(nc, [{f"in_{k}": v for k, v in data.items()}], core_ids=[0])
    return r.results[0]["out"].reshape(B, SEQ, D)
```

```python
from contextlib import ExitStack

import numpy as np
import concourse.bass as bass
from concourse import mybir

F32 = mybir.dt.float32
R32 = mybir.dt.float32r
I32 = mybir.dt.int32
U32 = mybir.dt.uint32
ALU = mybir.AluOpType
ACT = mybir.ActivationFunctionType
AX = mybir.AxisListType

P = 128
LAYERS = 2
B, SEQ, D = 2, 1024, 256
N = B * SEQ
NT = N // P
KD = D // P
H, DH, S = 16, 16, 77
HC = P // DH
SC = 512
FLAT = H * S
NCH = -(-FLAT // P)
HPB = SC // S
DV = DH + 1
SPAN = 3
E = 8
TOPK = (2, 4)
WIDE = 1024
KH = (8, 4)
REGION = N + P
MT = tuple(N * k // P + E - 1 for k in TOPK)
IDLE = E - 1
SPARE = (E + IDLE) * P
ROW = D + E
W2AT = KD * WIDE
WCOLS = W2AT + 8 * D
BCOLS = WIDE + D
EPS = 1e-5
GROUPS = ((0, 4), (4, 8), (8, NCH))


def first_head(c):
    return c * P // S


def build_program(nc, a):
    with ExitStack() as ctx:
        def sb(name, shape, dt=F32):
            return ctx.enter_context(nc.sbuf_tensor(name, shape, dt))

        def sem(name):
            return ctx.enter_context(nc.semaphore(name))

        def dram(name, shape, dt=F32):
            return nc.dram_tensor(name, shape, dt, kind="Internal").ap()

        dispatched = [dram(f"dispatched{l}", (E * REGION + IDLE * P, ROW)) for l in range(LAYERS)]
        results = [dram(f"results{l}", (SPARE + TOPK[l] * N, D)) for l in range(LAYERS)]
        attended = [dram(f"attended{l}", (NT, P, D)) for l in range(LAYERS)]
        flat_values = dram("flat_values", (LAYERS, B, H, S, DV))
        split_bias = dram("split_bias", (2, LAYERS * E, BCOLS))

        ident = sb("ident", [P, P])
        tri = sb("tri", [P, P])
        ones = sb("ones", [P, P])
        ones2 = sb("ones2", [2, P], R32)
        head_mask = sb("head_mask", [P, HC])
        block_mask = sb("block_mask", [P, NCH, SPAN])
        expert_ids = sb("expert_ids", [P, E])
        region_base = sb("region_base", [P, E])
        rank_rows = sb("rank_rows", [P, 4])
        token_ids = sb("token_ids", [P, LAYERS, NT])
        eps_col = sb("eps_col", [P, 1])
        minus_half = sb("minus_half", [P, 1])
        minus_one = sb("minus_one", [P, 1])
        tile_edges = sb("tile_edges", [1, 15])
        tri8 = sb("tri8", [1, E, E])
        alternate = sb("alternate", [1, E])
        tile_ids = sb("tile_ids", [1, max(MT)])
        zero_rows = sb("zero_rows", [P, ROW])
        gates = sb("gates", [P, 4])
        tgates = sb("tgates", [P, 4])

        wo = sb("wo", [P, LAYERS, KD, D])
        wq_hi = sb("wq_hi", [P, LAYERS, KD, D], R32)
        wq_lo = sb("wq_lo", [P, LAYERS, KD, D], R32)
        wr = sb("wr", [P, LAYERS, KD, E])
        ctxT = sb("ctxT", [P, B, KD, S])
        bq = sb("bq", [P, LAYERS, KD])
        bk = sb("bk", [P, LAYERS, KD])
        bv = sb("bv", [S, LAYERS, D])
        bo = sb("bo", [P, LAYERS, D])
        br = sb("br", [P, LAYERS, E])
        key_hi = sb("key_hi", [P, B, KD, HC * S], R32)
        key_lo = sb("key_lo", [P, B, KD, HC * S], R32)
        kT = sb("kT", [P, S])
        kT_hi = sb("kT_hi", [P, S], R32)
        kT_lo = sb("kT_lo", [P, S])
        vals = sb("vals", [S, B, H, DV])
        flat_v = sb("flat_v", [P, B, NCH, DV])
        v_blocks = sb("v_blocks", [P, B, NCH, SPAN * DV])
        xt = sb("xt", [P, 4, D])
        x2 = sb("x2", [P, 4, D])
        rows = sb("rows", [P, 4, ROW])
        xn = sb("xn", [P, 2, D])
        xT_hi = sb("xT_hi", [P, D], R32)
        xT_lo = sb("xT_lo", [P, D], R32)
        q_hi = sb("q_hi", [P, KD, P], R32)
        q_lo = sb("q_lo", [P, KD, P], R32)
        probs = sb("probs", [P, 2, NCH * P])
        probsT = sb("probsT", [P, NCH * P])
        top = sb("top", [P, H])
        rden = sb("rden", [P, H])
        ob = sb("ob", [P, D])
        oT = sb("oT", [P, D])
        xg = sb("xg", [P, 4, D])
        x2T = sb("x2T", [P, D])
        st1, mv1, rs1 = sb("st1", [P, 6]), sb("mv1", [P, 2]), sb("rs1", [P, 4])
        st2, mv2, rs2 = sb("st2", [P, 6]), sb("mv2", [P, 2]), sb("rs2", [P, 4])
        logits = sb("logits", [P, E])
        best = sb("best", [P, E])
        best_at = sb("best_at", [P, E], U32)
        best_f = sb("best_f", [P, 4])
        chosen = sb("chosen", [P, 4, E, 4])
        ranked = sb("ranked", [P, E, 4])
        ranks = sb("ranks", [P, E])
        mask = sb("mask", [P, 2, E])
        seen = sb("seen", [P, 2, E])
        slots = sb("slots", [P, E])
        slot_k = sb("slot_k", [P, 4, E])
        slot_f = sb("slot_f", [P, 4])
        slot_at = sb("slot_at", [P, 4, 4], U32)

        ysb = sb("ysb", [P, 2, 4, D])
        x2in = sb("x2in", [P, 2, D])
        bests = sb("bests", [P, NT, 4])
        mix = sb("mix", [P, NT, 4])
        mix_sum = sb("mix_sum", [P, NT])
        shares = sb("shares", [P, NT, 4])

        raw = sb("raw", [P, WCOLS])
        w_hi = sb("w_hi", [P, 2, WCOLS], R32)
        w_lo = sb("w_lo", [P, 2, WCOLS], R32)
        w_bias = sb("w_bias", [2, 2, BCOLS], R32)
        BPART = LAYERS * E * BCOLS // P
        early = x2in[:, :, :].rearrange("p a b -> p (a b)")
        braw, idle_rows = early[:, 0:BPART], early[:, BPART:BPART + ROW]
        finals = raw[:, :].rearrange("p (t k d) -> p t k d", t=4, k=4)
        hid = probs[:, 0, 0:WIDE]
        wkv = probs[:, 1, 0:2 * KD * D].rearrange("p (w k n) -> p w k n", w=2, k=KD)
        gate_s = probs[:, 1, 0:512]
        up_s = probs[:, 1, 512:1024]
        sig_s = probsT[:, 0:512]
        GH = SC // 2
        hT_hi = sb("hT_hi", [P, WIDE], R32)
        hT_lo = sb("hT_lo", [P, WIDE], R32)
        b_hi, b_lo = [t[:, 0:BPART] for t in (hT_hi, hT_lo)]
        xm = sb("xm", [P, 4, ROW])
        wq = xm[:, :, :].rearrange("p a b -> p (a b)")[:, 0:LAYERS * KD * D].rearrange(
            "p (l k n) -> p l k n", l=LAYERS, k=KD)
        y = ysb[:, :].rearrange("p a b c -> p (a b) c")
        y_at = sb("y_at", [P, 8], U32)
        TAB = 8
        ROWAT, EXPERT, SLOT, SPLIT0, SPLIT1, NEXT, LOAD, PLACE = range(TAB)
        row_of = lambda n, c0, d: probs[0:1, n, c0:c0 + E * max(MT)].rearrange(
            "p (a b) -> p a b", b=d)
        tab_f = row_of(1, 0, max(MT))
        tab = sb("tab", [1, TAB, max(MT)], I32)
        t_cnt = sb("t_cnt", [1, E])
        cnt_i = sb("cnt_i", [1, E], I32)
        t_gt = sb("t_gt", [1, E, 15])
        t_tiles = sb("t_tiles", [1, E])
        t_tri = sb("t_tri", [1, E, E])
        t_end = sb("t_end", [1, E])
        t_le = row_of(0, 0, E)
        t_m = row_of(0, E * max(MT), E)
        t_e = sb("t_e", [1, max(MT)])
        t_d = sb("t_d", [1, max(MT)])
        t_new = sb("t_new", [1, max(MT)])

        ps = ctx.enter_context(nc.psum_tensor("ps", [P, 8, SC], F32))

        (params_loaded, wkv_loaded, consts_made, small_made, gates_ready, bo_scaled,
         wq_hi_done, wq_lo_done, kT_ready, kT_done, kT_hi_done, kT_lo_done, keys_done, v_ready,
         v_done, v_stored, v_flat, v_blocks_done) = [sem(n) for n in (
            "params_loaded", "wkv_loaded", "consts_made", "small_made", "gates_ready",
            "bo_scaled", "wq_hi_done", "wq_lo_done", "kT_ready", "kT_done", "kT_hi_done",
            "kT_lo_done", "keys_done", "v_ready", "v_done", "v_stored", "v_flat",
            "v_blocks_done")]
        x_loaded = [sem(f"x_loaded{r}") for r in range(4)]
        (stats1, moments1, var1, rstd1, offset1, xn_done, xnT_ready, xT_hi_done, xT_lo_done, q_ready,
         q_hi_done, q_lo_done, scores_ready, max_done, shifted_part, shifted, exp_done, pT_ready, pT_copied,
         pv_ready, rden_done, o_done, oT_ready, oT_copied, proj_ready, xg_done, x2_done, stats2,
         moments2, var2, rstd2, offset2, rows_done, x2T_ready, x2T_copied, logits_ready, logits_done,
         best_done, best_at_done, best_f_done, chosen_done, mask_done, ranked_done, ranks_done,
         code_done, seen_done, count_ready, slots_done, slot_k_done, slot_f_done, slot_done) = [
            sem(n) for n in (
                "stats1", "moments1", "var1", "rstd1", "offset1", "xn_done", "xnT_ready", "xT_hi_done",
                "xT_lo_done", "q_ready", "q_hi_done", "q_lo_done", "scores_ready", "max_done",
                "shifted_part", "shifted", "exp_done", "pT_ready", "pT_copied", "pv_ready", "rden_done",
                "o_done", "oT_ready", "oT_copied", "proj_ready", "xg_done", "x2_done", "stats2",
                "moments2", "var2", "rstd2", "offset2", "rows_done", "x2T_ready", "x2T_copied",
                "logits_ready", "logits_done", "best_done", "best_at_done", "best_f_done",
                "chosen_done", "mask_done", "ranked_done", "ranks_done", "code_done",
                "seen_done", "count_ready", "slots_done", "slot_k_done", "slot_f_done",
                "slot_done")]
        x2_stored = [sem(f"x2_stored{r}") for r in range(4)]
        scattered = [sem(f"scattered{r}") for r in range(4)]
        (total_ready, seen_zero, table_step, table_ready, zeros_stored, gates_passed) = [
            sem(n) for n in ("total_ready", "seen_zero", "table_step", "table_ready",
                             "zeros_stored", "gates_passed")]
        results_loaded = [sem(f"results_loaded{r}") for r in range(2)]
        finals_loaded = [sem(f"finals_loaded{r}") for r in range(4)]
        (below_done, expw_done, mix_step, shares_done, added) = [sem(n) for n in (
            "below_done", "expw_done", "mix_step", "shares_done", "added")]
        out_stored = [sem(f"out_stored{r}") for r in range(4)]
        raw_loaded, hi_done, split_done, bias_split, bias_stored, bias_loaded = [sem(n) for n in (
            "raw_loaded", "hi_done", "split_done", "bias_split", "bias_stored", "bias_loaded")]
        rows_loaded = [sem(f"rows_loaded{r}") for r in range(4)]
        y_scattered = [sem(f"y_scattered{r}") for r in range(8)]
        (y_at_done, mT_ready, mT_hi_done, mT_lo_done, hid_ready, hid_dve, hid_act, gate_done,
         sig_done, up_done, glu_done, glu_hid, hT_ready, hT_hi_done, hT_lo_done, y_ready, y_done) = [
            sem(n) for n in (
                "y_at_done", "mT_ready", "mT_hi_done", "mT_lo_done", "hid_ready", "hid_dve",
                "hid_act", "gate_done", "sig_done", "up_done", "glu_done", "glu_hid", "hT_ready",
                "hT_hi_done", "hT_lo_done", "y_ready", "y_done")]

        def need(eng, s, count):
            if isinstance(count, int) and count <= 0:
                return
            eng.wait_ge(s, count)

        def gate(eng, s, count):
            if isinstance(count, int) and count <= 0:
                return
            eng.wait_ge(s, count)
            eng.sem_inc(gates_passed, 1)

        class Tile:
            def __init__(self, j, const, unroll=4):
                self.c = const
                self.slot = const % 4
                self.slot8 = const % 8
                self.par = const % 2
                self.at, self.pair, self.quad, self.oct = [
                    const // n if j is None else j * (unroll // n) + const // n
                    for n in (1, 2, 4, 8)]

        LAGS = 7
        LOOPS = (NT - LAGS) // 4

        def attention_steps(eng, step):
            for s in range(LAGS):
                step(None, s)
            with eng.Fori(0, LOOPS) as j:
                for u in range(4):
                    step(j, LAGS + u)
            for s in range(LAGS + 4 * LOOPS, NT + LAGS):
                step(None, s)

        def stage(j, s, lag):
            if j is None and not 0 <= s - lag < NT:
                return None
            return Tile(j, s - lag)

        def expert_steps(eng, l, step):
            for s in range(3):
                step(None, s)
            loops = (MT[l] - 4) // 8
            with eng.Fori(0, loops) as j:
                for u in range(8):
                    step(j, 3 + u)
            for s in range(8 * loops + 3, MT[l] + 2):
                step(None, s)

        def row_tile(l, j, s, lag):
            if j is None and not 0 <= s - lag < MT[l]:
                return None
            return Tile(j, s - lag, 8)

        def scatter_count(l, r, quad):
            return quad * (16 * TOPK[l]) + (l * (16 * TOPK[0] * (NT // 4)) + HEAD_START)

        def idle_part(k):
            at = E * REGION + k % IDLE * P
            return dispatched[k // IDLE][at:at + P, :]

        def uses(l, r, ring=4):
            return sum(len(range(r, MT[x], ring)) for x in range(l))

        def y_count(l, t):
            return t.oct * 16 + (uses(l, t.slot8, 8) * 16 + HEAD_START)

        def adds(cl, at):
            return at * TOPK[cl] + cl * NT * TOPK[0]

        HEAD_START = 16
        MBASE = [0, MT[0]]
        HBASE = [0, KH[0] // 4 * MT[0]]

        pieces = []
        for c in range(KD):
            h = c * HC
            while h < (c + 1) * HC:
                n = min((c + 1) * HC, (h // HPB + 1) * HPB) - h
                pieces.append((c, h, n))
                h += n
        SCORE_BANK, PT_BANK = 2, 5
        full = H // HPB
        rest = H - full * HPB


        tile_of = lambda ap: ap.rearrange("a p d -> (a p) d")
        x_tiles = a["x"].rearrange("(t p) d -> t p d", p=P)
        out_tiles = a["out"].rearrange("(t p) d -> t p d", p=P)

        block = ctx.enter_context(nc.Block())

        @block.sync
        def _(sp):
            for dst, src in ((wkv, a["wkv"][0]), (ctxT[:, :, :, :], a["ctxT"]),
                             (bk[:, :, :], a["bk"]),
                             (bv[:, :, :], a["bv"].partition_broadcast(S))):
                sp.dma_start(dst, src).then_inc(wkv_loaded, 16)
            for t in range(4):
                sp.dma_start(xt[:, t, :], x_tiles[t]).then_inc(x_loaded[t], 16)
            for dst, src in ((wq[:, :, :, :], a["wq"]), (wo[:, :, :, :], a["wo"]),
                             (wr[:, :, :, :], a["wr"]), (bq[:, :, :], a["bq"]),
                             (bo[:, :, :], a["bo"].partition_broadcast(P)),
                             (br[:, :, :], a["br"].partition_broadcast(P)),
                             (gates[:, :], a["gates"].partition_broadcast(P)),
                             (braw, a["biases"])):
                sp.dma_start(dst, src).then_inc(params_loaded, 16)

            def values(l):
                whole = FLAT // P
                for b in range(B):
                    sp.wait_ge(v_done, l * B + b + 1)
                    sp.dma_start(flat_values[l, b].rearrange("h s d -> s h d"),
                                 vals[:, b, :, :]).then_inc(v_stored, 16)
                sp.wait_ge(v_stored, 16 * B * (l + 1))
                need(sp, v_blocks_done, B * l)
                for b in range(B):
                    src = flat_values[l, b].rearrange("h s d -> (h s) d")
                    sp.dma_start(flat_v[:, b, 0:whole, :], src[0:whole * P].rearrange(
                        "(c p) d -> p c d", p=P)).then_inc(v_flat, 16)
                    sp.dma_start(flat_v[0:FLAT - whole * P, b, whole, :],
                                 src[whole * P:FLAT]).then_inc(v_flat, 16)

            def load_results(t):
                K = TOPK[0]
                gate(sp, added, adds(0, t.at - 1) if t.c > 1 else 0)
                sp.dma_start(x2in[:, t.par, :], tile_of(attended[0][bass.ds(t.at, 1)])
                             ).then_inc(results_loaded[t.par], 16)
                src = results[0][SPARE:].rearrange("(t p k) d -> t p k d", k=K, p=P)
                sp.dma_start(ysb[:, t.par, 0:K, :], src[bass.ds(t.at, 1)].rearrange(
                    "a p k d -> (a p) k d")).then_inc(results_loaded[t.par], 16)

            def results_there(l):
                for r in range(8):
                    sp.wait_ge(y_scattered[r], 16 * uses(l + 1, r, 8) + HEAD_START)
                for r in range(4):
                    sp.wait_ge(x2_stored[r], 16 * (l + 1) * (NT // 4) + HEAD_START)

            def experts(l):
                sp.wait_ge(table_ready, l + 1)
                if l + 1 < LAYERS:
                    sp.dma_start(wkv, a["wkv"][l + 1]).then_inc(wkv_loaded, 16)
                for e in range(0, E, 2):
                    c = sp.value_load(cnt_i[0:1, e:e + 1], min_val=0, max_val=N)
                    sp.dma_start(dispatched[l][bass.ds(c + e * REGION, P), :],
                                 zero_rows[:, :]).then_inc(zeros_stored, 16)
                for r in range(4):
                    sp.wait_ge(scattered[r], scatter_count(l, r, NT // 4))
                for r in range(8):
                    sp.wait_ge(y_scattered[r], uses(l, r, 8) * 16 + HEAD_START)
                sp.wait_ge(zeros_stored, 16 * (LAYERS * IDLE - 12 + E * (l + 1)))

                def load(t):
                    at = sp.value_load(tab[0:1, ROWAT, bass.ds(t.at, 1)], min_val=0,
                                       max_val=E * REGION + (IDLE - 1) * P)
                    before = MBASE[l] if isinstance(t.at, int) and t.at < 4 \
                        else t.at + (MBASE[l] - 3)
                    gate(sp, mT_ready, before)
                    gate(sp, y_at_done, before)
                    sp.dma_start(xm[:, t.slot, :], dispatched[l][bass.ds(at, P), :]
                                 ).then_inc(rows_loaded[t.slot], 16)

                for t in range(4):
                    load(Tile(None, t))
                loops = (MT[l] - 4) // 4
                with sp.Fori(0, loops) as j:
                    for u in range(4):
                        load(Tile(j, 4 + u))
                for t in range(4 + 4 * loops, MT[l]):
                    load(Tile(None, t))

            values(0)
            sp.wait_ge(consts_made, 1)
            for k in range(12, LAYERS * IDLE):
                sp.dma_start(idle_part(k), idle_rows).then_inc(zeros_stored, 16)
            for part, t in enumerate((b_hi, b_lo)):
                sp.wait_ge(bias_split, part + 1)
                sp.dma_start(split_bias[part].rearrange("e n -> (e n)").rearrange(
                    "(p n) -> p n", p=P), t.bitcast(F32)).then_inc(bias_stored, 16)
            with sp.Fori(0, NT // 4 - 1) as j:
                for u in range(4):
                    t = Tile(j, 4 + u)
                    gate(sp, xg_done, t.at - 3)
                    sp.dma_start(xt[:, t.slot, :], tile_of(x_tiles[bass.ds(t.at, 1)])
                                 ).then_inc(x_loaded[t.slot], 16)
            experts(0)
            values(1)
            results_there(0)
            for t in range(4):
                load_results(Tile(None, t))
            with sp.Fori(0, NT // 4 - 1) as j:
                for u in range(4):
                    load_results(Tile(j, 4 + u))
            experts(1)
            results_there(1)

            sp.wait_ge(raw_loaded, 16 * (LAYERS * E + 1))

            def load_final(t):
                if not isinstance(t.at, int):
                    gate(sp, added, adds(1, t.at - 2 - t.par))
                sp.dma_start(finals[:, t.slot, :, :], results[1][SPARE:].rearrange(
                    "(t p k) d -> t p k d", k=4, p=P)[bass.ds(t.at, 1)].rearrange(
                    "a p k d -> (a p) k d")).then_inc(finals_loaded[t.slot], 16)
                sp.dma_start(x2[:, t.slot, :], tile_of(attended[1][bass.ds(t.at, 1)])
                             ).then_inc(finals_loaded[t.slot], 16)

            for t in range(4):
                load_final(Tile(None, t))
            with sp.Fori(0, NT // 4 - 1) as j:
                for u in range(4):
                    load_final(Tile(j, 4 + u))

        @block.gpsimd
        def _(pool):
            made = [0]

            def make(ins):
                made[0] += 1
                ins.then_inc(small_made, 1)

            def all_made():
                pool.wait_ge(small_made, made[0])

            def load_raw(e):
                pool.dma_start(raw[:, :], tile_of(a["weights"][bass.ds(e, 1)])
                               ).then_inc(raw_loaded, 16)

            def split(slot, e):
                gate(pool, bias_loaded, e * 16)
                pool.dma_start(w_bias[:, slot, :].bitcast(F32), split_bias[:, bass.ds(e, 1), :]
                               .rearrange("h a n -> h (a n)")).then_inc(bias_loaded, 16)
                gate(pool, raw_loaded, (e + 1) * 16)
                pool.tensor_scalar(w_hi[:, slot, :], raw[:, :], 1.0, 1.0, ALU.mult,
                                   ALU.mult).then_inc(hi_done, 1)
                gate(pool, hi_done, e + 1)
                gate(pool, bias_loaded, (e + 1) * 16)
                pool.tensor_tensor(w_lo[:, slot, :], raw[:, :], w_hi[:, slot, :].bitcast(F32),
                                   ALU.subtract).then_inc(split_done, 1)

            load_raw(0)
            make(pool.memset(vals[:, :, :, :], 1.0))
            make(pool.memset(head_mask[:, :], 1.0))
            make(pool.memset(block_mask[:, :, :], 1.0))
            make(pool.memset(ident[:, :], 0.0))
            make(pool.memset(tri[:, :], 1.0))
            make(pool.memset(ones[:, :], 1.0))
            make(pool.memset(tri8[:, :, :], 1.0))
            make(pool.memset(zero_rows[:, :], 0.0))
            make(pool.memset(idle_rows, 0.0))
            make(pool.memset(flat_v[:, :, :, :], 0.0))
            make(pool.memset(alternate[:, 0:E:2], 1.0))
            make(pool.memset(alternate[:, 1:E:2], -1.0))
            all_made()

            def keep(t, pattern, compare, base, mult, fill=0.0):
                make(pool.affine_select(out=t, in_=t, pattern=pattern, compare_op=compare,
                                        fill=fill, base=base, channel_multiplier=mult))

            keep(head_mask[:, :], [[-DH, HC]], ALU.is_ge, 0, 1)
            all_made()
            keep(head_mask[:, :], [[DH, HC]], ALU.is_ge, DH - 1, -1)
            keep(ident[:, :], [[1, P]], ALU.not_equal, 0, -1, fill=1.0)
            for c in range(NCH):
                keep(block_mask[:, c, :], [[-S, SPAN]], ALU.is_ge, c * P - S * first_head(c), 1)
            all_made()
            for c in range(NCH):
                keep(block_mask[:, c, :], [[S, SPAN]], ALU.is_ge,
                     S - 1 - c * P + S * first_head(c), -1)
            keep(tri[:, :], [[1, P]], ALU.is_gt, 0, -1)
            keep(tri8[:, :, :], [[1, E], [-1, E]], ALU.is_ge, 0, 0)
            make(pool.memset(alternate[:, E - 1:E], 0.0))

            def count_up(t, pattern, base, mult):
                make(pool.iota(t, pattern=pattern, base=base, channel_multiplier=mult,
                               allow_small_or_imprecise_dtypes=True))

            count_up(expert_ids[:, :], [[1, E]], 0, 0)
            count_up(region_base[:, :], [[REGION, E]], 0, 0)
            count_up(rank_rows[:, :], [[1, 4]], 0, 0)
            for l in range(LAYERS):
                count_up(token_ids[:, l, :], [[P * TOPK[l], NT]], SPARE, TOPK[l])
            count_up(tile_edges[:, :], [[P, 15]], P, 0)
            count_up(tile_ids[:, :], [[1, max(MT)]], 0, 0)
            count_up(zero_rows[:, D:ROW], [[P, E]], 0, 1)
            count_up(idle_rows[:, D:ROW], [[P, E]], E * P, 1)
            make(pool.memset(eps_col[:, :], EPS))
            make(pool.memset(minus_half[:, :], -0.5))
            make(pool.memset(minus_one[:, :], -1.0))
            make(pool.memset(probs[:, :, FLAT:], 0.0))
            make(pool.tensor_copy(ones2[:, :], ones[0:2, :]))
            all_made()
            pool.sem_inc(consts_made, 1)
            for k, s in enumerate(scattered + y_scattered):
                pool.dma_start(idle_part(k), idle_rows).then_inc(s, HEAD_START)

            pool.wait_ge(params_loaded, 16 * 8)
            pool.tensor_scalar(b_hi, braw, 1.0, 1.0, ALU.mult,
                               ALU.mult).then_inc(bias_split, 1)
            pool.wait_ge(bias_split, 1)
            pool.tensor_tensor(b_lo, braw, b_hi.bitcast(F32),
                               ALU.subtract).then_inc(bias_split, 1)
            pool.wait_ge(bo_scaled, LAYERS)

            def attention(l):
                def scale_and_offset(T, mom, mv, rs, var, rstd, offset, used):
                    need(pool, used, T)
                    need(pool, mom, T + 1)
                    pool.tensor_tensor(rs[:, 0:1], mv[:, 1:2], eps_col[:, :],
                                       ALU.add).then_inc(var, 1)
                    pool.tensor_tensor(rs[:, 2:3], mv[:, 0:1], minus_one[:, :], ALU.mult)
                    need(pool, var, T + 1)
                    pool.tensor_tensor(rs[:, 1:2], rs[:, 0:1], minus_half[:, :],
                                       ALU.pow).then_inc(rstd, 1)
                    need(pool, rstd, T + 1)
                    pool.tensor_tensor(rs[:, 3:4], rs[:, 2:3], rs[:, 1:2],
                                       ALU.mult).then_inc(offset, 1)

                def step(j, s):
                    A, Q, _, _, G, _, _, Z = [stage(j, s, lag) for lag in range(LAGS + 1)]
                    if Z:
                        T = Z.at + NT * l
                        gate(pool, slot_done, T + 1)
                        gate(pool, code_done, T + 1)
                        gate(pool, rows_done, T + 1)
                        for k in range(TOPK[l]):
                            pool.indirect_dma_start(
                                out=dispatched[l], out_offset=bass.IndirectOffsetOnAxis(
                                    ap=slot_at[:, Z.slot, k:k + 1], axis=0),
                                in_=rows[:, Z.slot, :], in_offset=None
                            ).then_inc(scattered[Z.slot], 16)
                    if A:
                        scale_and_offset(A.at + NT * l, moments1, mv1, rs1, var1, rstd1, offset1,
                                         xn_done)
                    if G:
                        scale_and_offset(G.at + NT * l, moments2, mv2, rs2, var2, rstd2, offset2,
                                         rows_done)
                    if Q:
                        T = Q.at + NT * l
                        if l == 0:
                            need(pool, x_loaded[Q.slot], (Q.quad + 1) * 16)
                        else:
                            need(pool, added, adds(0, Q.at + 1))
                        need(pool, x2_done, T - 3)
                        need(pool, xn_done, T + 1)
                        pool.tensor_tensor(xg[:, Q.slot, :], xt[:, Q.slot, :], bo[:, l, :],
                                           ALU.add).then_inc(xg_done, 1)
                attention_steps(pool, step)

            def experts(l):
                def step(j, s):
                    if t := row_tile(l, j, s, 2):
                        G = t.at + MBASE[l]
                        gate(pool, y_at_done, G + 1)
                        gate(pool, y_done, G + 1)
                        pool.indirect_dma_start(
                            out=results[l], out_offset=bass.IndirectOffsetOnAxis(
                                ap=y_at[:, t.slot8:t.slot8 + 1], axis=0),
                            in_=y[:, t.slot8, :], in_offset=None
                        ).then_inc(y_scattered[t.slot8], 16)
                    t = row_tile(l, j, s, 1)
                    if t and not (j is None and t.c == 0):
                        read = lambda n, lo, hi: pool.value_load(
                            tab[0:1, n, bass.ds(t.at, 1)], min_val=lo, max_val=hi)
                        flags = [read(SPLIT0, 0, 1), read(SPLIT1, 0, 1)]
                        nxt = read(NEXT, 1, LAYERS * E - 1)
                        after = read(LOAD, 2, LAYERS * E - 1)
                        for slot in range(2):
                            with pool.If(flags[slot]):
                                split(slot, nxt)
                                gate(pool, split_done, nxt + 1)
                                load_raw(after)
                                pool.nop()
                expert_steps(pool, l, step)

            attention(0)
            pool.wait_ge(bias_stored, 32)
            split(0, 0)
            pool.wait_ge(split_done, 1)
            load_raw(1)
            split(1, 1)
            pool.wait_ge(split_done, 2)
            load_raw(2)
            pool.wait_ge(table_ready, 1)
            experts(0)
            split(1, E + 1)
            pool.wait_ge(split_done, E + 2)
            load_raw(E + 2)
            attention(1)
            pool.wait_ge(table_ready, 2)
            experts(1)
            pool.wait_ge(raw_loaded, 16 * (LAYERS * E + 1))

        @block.scalar
        def _(act):
            for r in range(4):
                act.sem_inc(x2_stored[r], HEAD_START)
            act.wait_ge(params_loaded, 16 * 8)
            act.activation(tgates[:, :], gates[:, :], ACT.Tanh).then_inc(gates_ready, 1)
            act.activation(wq_hi[:, :, :, :], wq[:, :, :, :], ACT.Copy).then_inc(wq_hi_done, 1)
            act.wait_ge(gates_ready, 1)
            for l in range(LAYERS):
                act.activation(bo[:, l, :], bo[:, l, :], ACT.Copy, scale=tgates[:, l:l + 1]
                               ).then_inc(bo_scaled, 1)

            def attention(l):
                def copy_probs(n, TF):
                    c0, c1 = GROUPS[n]
                    need(act, pT_ready, TF * 3 + (n + 1))
                    act.activation(probsT[:, c0 * P:c1 * P],
                                   ps[:, PT_BANK + n % 2, 0:(c1 - c0) * P],
                                   ACT.Copy).then_inc(pT_copied, 1)

                def step(j, s):
                    _, Q, S2, F, _, R, _, _ = [stage(j, s, lag) for lag in range(LAGS + 1)]
                    if Q:
                        T = Q.at + NT * l
                        need(act, xnT_ready, T - 1)
                        need(act, offset1, T + 1)
                        act.activation(xn[:, Q.par, :], xt[:, Q.slot, :], ACT.Identity,
                                       bias=rs1[:, 3:4], scale=rs1[:, 1:2]).then_inc(xn_done, 1)
                    if Q:
                        need(act, q_ready, T)
                        need(act, xnT_ready, T + 1)
                        act.activation(xT_hi[:, :], ps[:, 0, 0:D], ACT.Copy
                                       ).then_inc(xT_hi_done, 1)
                    if R:
                        TR = R.at + NT * l
                        need(act, scattered[R.slot], scatter_count(l, R.slot, R.quad))
                        need(act, offset2, TR + 1)
                        act.activation(rows[:, R.slot, 0:D], x2[:, R.slot, 0:D], ACT.Identity,
                                       bias=rs2[:, 3:4], scale=rs2[:, 1:2]).then_inc(rows_done, 1)
                    if F:
                        TF = F.at + NT * l
                        need(act, pv_ready, TF)
                        for n in range(2):
                            copy_probs(n, TF)
                    if Q:
                        need(act, scores_ready, T)
                        need(act, q_ready, T + 1)
                        for c in range(KD):
                            act.activation(q_hi[:, c, :], ps[:, 1, c * P:(c + 1) * P],
                                           ACT.Identity, bias=bq[:, l, c:c + 1]
                                           ).then_inc(q_hi_done, 1)
                    if F:
                        copy_probs(2, TF)
                    if R:
                        need(act, logits_ready, TR)
                        need(act, x2T_ready, TR + 1)
                        act.activation(x2T[:, :], ps[:, 0, 0:D], ACT.Copy
                                       ).then_inc(x2T_copied, 1)
                    if F:
                        need(act, proj_ready, TF)
                        need(act, oT_ready, TF + 1)
                        act.activation(oT[:, :], ps[:, 1, 0:D], ACT.Copy).then_inc(oT_copied, 1)
                    if S2:
                        T = S2.at + NT * l
                        need(act, shifted, T + 1)
                        act.activation(probs[:, S2.par, 0:FLAT], probs[:, S2.par, 0:FLAT],
                                       ACT.Exp, scale=(DH ** -0.5 if l == 0 else 1.0)
                                       ).then_inc(exp_done, 1)
                    if R:
                        need(act, x2_done, TR + 1)
                        act.dma_start(tile_of(attended[l][bass.ds(R.at, 1)]), x2[:, R.slot, :]
                                      ).then_inc(x2_stored[R.slot], 16)
                attention_steps(act, step)

            def experts(l):
                halves = KH[l] // 4

                def row_part(t):
                    need(act, hid_ready, (t.at + MBASE[l]) * 2)
                    need(act, mT_ready, t.at + MBASE[l] + 1)
                    act.activation(xT_hi[:, :], ps[:, 0, 0:D], ACT.Copy).then_inc(mT_hi_done, 1)

                def step(j, s):
                    t, n, h_t, y_t = [row_tile(l, j, s, lag) for lag in (0, -1, 1, 2)]
                    if y_t:
                        need(act, y_scattered[y_t.slot8], y_count(l, y_t))
                        need(act, y_ready, y_t.at + (MBASE[l] + 1))
                        act.activation(y[:, y_t.slot8, :], ps[:, 5, 0:D], ACT.Copy
                                       ).then_inc(y_done, 1)
                    if h_t:
                        for h in range(halves):
                            need(act, hT_ready, h_t.at * halves + (HBASE[l] + h + 1))
                            act.activation(hT_hi[:, h * SC:(h + 1) * SC], ps[:, 3 + h, :],
                                           ACT.Copy).then_inc(hT_hi_done, 1)
                    if t and l == 0:
                        need(act, hT_ready, t.at * 2)
                        need(act, hid_ready, t.at * 2 + 2)
                        act.activation(hid[:, SC:WIDE], ps[:, 2, :], ACT.Relu
                                       ).then_inc(hid_act, 1)
                    if t and l == 1:
                        need(act, glu_hid, t.at * 2)
                        for h in range(2):
                            half = slice(h * GH, (h + 1) * GH)
                            if h and n:
                                row_part(n)
                            need(act, gate_done, t.at * 2 + (h + 1))
                            act.activation(sig_s[:, half], gate_s[:, half], ACT.Sigmoid,
                                           scale=1.702).then_inc(sig_done, 1)
                    if n and not (t and l == 1):
                        row_part(n)
                act.wait_ge(table_ready, l + 1)
                for e in range(1, E, 2):
                    c = act.value_load(cnt_i[0:1, e:e + 1], min_val=0, max_val=N)
                    act.dma_start(dispatched[l][bass.ds(c + e * REGION, P), :],
                                  zero_rows[:, :]).then_inc(zeros_stored, 16)
                act.wait_ge(below_done, l + 1)
                act.activation(mix[:, :, 0:TOPK[l]], mix[:, :, 0:TOPK[l]], ACT.Exp
                               ).then_inc(expw_done, 1)
                row_part(Tile(None, 0))
                expert_steps(act, l, step)

            attention(0)
            experts(0)
            attention(1)
            experts(1)

            def store(t):
                need(act, added, adds(1, t.at + 2 - t.par))
                act.dma_start(tile_of(out_tiles[bass.ds(t.at, 1)]),
                              xt[:, t.slot, :]).then_inc(out_stored[t.slot], 16)

            with act.Fori(0, NT // 4) as j:
                for u in range(4):
                    store(Tile(j, u))
            for r in range(4):
                act.wait_ge(out_stored[r], 16 * (NT // 4))

        @block.vector
        def _(dve):
            dve.wait_ge(consts_made, 1)

            def over(ap, axis, n):
                view = ap.unsqueeze(axis)
                return view.broadcast_to([n if i == axis else size
                                          for i, size in enumerate(view.shape)])

            def keys_values(l):
                dve.wait_ge(wkv_loaded, 16 * (4 + l))
                need(dve, v_stored, 16 * B * l)
                for b in range(B):
                    dve.wait_ge(v_ready, l * B + b + 1)
                    dve.tensor_tensor(
                        vals[:, b, :, 0:DH],
                        ps[0:S, 2 + b, 0:D].rearrange("p (h d) -> p h d", h=H),
                        bv[:, l, :].rearrange("p (h d) -> p h d", h=H), ALU.add
                    ).then_inc(v_done, 1)
                for b in range(B):
                    for c in range(KD):
                        n = (l * B + b) * KD + c
                        dve.wait_ge(kT_ready, n + 1)
                        dve.tensor_scalar(kT[:, :], ps[:, n % 2, 0:S], bk[:, l, c:c + 1], None,
                                          ALU.add).then_inc(kT_done, 1)
                        dve.wait_ge(kT_done, n + 1)
                        dve.tensor_copy(kT_hi[:, :], kT[:, :]).then_inc(kT_hi_done, 1)
                        dve.wait_ge(kT_hi_done, n + 1)
                        dve.tensor_tensor(kT_lo[:, :], kT[:, :], kT_hi[:, :].bitcast(F32),
                                          ALU.subtract).then_inc(kT_lo_done, 1)
                        dve.wait_ge(kT_lo_done, n + 1)
                        for part, to in ((kT_hi[:, :].bitcast(F32), key_hi), (kT_lo[:, :], key_lo)):
                            dve.tensor_tensor(
                                to[:, b, c, :].rearrange("p (h s) -> p h s", h=HC),
                                over(part, 1, HC),
                                over(head_mask[:, :], 2, S),
                                ALU.mult).then_inc(keys_done, 1)
                dve.wait_ge(v_flat, 32 * B * (l + 1))
                for b in range(B):
                    for r in range(SPAN):
                        ins = dve.tensor_tensor(
                            v_blocks[:, b, :, r * DV:(r + 1) * DV], flat_v[:, b, :, :],
                            over(block_mask[:, :, r], 2, DV), ALU.mult)
                    ins.then_inc(v_blocks_done, 1)

            def mixture(l):
                K = TOPK[l]
                steps = 3 * l
                part = mix[:, :, 0:K]
                dve.tensor_tensor(part, bests[:, :, 0:K], over(bests[:, :, 0], 2, K),
                                  ALU.subtract).then_inc(below_done, 1)
                dve.wait_ge(expw_done, l + 1)
                dve.tensor_reduce(mix_sum[:, :], part, AX.X, ALU.add).then_inc(mix_step, 1)
                dve.wait_ge(mix_step, steps + 1)
                dve.reciprocal(mix_sum[:, :], mix_sum[:, :]).then_inc(mix_step, 1)
                dve.wait_ge(mix_step, steps + 2)
                dve.tensor_scalar(mix_sum[:, :], mix_sum[:, :], tgates[:, 2 + l:3 + l], None,
                                  ALU.mult).then_inc(mix_step, 1)
                dve.wait_ge(mix_step, steps + 3)
                dve.tensor_tensor(shares[:, :, 0:K], part, over(mix_sum[:, :], 2, K),
                                  ALU.mult).then_inc(shares_done, 1)

            def combine(t):
                dve.wait_ge(results_loaded[t.par], (t.pair + 1) * 32)
                for k in range(TOPK[0]):
                    if k:
                        dve.wait_ge(added, adds(0, t.at) + k)
                    prev = xt[:, t.slot, :] if k else x2in[:, t.par, :]
                    dve.scalar_tensor_tensor(
                        out=xt[:, t.slot, :], in0=ysb[:, t.par, k, :],
                        scalar=shares[:, bass.ds(t.at, 1), k], in1=prev, op0=ALU.mult,
                        op1=ALU.add).then_inc(added, 1)

            def attention(l):
                K = TOPK[l]

                def first_stats(A):
                    T = A.at + NT * l
                    if l == 0:
                        need(dve, x_loaded[A.slot], (A.quad + 1) * 16)
                    else:
                        combine(A)
                        need(dve, added, adds(0, A.at + 1))
                    need(dve, moments1, T)
                    dve.bn_stats(st1[:, :], xt[:, A.slot, :]).then_inc(stats1, 1)

                a_cols, n_a = HPB * S, full * HPB
                banks = ps[:, SCORE_BANK:SCORE_BANK + full, 0:a_cols].rearrange(
                    "p b (h s) -> p b h s", h=HPB)
                last = ps[:, SCORE_BANK + full, 0:rest * S].rearrange(
                    "p (h s) -> p h s", h=rest)
                top_a = top[:, 0:n_a].rearrange("p (b h) -> p b h", b=full)

                def maxima(Q):
                    need(dve, scores_ready, Q.at + (NT * l + 1))
                    dve.tensor_reduce(top[:, n_a:H], last, AX.X, ALU.max).then_inc(max_done, 1)
                    dve.tensor_reduce(top_a, banks, AX.X, ALU.max).then_inc(max_done, 1)

                def softmax_shift(Q):
                    T = Q.at + NT * l
                    need(dve, pT_ready, T * 3 - 3)
                    need(dve, max_done, T * 2 + 1)
                    dve.tensor_tensor(
                        probs[:, Q.par, n_a * S:FLAT].rearrange("p (h s) -> p h s", h=rest),
                        last, over(top[:, n_a:H], 2, S), ALU.subtract
                    ).then_inc(shifted_part, 1)
                    need(dve, max_done, T * 2 + 2)
                    dve.tensor_tensor(
                        probs[:, Q.par, 0:n_a * S].rearrange("p (b h s) -> p b h s", b=full,
                                                             h=HPB),
                        banks, over(top_a, 3, S), ALU.subtract
                    ).then_inc(shifted, 1)

                def choose(R, Z):
                    if R:
                        T = R.at + NT * l
                        need(dve, oT_copied,
                             min(T + 3, NT * (l + 1)) if isinstance(T, int) else T + 3)
                        need(dve, logits_ready, T + 1)
                        dve.tensor_tensor(logits[:, :], ps[:, 1, D:D + E], br[:, l, :],
                                          ALU.add).then_inc(logits_done, 1)
                    if Z:
                        TZ = Z.at + NT * l
                        need(dve, count_ready, TZ + 1)
                        dve.tensor_tensor(slots[:, :], ps[:, 1, D + E:D + 2 * E],
                                          region_base[:, :], ALU.add).then_inc(slots_done, 1)
                    if R:
                        gate(dve, logits_done, T + 1)
                        dve.max(best[:, :], logits[:, :]).then_inc(best_done, 1)
                        gate(dve, best_done, T + 1)
                        dve.tensor_copy(bests[:, bass.ds(R.at, 1), :], best[:, 0:4].unsqueeze(1))
                        dve.max_index(best_at[:, :], best[:, :], logits[:, :]
                                      ).then_inc(best_at_done, 1)
                        need(dve, best_at_done, T + 1)
                        dve.tensor_copy(best_f[:, 0:K], best_at[:, 0:K]).then_inc(best_f_done, 1)
                    if Z:
                        need(dve, slots_done, TZ + 1)
                        dve.tensor_tensor(
                            slot_k[:, 0:K, :],
                            chosen[:, Z.slot, :, 0:K].rearrange("p e k -> p k e"),
                            over(slots[:, :], 1, K), ALU.mult
                        ).then_inc(slot_k_done, 1)
                    if R:
                        need(dve, best_f_done, T + 1)
                        dve.tensor_tensor(
                            chosen[:, R.slot, :, 0:K],
                            over(expert_ids[:, :], 2, K),
                            over(best_f[:, 0:K], 1, E),
                            ALU.is_equal).then_inc(chosen_done, 1)
                    if Z:
                        need(dve, slot_k_done, TZ + 1)
                        dve.tensor_reduce(slot_f[:, 0:K], slot_k[:, 0:K, :], AX.X,
                                          ALU.add).then_inc(slot_f_done, 1)
                    if R:
                        need(dve, chosen_done, T + 1)
                        dve.tensor_reduce(mask[:, R.par, :], chosen[:, R.slot, :, 0:K], AX.X,
                                          ALU.add).then_inc(mask_done, 1)
                        dve.tensor_tensor(
                            ranked[:, :, 0:K], chosen[:, R.slot, :, 0:K],
                            over(rank_rows[:, 0:K], 1, E),
                            ALU.mult).then_inc(ranked_done, 1)
                    if Z:
                        need(dve, scattered[Z.slot], scatter_count(l, Z.slot, Z.quad))
                        need(dve, slot_f_done, TZ + 1)
                        dve.tensor_copy(slot_at[:, Z.slot, 0:K], slot_f[:, 0:K]
                                        ).then_inc(slot_done, 1)
                    if R:
                        need(dve, mask_done, T + 1)
                        need(dve, seen_done, T)
                        dve.tensor_tensor(seen[:, 1 - R.par, :], seen[:, R.par, :],
                                          mask[:, R.par, :], ALU.add).then_inc(seen_done, 1)
                        need(dve, ranked_done, T + 1)
                        dve.tensor_reduce(ranks[:, :], ranked[:, :, 0:K], AX.X,
                                          ALU.add).then_inc(ranks_done, 1)
                        need(dve, ranks_done, T + 1)
                        dve.tensor_scalar(rows[:, R.slot, D:ROW], ranks[:, :],
                                          token_ids[:, l, bass.ds(R.at, 1)], None, ALU.add
                                          ).then_inc(code_done, 1)

                def step(j, s):
                    A, Q, S2, F, G, _, C, Z = [stage(j, s, lag) for lag in range(LAGS + 1)]
                    choose(C, Z)
                    if G:
                        TG = G.at + NT * l
                        need(dve, x2_stored[G.slot],
                             G.quad * 16 + (l * (NT // 4) * 16 + HEAD_START))
                        need(dve, xg_done, TG + 1)
                        need(dve, proj_ready, TG + 1)
                        dve.scalar_tensor_tensor(
                            out=x2[:, G.slot, 0:D], in0=ps[:, 7, 0:D], scalar=tgates[:, l:l + 1],
                            in1=xg[:, G.slot, :], op0=ALU.mult, op1=ALU.add
                        ).then_inc(x2_done, 1)
                    if Q:
                        T = Q.at + NT * l
                        need(dve, xT_hi_done, T + 1)
                        dve.tensor_tensor(xT_lo[:, :], ps[:, 0, 0:D], xT_hi[:, :].bitcast(F32),
                                          ALU.subtract).then_inc(xT_lo_done, 1)
                    if S2:
                        maxima(S2)
                        softmax_shift(S2)
                    if Q:
                        need(dve, q_hi_done, T * 2 + 2)
                        for c in range(KD):
                            dve.scalar_tensor_tensor(
                                out=q_lo[:, c, :], in0=ps[:, 1, c * P:(c + 1) * P],
                                scalar=bq[:, l, c:c + 1], in1=q_hi[:, c, :].bitcast(F32),
                                op0=ALU.add, op1=ALU.subtract).then_inc(q_lo_done, 1)
                    if F:
                        TF = F.at + NT * l
                        out = ps[:, 7, 0:H * DV].rearrange("p (h d) -> p h d", h=H)
                        need(dve, pv_ready, TF + 1)
                        dve.reciprocal(rden[:, :].rearrange("p (h o) -> p h o", o=1),
                                       out[:, :, DH:DV]).then_inc(rden_done, 1)
                    if G:
                        need(dve, moments2, TG)
                        need(dve, x2_done, TG + 1)
                        dve.bn_stats(st2[:, :], x2[:, G.slot, 0:D]).then_inc(stats2, 1)
                    if F:
                        need(dve, oT_ready, TF)
                        need(dve, rden_done, TF + 1)
                        dve.tensor_tensor(ob[:, :].rearrange("p (h d) -> p h d", h=H),
                                          out[:, :, 0:DH],
                                          over(rden[:, :], 2, DH),
                                          ALU.mult).then_inc(o_done, 1)
                    if A:
                        first_stats(A)
                    if G:
                        gate(dve, stats2, TG + 1)
                        gate(dve, offset2, TG)
                        dve.bn_aggr(mv2[:, :], st2[:, :]).then_inc(moments2, 1)
                    if A:
                        TA = A.at + NT * l
                        gate(dve, stats1, TA + 1)
                        gate(dve, offset1, TA)
                        dve.bn_aggr(mv1[:, :], st1[:, :]).then_inc(moments1, 1)

                dve.memset(seen[:, 0, :], 0.0).then_inc(seen_zero, 1)
                dve.wait_ge(seen_zero, l + 1)
                attention_steps(dve, step)

            steps = [0]

            def table(l):
                M = MT[l]
                ids, end, tiles = tile_ids[:, 0:M], t_end[:, :], t_tiles[:, :]
                le, m, e_, d = t_le[:, 0:M, :], t_m[:, 0:M, :], t_e[:, 0:M], t_d[:, 0:M]

                def then(ins):
                    steps[0] += 1
                    ins.then_inc(table_step, 1)
                    dve.wait_ge(table_step, steps[0])

                def row(n):
                    return tab_f[:, n, 0:M]

                dve.wait_ge(total_ready, l + 1)
                then(dve.tensor_copy(t_cnt[:, :], ps[0:1, 0, 0:E]))
                then(dve.tensor_copy(cnt_i[:, :], t_cnt[:, :]))
                then(dve.tensor_tensor(t_gt[:, :, :], over(t_cnt[:, :], 2, 15),
                                       over(tile_edges[:, :], 1, E),
                                       ALU.is_gt))
                then(dve.tensor_reduce(tiles, t_gt[:, :, :], AX.X, ALU.add))
                then(dve.tensor_scalar(tiles, tiles, 1.0, None, ALU.add))
                then(dve.tensor_tensor(t_tri[:, :, :], over(tiles, 1, E),
                                       tri8[:, :, :], ALU.mult))
                then(dve.tensor_reduce(end, t_tri[:, :, :], AX.X, ALU.add))
                then(dve.tensor_tensor(le, over(end, 1, M),
                                       over(ids, 2, E), ALU.is_le))
                then(dve.tensor_reduce(e_, le, AX.X, ALU.add))
                then(dve.tensor_tensor(m, le, over(tiles, 1, M), ALU.mult))
                then(dve.tensor_reduce(d, m, AX.X, ALU.add))
                then(dve.tensor_tensor(d, ids, d, ALU.subtract))
                then(dve.tensor_scalar(row(ROWAT), e_, float(REGION), None, ALU.mult))
                then(dve.scalar_tensor_tensor(out=row(ROWAT), in0=d, scalar=float(P),
                                              in1=row(ROWAT), op0=ALU.mult, op1=ALU.add))
                then(dve.tensor_tensor(m, le, over(alternate[:, :], 1, M),
                                       ALU.mult))
                then(dve.tensor_reduce(row(SLOT), m, AX.X, ALU.add))
                then(dve.tensor_scalar(row(EXPERT), e_, float(E - 1), None, ALU.min))
                then(dve.tensor_scalar(t_new[:, 0:M], e_, float(E), None, ALU.is_ge))
                then(dve.scalar_tensor_tensor(out=d, in0=d, scalar=1.0 - E, in1=t_new[:, 0:M],
                                              op0=ALU.add, op1=ALU.mult))
                then(dve.tensor_tensor(row(PLACE), row(EXPERT), d, ALU.add))
                then(dve.memset(t_new[:, 0:1], 0.0))
                then(dve.tensor_tensor(t_new[:, 1:M], row(EXPERT)[:, 1:M],
                                       row(EXPERT)[:, 0:M - 1], ALU.not_equal))
                if l == LAYERS - 1:
                    then(dve.scalar_tensor_tensor(
                        out=t_new[:, 0:M], in0=row(EXPERT), scalar=float(E - 1),
                        in1=t_new[:, 0:M], op0=ALU.is_lt, op1=ALU.mult))
                then(dve.tensor_tensor(row(SPLIT0), t_new[:, 0:M], row(SLOT), ALU.mult))
                then(dve.tensor_tensor(row(SPLIT1), t_new[:, 0:M], row(SPLIT0), ALU.subtract))
                last = float(LAYERS * E - 1)
                then(dve.tensor_scalar(row(NEXT), row(EXPERT), float(l * E + 1), last, ALU.add,
                                       ALU.min))
                then(dve.tensor_scalar(row(LOAD), row(EXPERT), float(l * E + 2), last, ALU.add,
                                       ALU.min))
                dve.tensor_copy(tab[:, :, 0:M], tab_f[:, :, 0:M]).then_inc(table_ready, 1)

            def experts(l):
                halves = KH[l] // 4

                def place_of(t):
                    return dve.value_load(tab[0:1, PLACE, bass.ds(t.at, 1)], min_val=0,
                                          max_val=E - 1)

                def row_low(t):
                    G = t.at + MBASE[l]
                    need(dve, mT_hi_done, G + 1)
                    dve.tensor_tensor(xT_lo[:, :], ps[:, 0, 0:D], xT_hi[:, :].bitcast(F32),
                                      ALU.subtract).then_inc(mT_lo_done, 1)

                def keep_places(t, place):
                    gate(dve, y_scattered[t.slot8], y_count(l, t))
                    gate(dve, rows_loaded[t.slot], (t.quad + (uses(l, t.slot) + 1)) * 16)
                    dve.tensor_copy(y_at[:, t.slot8:t.slot8 + 1],
                                    xm[:, t.slot, bass.ds(place + D, 1)]).then_inc(y_at_done, 1)

                def step(j, s):
                    t, n, h_t = [row_tile(l, j, s, lag) for lag in (0, -1, 1)]
                    place = place_of(n) if n else None
                    if h_t:
                        for h in range(halves):
                            need(dve, hT_hi_done, h_t.at * halves + (HBASE[l] + h + 1))
                            dve.tensor_tensor(
                                hT_lo[:, h * SC:(h + 1) * SC], ps[:, 3 + h, :],
                                hT_hi[:, h * SC:(h + 1) * SC].bitcast(F32), ALU.subtract
                            ).then_inc(hT_lo_done, 1)
                    if t and l == 0:
                        need(dve, hT_ready, t.at * 2)
                        need(dve, hid_ready, t.at * 2 + 1)
                        dve.tensor_scalar(hid[:, 0:SC], ps[:, 1, :], 0.0, None, ALU.max
                                          ).then_inc(hid_dve, 1)
                    if t and l == 1:
                        for h in range(2):
                            T = t.at * 2 + h
                            half = slice(h * GH, (h + 1) * GH)
                            need(dve, hid_ready, T + (MBASE[1] * 2 + 1))
                            dve.tensor_scalar(gate_s[:, half], ps[:, 1 + h, 0:GH], 7.0, None,
                                              ALU.min).then_inc(gate_done, 1)
                            dve.tensor_scalar(up_s[:, half], ps[:, 1 + h, GH:2 * GH], 7.0, -7.0,
                                              ALU.min, ALU.max).then_inc(up_done, 1)
                            if h and n:
                                row_low(n)
                            need(dve, sig_done, T + 1)
                            dve.tensor_tensor(gate_s[:, half], gate_s[:, half],
                                              sig_s[:, half], ALU.mult).then_inc(glu_done, 1)
                            if h == 0:
                                need(dve, hT_ready, t.at + HBASE[1])
                            need(dve, glu_done, T + 1)
                            dve.scalar_tensor_tensor(
                                out=hid[:, half], in0=up_s[:, half], scalar=1.0,
                                in1=gate_s[:, half], op0=ALU.add, op1=ALU.mult
                            ).then_inc(glu_hid, 1)
                    if n:
                        if not (t and l == 1):
                            row_low(n)
                        keep_places(n, place)
                dve.wait_ge(table_ready, l + 1)
                row_low(Tile(None, 0))
                keep_places(Tile(None, 0), place_of(Tile(None, 0)))
                expert_steps(dve, l, step)

            keys_values(0)
            dve.wait_ge(wq_hi_done, 1)
            dve.tensor_tensor(wq_lo[:, :, :, :], wq[:, :, :, :],
                              wq_hi[:, :, :, :].bitcast(F32), ALU.subtract
                              ).then_inc(wq_lo_done, 1)
            attention(0)
            table(0)
            mixture(0)
            experts(0)
            keys_values(1)
            dve.wait_ge(shares_done, 1)
            attention(1)
            table(1)
            mixture(1)
            experts(1)
            dve.wait_ge(shares_done, 2)

            def final_pair(a, b):
                for t in (a, b):
                    need(dve, out_stored[t.slot], t.quad * 16)
                for k in range(TOPK[1]):
                    for n, t in enumerate((a, b)):
                        if k:
                            gate(dve, added, adds(1, a.at) + (2 * k - 1 + n))
                        else:
                            gate(dve, finals_loaded[t.slot], t.quad * 32 + 32)
                        dve.scalar_tensor_tensor(
                            out=xt[:, t.slot, :], in0=finals[:, t.slot, k, :],
                            scalar=shares[:, bass.ds(t.at, 1), k],
                            in1=xt[:, t.slot, :] if k else x2[:, t.slot, :],
                            op0=ALU.mult, op1=ALU.add).then_inc(added, 1)

            for t in (0, 2):
                final_pair(Tile(None, t), Tile(None, t + 1))
            with dve.Fori(0, NT // 4 - 1) as j:
                for u in (0, 2):
                    final_pair(Tile(j, 4 + u), Tile(j, 5 + u))

        @block.tensor
        def _(pe):
            def keys_values(l):
                need(pe, mT_lo_done, MBASE[l])
                need(pe, hT_lo_done, HBASE[l])
                pe.wait_ge(wkv_loaded, 16 * (4 + l))
                for b in range(B):
                    for k in range(KD):
                        mm = pe.matmul(ps[0:S, 2 + b, 0:D], ctxT[:, b, k, :], wkv[:, 1, k, :],
                                       start=k == 0, stop=k == KD - 1)
                    mm.then_inc(v_ready, 1)
                for b in range(B):
                    for c in range(KD):
                        n = (l * B + b) * KD + c
                        need(pe, kT_done, n - 1)
                        for k in range(KD):
                            mm = pe.matmul(ps[:, n % 2, 0:S], wkv[:, 0, k, c * P:(c + 1) * P],
                                           ctxT[:, b, k, :], start=k == 0, stop=k == KD - 1)
                        mm.then_inc(kT_ready, 1)
                pe.wait_ge(keys_done, 2 * B * KD * (l + 1))
                pe.wait_ge(v_blocks_done, B * (l + 1))

            def transposed(bank, src, ready):
                for c in range(KD):
                    mm = pe.transpose(ps[:, bank, c * P:(c + 1) * P],
                                      src[:, c * P:(c + 1) * P], ident[:, :])
                mm.then_inc(ready, 1)

            def split_product(out, terms, start=True, stop=True):
                for n, (l_hi, l_lo, r_hi, r_lo) in enumerate(terms):
                    for m, (lhs, rhs) in enumerate(((l_hi, r_hi), (l_hi, r_lo), (l_lo, r_hi))):
                        mm = pe.matmul(out, lhs, rhs, start=start and n == 0 and m == 0,
                                       stop=stop and n == len(terms) - 1 and m == 2)
                return mm

            def attention(l):
                def scores(Q):
                    T = Q.at + NT * l
                    batch = Q.at // (NT // B)
                    need(pe, shifted, T)
                    need(pe, q_lo_done, T * 2 + 2)
                    for c, h, n in pieces:
                        at = (h - c * HC) * S
                        keys = [key[:, bass.ds(batch, 1), c, at:at + n * S].rearrange(
                            "p a n -> p (a n)") for key in (key_hi, key_lo)]
                        mm = split_product(
                            ps[:, SCORE_BANK + h // HPB, h % HPB * S:(h % HPB + n) * S],
                            [(q_hi[:, c, :], q_lo[:, c, :], *keys)])
                    mm.then_inc(scores_ready, 1)

                def transpose_probs(F, n):
                    c0, c1 = GROUPS[n]
                    need(pe, pT_copied, (F.at + NT * l) * 3 + (1 if n == 2 else 0))
                    for c in range(c0, c1):
                        mm = pe.transpose(ps[:, PT_BANK + n % 2, (c - c0) * P:(c - c0 + 1) * P],
                                          probs[:, F.par, c * P:(c + 1) * P], ident[:, :])
                    mm.then_inc(pT_ready, 1)

                def step(j, s):
                    _, Q, S2, F, G, R, C, _ = [stage(j, s, lag) for lag in range(LAGS + 1)]
                    if S2:
                        scores(S2)
                    if G:
                        TG = G.at + NT * l
                        need(pe, oT_copied, TG + 1)
                        for k in range(KD):
                            mm = pe.matmul(ps[:, 7, 0:D], oT[:, k * P:(k + 1) * P],
                                           wo[:, l, k, :], start=k == 0, stop=k == KD - 1)
                        mm.then_inc(proj_ready, 1)
                    if Q:
                        T = Q.at + NT * l
                        need(pe, xn_done, T + 1)
                        transposed(0, xn[:, Q.par, :], xnT_ready)
                    if F:
                        TF = F.at + NT * l
                        need(pe, exp_done, TF + 1)
                        transpose_probs(F, 0)
                        transpose_probs(F, 1)
                    if Q:
                        need(pe, best_done, T - 4)
                        need(pe, xT_lo_done, T + 1)
                        for c in range(KD):
                            mm = split_product(ps[:, 1, c * P:(c + 1) * P], [
                                (wq_hi[:, l, k, c * P:(c + 1) * P],
                                 wq_lo[:, l, k, c * P:(c + 1) * P],
                                 xT_hi[:, k * P:(k + 1) * P], xT_lo[:, k * P:(k + 1) * P])
                                for k in range(KD)])
                        mm.then_inc(q_ready, 1)
                    if F:
                        transpose_probs(F, 2)
                        need(pe, x2_done, TF)
                        batch = F.at // (NT // B)
                        for n, (c0, c1) in enumerate(GROUPS):
                            need(pe, pT_copied, TF * 3 + (n + 1))
                            for c in range(c0, c1):
                                at = first_head(c) * DV
                                mm = pe.matmul(
                                    ps[:, 7, at:at + SPAN * DV], probsT[:, c * P:(c + 1) * P],
                                    v_blocks[:, bass.ds(batch, 1), c, :].rearrange(
                                        "p a n -> p (a n)"),
                                    start=c == 0, stop=c == NCH - 1, skip_group_check=True)
                        mm.then_inc(pv_ready, 1)
                    if R:
                        TR = R.at + NT * l
                        need(pe, rows_done, TR + 1)
                        transposed(0, rows[:, R.slot, :], x2T_ready)
                    if Q:
                        need(pe, q_lo_done, T * 2 + 2)
                    if C:
                        TC = C.at + NT * l
                        need(pe, mask_done, TC + 1)
                        pe.matmul(ps[:, 1, D + E:D + 2 * E], tri[:, :], mask[:, C.par, :],
                                  start=True, stop=False)
                        pe.matmul(ps[:, 1, D + E:D + 2 * E], ones[:, :], seen[:, C.par, :],
                                  start=False, stop=True).then_inc(count_ready, 1)
                    if R:
                        need(pe, x2T_copied, TR + 1)
                        for k in range(KD):
                            mm = pe.matmul(ps[:, 1, D:D + E], x2T[:, k * P:(k + 1) * P],
                                           wr[:, l, k, :], start=k == 0, stop=k == KD - 1)
                        mm.then_inc(logits_ready, 1)
                    if F:
                        need(pe, o_done, TF + 1)
                        transposed(1, ob, oT_ready)
                attention_steps(pe, step)
                pe.wait_ge(slots_done, NT * (l + 1))
                pe.wait_ge(seen_done, NT * (l + 1))
                pe.matmul(ps[:, 0, 0:E], ones[:, :], seen[:, 0, :], start=True,
                          stop=True).then_inc(total_ready, 1)

            def experts(l):
                def row_part(t):
                    G = t.at + MBASE[l]
                    need(pe, mT_lo_done, G)
                    pe.wait_ge(rows_loaded[t.slot], (t.quad + (uses(l, t.slot) + 1)) * 16)
                    transposed(0, xm[:, t.slot, :], mT_ready)

                def expert_of(t):
                    return pe.value_load(tab[0:1, EXPERT, bass.ds(t.at, 1)], min_val=0,
                                         max_val=E - 1)

                def at_slot(w, slot, c0, n):
                    return w[:, bass.ds(slot, 1), c0:c0 + n].rearrange("p a n -> p (a n)")

                def first_product(t, slot):
                    T = t.at
                    need(pe, mT_lo_done, T + MBASE[l] + 1)
                    for half in range(2):
                        if l == 0:
                            need(pe, (hid_dve, hid_act)[half], T)
                        else:
                            need(pe, up_done, T * 2 + (half - 1))
                        split_product(ps[:, 1 + half, :], [
                            (xT_hi[:, k * P:(k + 1) * P], xT_lo[:, k * P:(k + 1) * P],
                             at_slot(w_hi, slot, k * WIDE + half * SC, SC),
                             at_slot(w_lo, slot, k * WIDE + half * SC, SC)) for k in range(KD)],
                            stop=False)
                        pe.matmul(ps[:, 1 + half, :], ones2[:, :],
                                  at_slot(w_bias, slot, half * SC, SC), start=False, stop=True
                                  ).then_inc(hid_ready, 1)

                halves = KH[l] // 4
                early = 2 if l == 1 else 0

                def second_product(t, slot):
                    G = t.at + MBASE[l]
                    need(pe, y_done, G)
                    need(pe, hT_lo_done, t.at * halves + (HBASE[l] + halves))
                    split_product(ps[:, 5, 0:D], [
                        (hT_hi[:, k * P:(k + 1) * P], hT_lo[:, k * P:(k + 1) * P],
                         at_slot(w_hi, slot, W2AT + k * D, D),
                         at_slot(w_lo, slot, W2AT + k * D, D)) for k in range(KH[l])],
                        stop=False)
                    pe.matmul(ps[:, 5, 0:D], ones2[:, :], at_slot(w_bias, slot, WIDE, D),
                              start=False, stop=True).then_inc(y_ready, 1)

                def hidden_transposes(t, cols):
                    need(pe, hT_lo_done, t.at * halves + HBASE[l])
                    for c in cols:
                        if l == 0 and c % 4 == 0:
                            need(pe, (hid_dve, hid_act)[c // 4], t.at + 1)
                        if l == 1 and c % 2 == 0:
                            need(pe, glu_hid, t.at * 2 + (c // 2 + 1))
                        mm = pe.transpose(ps[:, 3 + c // 4, c % 4 * P:(c % 4 + 1) * P],
                                          hid[:, c * P:(c + 1) * P], ident[:, :])
                        if c % 4 == 3:
                            mm.then_inc(hT_ready, 1)

                experts_of, stretch = {}, []

                def step(j, s):
                    if not stretch or stretch[-1] is not j:
                        stretch.append(j)
                        experts_of.clear()
                    t, n, h_t, y_t = [row_tile(l, j, s, lag) for lag in (0, -1, 1, 2)]
                    for lag, tile in ((0, t), (2, y_t)):
                        if tile and s - lag not in experts_of:
                            experts_of[s - lag] = expert_of(tile)
                    expert = experts_of.get(s)
                    slot = expert & 1 if t else None
                    y_slot = experts_of[s - 2] & 1 if y_t else None
                    if h_t:
                        hidden_transposes(h_t, range(early))
                    if y_t:
                        second_product(y_t, y_slot)
                    if t:
                        pe.wait_ge(split_done, expert + (l * E + 1))
                    if h_t:
                        hidden_transposes(h_t, range(early, KH[l]))
                    if t:
                        first_product(t, slot)
                    if n:
                        row_part(n)
                pe.wait_ge(table_ready, l + 1)
                row_part(Tile(None, 0))
                expert_steps(pe, l, step)
                pe.wait_ge(y_done, MBASE[l] + MT[l])

            pe.wait_ge(consts_made, 1)
            keys_values(0)
            pe.wait_ge(params_loaded, 16 * 8)
            pe.wait_ge(wq_lo_done, 1)
            attention(0)
            experts(0)
            keys_values(1)
            attention(1)
            experts(1)


def _chunks(w):
    return w.reshape(-1, P, w.shape[-1]).transpose(1, 0, 2)


def _halves(w):
    return w.reshape(*w.shape[:-1], 2, 2, WIDE // 4).swapaxes(-3, -2).reshape(w.shape)


def kernel(**inputs):
    import concourse.bacc as bacc
    from concourse.bass_utils import run_bass_kernel_spmd

    i = {k: np.asarray(v) for k, v in inputs.items()}
    attn = lambda n: [i["L0_xattn_W" + n], i["L1_xattn_W" + n].T]
    bias = lambda n: np.stack([i[f"L{l}_xattn_b{n}"] for l in range(LAYERS)])
    both = lambda n: np.stack([_chunks(w) for w in attn(n)], axis=1)
    w = np.zeros((LAYERS * E, P, WCOLS), np.float32)
    firsts = (i["L0_ffn_W1"], _halves(i["L1_ffn_gate_up_proj"].transpose(0, 2, 1)))
    seconds = (i["L0_ffn_W2"], i["L1_ffn_down_proj"].transpose(0, 2, 1))
    for l in range(LAYERS):
        for e in range(E):
            w[l * E + e, :, 0:W2AT] = _chunks(firsts[l][e]).reshape(P, -1)
            second = _chunks(seconds[l][e]).reshape(P, -1)
            w[l * E + e, :, W2AT:W2AT + second.shape[1]] = second
    biases = np.concatenate([
        np.concatenate([i["L0_ffn_b1"], i["L0_ffn_b2"]], axis=1),
        np.concatenate([_halves(i["L1_ffn_gate_up_proj_bias"]), i["L1_ffn_down_proj_bias"]], axis=1)])
    per_row = lambda v: v.reshape(LAYERS, KD, P).transpose(2, 0, 1)
    data = {
        "x": i["x"].reshape(N, D),
        "ctxT": i["ctx_1024"].transpose(2, 0, 1).reshape(KD, P, B, S).transpose(1, 2, 0, 3),
        "wkv": np.stack([both("k"), both("v")], axis=2).transpose(1, 0, 2, 3, 4),
        "wq": both("q"), "wo": both("o"),
        "wr": np.stack([_chunks(i["L0_ffn_Wr"]), _chunks(i["L1_ffn_router_weight"].T)], axis=1),
        "bq": per_row(bias("q")), "bk": per_row(bias("k")), "bv": bias("v"), "bo": bias("o"),
        "br": np.stack([i["L0_ffn_br"], i["L1_ffn_router_bias"]]),
        "gates": np.concatenate([i["g_xattn"], i["g_ffn"]]),
        "biases": biases.reshape(P, -1), "weights": w,
    }
    data = {k: np.ascontiguousarray(v) for k, v in data.items()}
    nc = bacc.Bacc("TRN2", target_bir_lowering=False, num_devices=1)
    aps = {k: nc.dram_tensor(f"in_{k}", v.shape, F32, kind="ExternalInput").ap()
           for k, v in data.items()}
    aps["out"] = nc.dram_tensor("out", (N, D), F32, kind="ExternalOutput").ap()
    build_program(nc, aps)
    r = run_bass_kernel_spmd(nc, [{f"in_{k}": v for k, v in data.items()}], core_ids=[0])
    return r.results[0]["out"].reshape(B, SEQ, D)
```
